# Optimizing a Trainium2 kernel written in Bass

```python
import numpy as np
import jax
import jax.numpy as jnp

def _softmax(x, axis=-1):
    return jax.nn.softmax(x, axis=axis)

def _gelu(x):
    return jax.nn.gelu(x, approximate=True)

def _silu(x):
    return jax.nn.silu(x)

def _sigmoid(x):
    return jax.nn.sigmoid(x)

def _layernorm(x, axis=-1, eps=1e-05):
    m = jnp.mean(x, axis=axis, keepdims=True)
    v = jnp.var(x, axis=axis, keepdims=True)
    return (x - m) / jnp.sqrt(v + eps)

def _scatter_add(tgt, idx, src, axis=0):
    return tgt.at[idx].add(src)

def _segment_sum(src, seg, n):
    return jax.ops.segment_sum(src, seg, n)
kernel_name = 'mk_audio_tower_d2_tok_audfeat1024_r4_430b46'

def setup_inputs(seed: int=0):
    np.random.seed(seed)
    _w = jnp.asarray

    def _rec_inputs():
        import jax
        import jax.numpy as jnp
        _rk = jax.random.key(seed)
        x = -0.000125008 + 0.999885 * jax.random.normal(jax.random.fold_in(_rk, 1), (4, 128, 750), jnp.float32)
        return x
    x = _rec_inputs()

    def _L0_tok_setup():
        import jax, jax.numpy as jnp
        import numpy as np
        from jax import lax
        ALPHA = 0.1
        B, C_IN, T, D_MODEL = (32, 128, 512, 256)

        def _ewma_scan(xt):

            def step(carry, xi):
                carry = ALPHA * xi + (1.0 - ALPHA) * carry
                return (carry, carry)
            _, ys = lax.scan(step, xt[0], xt[1:])
            return jnp.concatenate([xt[:1], ys], axis=0)
        key = jax.random.key(seed)
        k_x, k_w, k_b = jax.random.split(key, 3)
        x = jax.random.normal(k_x, (B, C_IN, T), dtype=jnp.float32)
        bound = 1.0 / np.sqrt(C_IN)
        W = jax.random.uniform(k_w, (D_MODEL, C_IN), dtype=jnp.float32, minval=-bound, maxval=bound)
        b = jax.random.uniform(k_b, (D_MODEL,), dtype=jnp.float32, minval=-bound, maxval=bound)
        return {'x': x, 'W': W, 'b': b}
    _L0_tok_all = _L0_tok_setup()
    _L0_tok_in = {k: v for k, v in _L0_tok_all.items() if k in ('W', 'b')}
    del _L0_tok_all

    def _L0_attn_setup():
        import jax, jax.numpy as jnp
        import numpy as np

        def _rope_tables(T, d):
            half = d // 2
            i = jnp.arange(half, dtype=jnp.float32)
            theta = 10000.0 ** (-2.0 * i / d)
            m = jnp.arange(T, dtype=jnp.float32)[:, None]
            ang = m * theta[None, :]
            return (jnp.cos(ang), jnp.sin(ang))

        def _rotate(v, cos, sin):
            B, T, d = v.shape
            half = d // 2
            v2 = v.reshape(B, T, half, 2)
            even, odd = (v2[..., 0], v2[..., 1])
            c = cos[None, :, :]
            s = sin[None, :, :]
            new_even = even * c - odd * s
            new_odd = even * s + odd * c
            return jnp.stack([new_even, new_odd], axis=-1).reshape(B, T, d)
        key = jax.random.key(seed)
        k1, k2, k3, k4 = jax.random.split(key, 4)
        B, T, d = (4, 512, 256)
        x = jax.random.normal(k1, (B, T, d), dtype=jnp.float32)
        scale = 0.02
        Wq = jax.random.normal(k2, (d, d), dtype=jnp.float32) * scale
        Wk = jax.random.normal(k3, (d, d), dtype=jnp.float32) * scale
        Wv = jax.random.normal(k4, (d, d), dtype=jnp.float32) * scale
        return {'x': x, 'Wq': Wq, 'Wk': Wk, 'Wv': Wv}
    _L0_attn_all = _L0_attn_setup()
    _L0_attn_in = {k: v for k, v in _L0_attn_all.items() if k in ('Wq', 'Wk', 'Wv')}
    del _L0_attn_all

    def _L0_ffn_setup():
        import jax, jax.numpy as jnp
        import numpy as np
        D = 256
        H = 16
        FF = 1024
        E = 8
        K = 2
        EH = 256
        B, S = (2, 512)
        EPS = 1e-05

        def rmsnorm(x, w):
            v = jnp.mean(jnp.square(x), axis=-1, keepdims=True)
            return x * jax.lax.rsqrt(v + EPS) * w

        def _dense_path(x, wq, wk, wv, wo, w1, w2, w3, attn_norm_w, ff_norm_w):
            b, s, d = x.shape
            hd = d // H
            q = (x @ wq).reshape(b, s, H, hd)
            k = (x @ wk).reshape(b, s, H, hd)
            v = (x @ wv).reshape(b, s, H, hd)
            scores = jnp.einsum('bqhd,bkhd->bhqk', q, k) / np.sqrt(hd).astype(np.float32)
            causal = jnp.tril(jnp.ones((s, s), bool))
            scores = jnp.where(causal, scores, jnp.finfo(scores.dtype).min)
            attn = jax.nn.softmax(scores, axis=-1)
            o = jnp.einsum('bhqk,bkhd->bqhd', attn, v).reshape(b, s, d)
            h = x + rmsnorm(o @ wo, attn_norm_w)
            ffn = jax.nn.silu(h @ w1) * (h @ w3) @ w2
            return h + rmsnorm(ffn, ff_norm_w)

        def _sparse_path(x, router_w, ew1, ew2, ew3, moe_norm_w):
            b, s, d = x.shape
            xt = x.reshape(-1, d)
            probs = jax.nn.softmax(xt @ router_w, axis=-1)
            topw, topi = jax.lax.top_k(probs, K)
            g = jax.nn.silu(jnp.einsum('td,edh->eth', xt, ew1)) * jnp.einsum('td,edh->eth', xt, ew3)
            eo = jnp.einsum('eth,ehd->ted', g, ew2)
            sel = jnp.take_along_axis(eo, topi[:, :, None], axis=1)
            moe_out = jnp.sum(topw[:, :, None] * sel, axis=1).reshape(b, s, d)
            return rmsnorm(moe_out, moe_norm_w)
        key = jax.random.key(seed)
        ks = jax.random.split(key, 16)
        s = 0.02
        return {'x': jax.random.normal(ks[0], (B, S, D), jnp.float32), 'wq': jax.random.normal(ks[1], (D, D), jnp.float32) * s, 'wk': jax.random.normal(ks[2], (D, D), jnp.float32) * s, 'wv': jax.random.normal(ks[3], (D, D), jnp.float32) * s, 'wo': jax.random.normal(ks[4], (D, D), jnp.float32) * s, 'w1': jax.random.normal(ks[5], (D, FF), jnp.float32) * s, 'w2': jax.random.normal(ks[6], (FF, D), jnp.float32) * s, 'w3': jax.random.normal(ks[7], (D, FF), jnp.float32) * s, 'attn_norm_w': jnp.ones((D,), jnp.float32), 'ff_norm_w': jnp.ones((D,), jnp.float32), 'moe_norm_w': jnp.ones((D,), jnp.float32), 'router_w': jax.random.normal(ks[8], (D, E), jnp.float32) * s, 'ew1': jax.random.normal(ks[9], (E, D, EH), jnp.float32) * s, 'ew2': jax.random.normal(ks[10], (E, EH, D), jnp.float32) * s, 'ew3': jax.random.normal(ks[11], (E, D, EH), jnp.float32) * s}
    _L0_ffn_all = _L0_ffn_setup()
    _L0_ffn_in = {k: v for k, v in _L0_ffn_all.items() if k in ('wq', 'wk', 'wv', 'wo', 'w1', 'w2', 'w3', 'attn_norm_w', 'ff_norm_w', 'moe_norm_w', 'router_w', 'ew1', 'ew2', 'ew3')}
    del _L0_ffn_all

    def _L1_attn_setup():
        import jax, jax.numpy as jnp
        import numpy as np
        B, T, D, H = (4, 512, 256, 16)
        HEAD_DIM = D // H
        LOCAL_WINDOW = 128

        def _rotate_half(t):
            t1, t2 = jnp.split(t, 2, axis=-1)
            return jnp.concatenate([-t2, t1], axis=-1)

        def _apply_rope(q, k):
            Tq, d = (q.shape[2], q.shape[3])
            half = d // 2
            theta = 1.0 / 10000.0 ** (jnp.arange(half, dtype=jnp.float32) / half)
            pos = jnp.arange(Tq, dtype=jnp.float32)
            freqs = pos[:, None] * theta[None, :]
            freqs = jnp.concatenate([freqs, freqs], axis=-1)
            cos = jnp.cos(freqs)[None, None]
            sin = jnp.sin(freqs)[None, None]
            q = q * cos + _rotate_half(q) * sin
            k = k * cos + _rotate_half(k) * sin
            return (q, k)
        key = jax.random.key(seed)
        k1, k2, k3 = jax.random.split(key, 3)
        x = jax.random.normal(k1, (B, T, D), dtype=jnp.float32)
        Wqkv = jax.random.normal(k2, (D, 3 * D), dtype=jnp.float32) * 0.02
        Wout = jax.random.normal(k3, (D, D), dtype=jnp.float32) * 0.02
        return {'x': x, 'Wqkv': Wqkv, 'Wout': Wout}
    _L1_attn_all = _L1_attn_setup()
    _L1_attn_in = {k: v for k, v in _L1_attn_all.items() if k in ('Wqkv', 'Wout')}
    del _L1_attn_all

    def _L1_ffn_setup():
        import jax, jax.numpy as jnp
        import numpy as np
        QP = 127.0
        MIN_RANGE = 1e-06

        def _ste_round(x):
            return x + jax.lax.stop_gradient(jnp.round(x) - x)

        def _quant_per_tensor(x):
            scale = jnp.maximum(jnp.max(jnp.abs(x)), MIN_RANGE) / QP
            return (_ste_round(x / scale), scale)

        def _qlinear(x2d, w, b):
            xq, sx = _quant_per_tensor(x2d)
            wq, sw = _quant_per_tensor(w)
            out = jnp.matmul(xq, wq.T) + b[None, :]
            return out * (sw * sx)
        key = jax.random.key(seed)
        k = jax.random.split(key, 5)
        B, N, D, H = (8, 256, 256, 1024)
        return {'x': jax.random.normal(k[0], (B, N, D), dtype=jnp.float32), 'w1': jax.random.normal(k[1], (H, D), dtype=jnp.float32) * 0.02, 'b1': jax.random.normal(k[2], (H,), dtype=jnp.float32) * 0.02, 'w2': jax.random.normal(k[3], (D, H), dtype=jnp.float32) * 0.02, 'b2': jax.random.normal(k[4], (D,), dtype=jnp.float32) * 0.02}
    _L1_ffn_all = _L1_ffn_setup()
    _L1_ffn_in = {k: v for k, v in _L1_ffn_all.items() if k in ('w1', 'b1', 'w2', 'b2')}
    del _L1_ffn_all
    return {'x': x, 'L0_tok_W': _L0_tok_in['W'], 'L0_tok_b': _L0_tok_in['b'], 'L0_attn_Wq': _L0_attn_in['Wq'], 'L0_attn_Wk': _L0_attn_in['Wk'], 'L0_attn_Wv': _L0_attn_in['Wv'], 'L0_ffn_wq': _L0_ffn_in['wq'], 'L0_ffn_wk': _L0_ffn_in['wk'], 'L0_ffn_wv': _L0_ffn_in['wv'], 'L0_ffn_wo': _L0_ffn_in['wo'], 'L0_ffn_w1': _L0_ffn_in['w1'], 'L0_ffn_w2': _L0_ffn_in['w2'], 'L0_ffn_w3': _L0_ffn_in['w3'], 'L0_ffn_attn_norm_w': _L0_ffn_in['attn_norm_w'], 'L0_ffn_ff_norm_w': _L0_ffn_in['ff_norm_w'], 'L0_ffn_moe_norm_w': _L0_ffn_in['moe_norm_w'], 'L0_ffn_router_w': _L0_ffn_in['router_w'], 'L0_ffn_ew1': _L0_ffn_in['ew1'], 'L0_ffn_ew2': _L0_ffn_in['ew2'], 'L0_ffn_ew3': _L0_ffn_in['ew3'], 'L1_attn_Wqkv': _L1_attn_in['Wqkv'], 'L1_attn_Wout': _L1_attn_in['Wout'], 'L1_ffn_w1': _L1_ffn_in['w1'], 'L1_ffn_b1': _L1_ffn_in['b1'], 'L1_ffn_w2': _L1_ffn_in['w2'], 'L1_ffn_b2': _L1_ffn_in['b2']}

def reference(x, L0_tok_W, L0_tok_b, L0_attn_Wq, L0_attn_Wk, L0_attn_Wv, L0_ffn_wq, L0_ffn_wk, L0_ffn_wv, L0_ffn_wo, L0_ffn_w1, L0_ffn_w2, L0_ffn_w3, L0_ffn_attn_norm_w, L0_ffn_ff_norm_w, L0_ffn_moe_norm_w, L0_ffn_router_w, L0_ffn_ew1, L0_ffn_ew2, L0_ffn_ew3, L1_attn_Wqkv, L1_attn_Wout, L1_ffn_w1, L1_ffn_b1, L1_ffn_w2, L1_ffn_b2):
    import jax
    import jax.numpy as jnp

    def _L0_tok_ref(x, W, b):
        import jax, jax.numpy as jnp
        import numpy as np
        from jax import lax
        ALPHA = 0.1
        B, C_IN, T, D_MODEL = (32, 128, 512, 256)

        def _ewma_scan(xt):

            def step(carry, xi):
                carry = ALPHA * xi + (1.0 - ALPHA) * carry
                return (carry, carry)
            _, ys = lax.scan(step, xt[0], xt[1:])
            return jnp.concatenate([xt[:1], ys], axis=0)
        xp = jnp.transpose(x, (0, 2, 1))
        xt = jnp.moveaxis(xp, 1, 0)
        fwd = _ewma_scan(xt)
        bwd = _ewma_scan(xt[::-1])[::-1]
        ewma = jnp.moveaxis((fwd + bwd) * 0.5, 0, 1)
        return jnp.einsum('btc,dc->btd', ewma, W) + b

    def _L0_attn_ref(x, Wq, Wk, Wv):
        import jax, jax.numpy as jnp
        import numpy as np

        def _rope_tables(T, d):
            half = d // 2
            i = jnp.arange(half, dtype=jnp.float32)
            theta = 10000.0 ** (-2.0 * i / d)
            m = jnp.arange(T, dtype=jnp.float32)[:, None]
            ang = m * theta[None, :]
            return (jnp.cos(ang), jnp.sin(ang))

        def _rotate(v, cos, sin):
            B, T, d = v.shape
            half = d // 2
            v2 = v.reshape(B, T, half, 2)
            even, odd = (v2[..., 0], v2[..., 1])
            c = cos[None, :, :]
            s = sin[None, :, :]
            new_even = even * c - odd * s
            new_odd = even * s + odd * c
            return jnp.stack([new_even, new_odd], axis=-1).reshape(B, T, d)
        B, T, d = x.shape
        cos, sin = _rope_tables(T, d)
        Q = jnp.einsum('btd,ed->bte', x, Wq)
        K = jnp.einsum('btd,ed->bte', x, Wk)
        V = jnp.einsum('btd,ed->bte', x, Wv)
        Qr = _rotate(Q, cos, sin)
        Kr = _rotate(K, cos, sin)
        scores = jnp.einsum('bqd,bkd->bqk', Qr, Kr) / jnp.sqrt(jnp.float32(d))
        mask = jnp.tril(jnp.ones((T, T), dtype=bool), k=1)
        scores = jnp.where(mask[None, :, :], scores, -jnp.inf)
        attn = jax.nn.softmax(scores, axis=-1)
        out = jnp.einsum('bqk,bkd->bqd', attn, V)
        return out

    def _L0_ffn_ref(x, wq, wk, wv, wo, w1, w2, w3, attn_norm_w, ff_norm_w, moe_norm_w, router_w, ew1, ew2, ew3):
        import jax, jax.numpy as jnp
        import numpy as np
        D = 256
        H = 16
        FF = 1024
        E = 8
        K = 2
        EH = 256
        B, S = (2, 512)
        EPS = 1e-05

        def rmsnorm(x, w):
            v = jnp.mean(jnp.square(x), axis=-1, keepdims=True)
            return x * jax.lax.rsqrt(v + EPS) * w

        def _dense_path(x, wq, wk, wv, wo, w1, w2, w3, attn_norm_w, ff_norm_w):
            b, s, d = x.shape
            hd = d // H
            q = (x @ wq).reshape(b, s, H, hd)
            k = (x @ wk).reshape(b, s, H, hd)
            v = (x @ wv).reshape(b, s, H, hd)
            scores = jnp.einsum('bqhd,bkhd->bhqk', q, k) / np.sqrt(hd).astype(np.float32)
            causal = jnp.tril(jnp.ones((s, s), bool))
            scores = jnp.where(causal, scores, jnp.finfo(scores.dtype).min)
            attn = jax.nn.softmax(scores, axis=-1)
            o = jnp.einsum('bhqk,bkhd->bqhd', attn, v).reshape(b, s, d)
            h = x + rmsnorm(o @ wo, attn_norm_w)
            ffn = jax.nn.silu(h @ w1) * (h @ w3) @ w2
            return h + rmsnorm(ffn, ff_norm_w)

        def _sparse_path(x, router_w, ew1, ew2, ew3, moe_norm_w):
            b, s, d = x.shape
            xt = x.reshape(-1, d)
            probs = jax.nn.softmax(xt @ router_w, axis=-1)
            topw, topi = jax.lax.top_k(probs, K)
            g = jax.nn.silu(jnp.einsum('td,edh->eth', xt, ew1)) * jnp.einsum('td,edh->eth', xt, ew3)
            eo = jnp.einsum('eth,ehd->ted', g, ew2)
            sel = jnp.take_along_axis(eo, topi[:, :, None], axis=1)
            moe_out = jnp.sum(topw[:, :, None] * sel, axis=1).reshape(b, s, d)
            return rmsnorm(moe_out, moe_norm_w)
        dense_out = _dense_path(x, wq, wk, wv, wo, w1, w2, w3, attn_norm_w, ff_norm_w)
        sparse_out = _sparse_path(x, router_w, ew1, ew2, ew3, moe_norm_w)
        return dense_out + sparse_out

    def _L1_attn_ref(x, Wqkv, Wout):
        import jax, jax.numpy as jnp
        import numpy as np
        B, T, D, H = (4, 512, 256, 16)
        HEAD_DIM = D // H
        LOCAL_WINDOW = 128

        def _rotate_half(t):
            t1, t2 = jnp.split(t, 2, axis=-1)
            return jnp.concatenate([-t2, t1], axis=-1)

        def _apply_rope(q, k):
            Tq, d = (q.shape[2], q.shape[3])
            half = d // 2
            theta = 1.0 / 10000.0 ** (jnp.arange(half, dtype=jnp.float32) / half)
            pos = jnp.arange(Tq, dtype=jnp.float32)
            freqs = pos[:, None] * theta[None, :]
            freqs = jnp.concatenate([freqs, freqs], axis=-1)
            cos = jnp.cos(freqs)[None, None]
            sin = jnp.sin(freqs)[None, None]
            q = q * cos + _rotate_half(q) * sin
            k = k * cos + _rotate_half(k) * sin
            return (q, k)
        Bx, Tx, C = x.shape
        h, d, w = (H, HEAD_DIM, LOCAL_WINDOW)
        qkv = x @ Wqkv
        q, k, v = jnp.split(qkv, 3, axis=-1)
        q = q.reshape(Bx, Tx, h, d).transpose(0, 2, 1, 3)
        k = k.reshape(Bx, Tx, h, d).transpose(0, 2, 1, 3)
        v = v.reshape(Bx, Tx, h, d).transpose(0, 2, 1, 3)
        q, k = _apply_rope(q, k)
        idx = jnp.arange(Tx)
        dist = idx[None, :] - idx[:, None]
        allowed = (dist <= 0) & (dist >= -(w - 1))
        scores = jnp.einsum('bhqd,bhkd->bhqk', q, k) / jnp.sqrt(jnp.float32(d))
        scores = jnp.where(allowed[None, None], scores, -jnp.inf)
        weights = jax.nn.softmax(scores, axis=-1)
        out = jnp.einsum('bhqk,bhkd->bhqd', weights, v)
        out = out.transpose(0, 2, 1, 3).reshape(Bx, Tx, C)
        return out @ Wout

    def _L1_ffn_ref(x, w1, b1, w2, b2):
        import jax, jax.numpy as jnp
        import numpy as np
        QP = 127.0
        MIN_RANGE = 1e-06

        def _ste_round(x):
            return x + jax.lax.stop_gradient(jnp.round(x) - x)

        def _quant_per_tensor(x):
            scale = jnp.maximum(jnp.max(jnp.abs(x)), MIN_RANGE) / QP
            return (_ste_round(x / scale), scale)

        def _qlinear(x2d, w, b):
            xq, sx = _quant_per_tensor(x2d)
            wq, sw = _quant_per_tensor(w)
            out = jnp.matmul(xq, wq.T) + b[None, :]
            return out * (sw * sx)
        B, N, D = x.shape
        h = _qlinear(x.reshape(-1, D), w1, b1)
        h = jax.nn.gelu(h, approximate=False)
        o = _qlinear(h, w2, b2)
        return o.reshape(B, N, -1)
    h = _L0_tok_ref(x, L0_tok_W, L0_tok_b)
    h = h + _L0_attn_ref(_layernorm(h, axis=-1), L0_attn_Wq, L0_attn_Wk, L0_attn_Wv)
    h = h + _L0_ffn_ref(_layernorm(h, axis=-1), L0_ffn_wq, L0_ffn_wk, L0_ffn_wv, L0_ffn_wo, L0_ffn_w1, L0_ffn_w2, L0_ffn_w3, L0_ffn_attn_norm_w, L0_ffn_ff_norm_w, L0_ffn_moe_norm_w, L0_ffn_router_w, L0_ffn_ew1, L0_ffn_ew2, L0_ffn_ew3)
    h = h + _L1_attn_ref(_layernorm(h, axis=-1), L1_attn_Wqkv, L1_attn_Wout)
    h = h + _L1_ffn_ref(_layernorm(h, axis=-1), L1_ffn_w1, L1_ffn_b1, L1_ffn_w2, L1_ffn_b2)
    return h

_drawn_inputs = setup_inputs


def setup_inputs(seed=0):
    import zlib

    import numpy as np

    out = dict(_drawn_inputs(seed))
    spreads = {'L0_ffn_attn_norm_w': (1.0, 0.2),
     'L0_ffn_ff_norm_w': (1.0, 0.2),
     'L0_ffn_moe_norm_w': (1.0, 0.2)}
    factors = {'L0_ffn_wq': 5.507, 'L0_ffn_wk': 5.211, 'L1_ffn_b1': 8.0, 'L1_ffn_b2': 8.0}
    for name, (base, spread) in spreads.items():
        noise = np.random.default_rng([zlib.crc32(name.encode()), seed]).standard_normal(out[name].shape)
        drawn = base * np.exp(spread * noise) if base else spread * noise
        out[name] = jnp.asarray(drawn.astype(out[name].dtype))
    for name, factor in factors.items():
        out[name] = (out[name] * factor).astype(out[name].dtype)
    return out
```

```python
from contextlib import ExitStack

import concourse.bass as bass
from concourse import mybir
import numpy as np

F32 = mybir.dt.float32
F32R = mybir.dt.float32r
BF16 = mybir.dt.bfloat16
U32 = mybir.dt.uint32
ACT = mybir.ActivationFunctionType
ALU = mybir.AluOpType
AX_X = mybir.AxisListType.X

P = 128
B, C_IN, T = 4, 128, 750
D, KC = 256, 2
TT, NT = 125, 6
NTILES = B * NT
BANK = 512
LN_EPS = 1e-5
SEGS = ((0, BANK), (BANK, T))
NEG = -1e30


class Count:

    def __init__(self, shared, name, per):
        self.shared, self.name, self.per, self.used = shared, name, per, False

    @property
    def sem(self):
        self.used = True
        return self.shared.get(self.name)

    def at(self, i, k=None):
        return i * self.per + (self.per if k is None else k) + self.shared.left.get(self.name, 0)


class SharedSemaphores:

    def __init__(self, nc, stack):
        self.nc, self.stack, self.held, self.left = nc, stack, {}, {}

    def get(self, name):
        if name not in self.held:
            self.held[name] = self.stack.enter_context(self.nc.semaphore(name))
        return self.held[name]

    def close(self, counts):
        for c in counts.values():
            if c.used:
                self.left[c.name] = self.left.get(c.name, 0) + B * c.per


class Memory:

    def __init__(self, nc, stack, keep=None):
        self.nc, self.stack, self.keep = nc, stack, keep.keep if keep else stack
        self.shared = keep.shared if keep else SharedSemaphores(nc, stack)

    def sb(self, name, shape, dt):
        return self.stack.enter_context(self.nc.sbuf_tensor(name, shape, dt))

    def ps(self, name, shape):
        return self.stack.enter_context(self.nc.psum_tensor(name, shape, F32))

    def sem(self, name):
        return self.keep.enter_context(self.nc.semaphore(name))

    def counts(self, **per):
        return {k: Count(self.shared, k, n) for k, n in per.items()}


def split3(eng, out, lhs, rhs, first=True, last=True):
    eng.matmul(out, lhs[0], rhs[0], start=first, stop=False)
    eng.matmul(out, lhs[0], rhs[1], start=False, stop=False)
    return eng.matmul(out, lhs[1], rhs[0], start=False, stop=last)


def stage_tok_attn(nc, keep, io, h, ident, identb):
    with ExitStack() as stack:
        m = Memory(nc, stack, keep)
        x_sb = m.sb("a_x", [P, B, T], F32)
        w_raw = m.sb("a_w_raw", [P, 3, KC, D], F32)
        wt_raw = m.sb("a_wt_raw", [P, KC, P], F32)
        tok_wT = m.sb("a_tok_wT", [P, D], F32)
        bias = m.sb("a_bias", [TT, 2, D], F32)
        w_hi = m.sb("a_w_hi", [P, 3, KC, D], F32R)
        w_lo = m.sb("a_w_lo", [P, 3, KC, D], F32R)
        cos = m.sb("a_cos", [P, T], F32)
        sin = m.sb("a_sin", [P, T], F32)
        mask = m.sb("a_mask", [TT, 2 * TT], BF16)
        decay = m.sb("a_decay", [P, T], F32)
        xs = m.sb("a_xs", [P, T], F32)
        fwd = m.sb("a_fwd", [P, T], F32)
        bwd = m.sb("a_bwd", [P, T], F32)
        ew = m.sb("a_ew", [P, T], F32)
        stats = m.sb("a_stats", [TT, NT, 6], F32)
        waiter = m.sb("a_waiter", [TT, 1], F32)
        mv = m.sb("a_mv", [TT, NT, 2], F32)
        rstd = m.sb("a_rstd", [TT, NT], F32)
        half = m.sb("a_half", [TT, NT], F32)
        u = m.sb("a_u", [TT, NT, D], F32)
        uT_hi = m.sb("a_uT_hi", [P, KC, T], F32R)
        uT_lo = m.sb("a_uT_lo", [P, KC, T], F32R)
        prod = m.sb("a_prod", [P, 4, T], F32)
        rot = m.sb("a_rot", [P, 2, KC, T], F32)
        qk_hi = m.sb("a_qk_hi", [P, 2, KC, T], F32R)
        qk_lo = m.sb("a_qk_lo", [P, 2, KC, T], F32R)
        v_hi = m.sb("a_v_hi", [TT, NT, D], F32R)
        v_lo = m.sb("a_v_lo", [TT, NT, D], F32R)
        neg_max = m.sb("a_neg_max", [TT, NT], F32)
        denom = m.sb("a_denom", [TT, NT], F32)
        rden = m.sb("a_rden", [TT, NT], F32)
        probs = m.sb("a_probs", [TT, 2, T], F32)
        pT_hi = m.sb("a_pT_hi", [TT, 2, NT, TT], F32R)
        pT_lo = m.sb("a_pT_lo", [TT, 2, NT, TT], F32R)
        ps = m.ps("a_ps", [P, 8, BANK])

        load = m.sem("a_load")
        set_wT = m.sem("a_set_wT")
        set_hi = m.sem("a_set_hi")
        set_lo = m.sem("a_set_lo")
        set_scale = m.sem("a_set_scale")
        set_const = m.sem("a_set_const")
        c = m.counts(xs=1, scan=2, ew=1, tok_mm=3, h=3, stats=6, mv=6, ve=1, rstd=1, u=6, uT_mm=2,
                     uT_hi=2, uT_lo=2, qk_mm=2, rope_mul=8, rope_sum=4, qk_hi=2, qk_lo=2, v_mm=3, v_hi=3,
                     v_lo=3, s_mm=6, neg_max=6, exp=6, pT_mm=6, pT_hi=6, pT_lo=6, rden=6, pv_mm=6, h_upd=6)

        def flat(bank):
            return ps[:, bank:bank + 2, :].rearrange("p b n -> p (b n)")

        def width(i):
            return min(T, (i + 2) * TT)

        block = stack.enter_context(nc.Block())
        loads = 16 * 11

        @block.sync
        def _(sp):
            sp.dma_start(wt_raw[:], io["L0_tok_W"].rearrange("(c p) d -> p c d", p=P)).then_inc(load, 16)
            sp.dma_start(x_sb[:], io["x"].rearrange("b c t -> c b t")).then_inc(load, 16)
            for n, name in enumerate(("L0_attn_Wq", "L0_attn_Wk")):
                sp.dma_start(w_raw[:, n], io[name].rearrange("(p c) d -> p c d", c=KC)).then_inc(load, 16)
            sp.dma_start(w_raw[:, 2], io["L0_attn_Wv"].rearrange("(c p) d -> p c d", p=P)).then_inc(load, 16)
            for k in range(2):
                sp.dma_start(bias[:, k], io["L0_tok_b"].rearrange("(a d) -> a d", a=1).to_broadcast([TT, D]))\
                  .then_inc(load, 16)
            sp.dma_start(cos[:], io["cos_one"]).then_inc(load, 16)
            sp.dma_start(sin[:], io["sin_one"]).then_inc(load, 16)
            sp.dma_start(mask[:], io["mask_next"]).then_inc(load, 16)
            sp.dma_start(half[:], io["minus_half"]).then_inc(load, 16)

        @block.tensor
        def _(pe):
            pe.wait_ge(load, loads)
            for ec in range(KC):
                mm = pe.transpose(ps[:, 0, ec * P:(ec + 1) * P], wt_raw[:, ec, :], ident[:])
            mm.then_inc(set_wT, 1)
            pe.wait_ge(set_scale, 1)
            for n in range(3):
                for kc in range(KC):
                    for ec in range(KC):
                        mm = pe.transpose(ps[:, 1 + n, (kc * KC + ec) * P:(kc * KC + ec + 1) * P],
                                          w_raw[:, n, ec, kc * P:(kc + 1) * P], ident[:])
                mm.then_inc(set_wT, 1)
            pe.wait_ge(set_lo, 3)
            with pe.Fori(0, B) as b:
                pe.wait_ge(c["ew"].sem, c["ew"].at(b))
                for g in range(3):
                    for i in (2 * g, 2 * g + 1):
                        mm = pe.matmul(ps[:TT, g, (i % 2) * D:(i % 2 + 1) * D], ew[:, i * TT:(i + 1) * TT],
                                       tok_wT[:], start=True, stop=True)
                    mm.then_inc(c["tok_mm"].sem, 1)
                for i in range(NT):
                    pe.wait_ge(c["u"].sem, c["u"].at(b, i + 1))
                    if i == 0:
                        pe.wait_ge(c["h_upd"].sem, c["h_upd"].at(b, 0))
                    for kc in range(KC):
                        mm = pe.transpose(ps[:, 4 + kc + 2 * (i // 4), (i % 4) * TT:(i % 4 + 1) * TT],
                                          u[:, i, kc * P:(kc + 1) * P], ident[:TT, :TT])
                    if i in (3, 5):
                        mm.then_inc(c["uT_mm"].sem, 1)
                pe.wait_ge(c["uT_lo"].sem, c["uT_lo"].at(b))
                pe.wait_ge(c["h"].sem, c["h"].at(b))
                for n in range(2):
                    for ec in range(KC):
                        for s0, s1 in SEGS:
                            for kc in range(KC):
                                mm = split3(pe, flat(4 * n + 2 * ec)[:, s0:s1],
                                            [w[:, n, kc, ec * P:(ec + 1) * P] for w in (w_hi, w_lo)],
                                            [t[:, kc, s0:s1] for t in (uT_hi, uT_lo)], kc == 0, kc == KC - 1)
                    mm.then_inc(c["qk_mm"].sem, 1)
                pe.wait_ge(c["rope_mul"].sem, c["rope_mul"].at(b, 4))
                for g in range(3):
                    for i in (2 * g, 2 * g + 1):
                        for kc in range(KC):
                            mm = split3(pe, ps[:TT, g, (i % 2) * D:(i % 2 + 1) * D],
                                        [t[:, kc, i * TT:(i + 1) * TT] for t in (uT_hi, uT_lo)],
                                        [w[:, 2, kc, :] for w in (w_hi, w_lo)], kc == 0, kc == KC - 1)
                    mm.then_inc(c["v_mm"].sem, 1)

                def scores(i):
                    pe.wait_ge(c["qk_lo"].sem, c["qk_lo"].at(b))
                    if i < 2:
                        pe.wait_ge(c["v_lo"].sem, c["v_lo"].at(b))
                    else:
                        pe.wait_ge(c["exp"].sem, c["exp"].at(b, i - 1))
                    out = flat(2 * (i % 2))
                    for s0 in range(0, width(i), BANK):
                        s1 = min(s0 + BANK, width(i))
                        s2 = s1 + (s1 - s0) % 2
                        for kc in range(KC):
                            mm = split3(pe, out[:TT, s0:s2], [t[:, 0, kc, i * TT:(i + 1) * TT] for t in (qk_hi, qk_lo)],
                                        [t[:, 1, kc, s0:s2] for t in (qk_hi, qk_lo)], kc == 0, kc == KC - 1)
                            m0 = max(s0, i * TT)
                            if kc == 0 and m0 < s1:
                                pe.matmul(out[:TT, m0:s1], identb[:TT, :TT], mask[:, m0 - i * TT:s1 - i * TT],
                                          start=False, stop=False)
                    mm.then_inc(c["s_mm"].sem, 1)

                def turn_probs(i):
                    pe.wait_ge(c["exp"].sem, c["exp"].at(b, i + 1))
                    if i == 0:
                        pe.wait_ge(c["rope_mul"].sem, c["rope_mul"].at(b))
                    else:
                        pe.wait_ge(c["pT_lo"].sem, c["pT_lo"].at(b, i))
                    for j in range(width(i) // TT):
                        mm = pe.transpose(ps[:TT, 4 + j // 4, (j % 4) * P:(j % 4) * P + TT],
                                          probs[:, i % 2, j * TT:(j + 1) * TT], ident[:TT, :TT])
                    mm.then_inc(c["pT_mm"].sem, 1)

                def weigh(i):
                    pe.wait_ge(c["pT_lo"].sem, c["pT_lo"].at(b, i + 1))
                    if i >= 2:
                        pe.wait_ge(c["h_upd"].sem, c["h_upd"].at(b, i - 1))
                    n = width(i) // TT
                    for j in range(n):
                        mm = split3(pe, ps[:TT, 6 + i % 2, 0:D], [t[:, i % 2, j, :] for t in (pT_hi, pT_lo)],
                                    [t[:, j, :] for t in (v_hi, v_lo)], j == 0, j == n - 1)
                    mm.then_inc(c["pv_mm"].sem, 1)

                scores(0)
                for i in range(NT):
                    if i + 1 < NT:
                        scores(i + 1)
                    turn_probs(i)
                    if i >= 1:
                        weigh(i - 1)
                weigh(NT - 1)

        @block.scalar
        def _(act):
            for n in range(3):
                act.wait_ge(set_wT, n + 2)
                act.activation(w_hi[:, n].rearrange("p k e -> p (k e)"), ps[:, 1 + n, :], ACT.Copy)\
                   .then_inc(set_hi, 1)
            with act.Fori(0, B) as b:
                for g, (i0, i1) in enumerate(((0, 4), (4, 6))):
                    act.wait_ge(c["uT_mm"].sem, c["uT_mm"].at(b, g + 1))
                    if g == 0:
                        act.wait_ge(c["v_mm"].sem, c["v_mm"].at(b, 0))
                    act.activation(uT_hi[:, :, i0 * TT:i1 * TT],
                                   ps[:, 4 + 2 * g:6 + 2 * g, 0:(i1 - i0) * TT], ACT.Copy).then_inc(c["uT_hi"].sem, 1)
                for n in range(2):
                    act.wait_ge(c["rope_sum"].sem, c["rope_sum"].at(b, 2 * n + 2))
                    if n == 0:
                        act.wait_ge(c["s_mm"].sem, c["s_mm"].at(b, 0))
                    act.activation(qk_hi[:, n], rot[:, n], ACT.Copy).then_inc(c["qk_hi"].sem, 1)
                for g in range(3):
                    act.wait_ge(c["v_mm"].sem, c["v_mm"].at(b, g + 1))
                    if g == 0:
                        act.wait_ge(c["pv_mm"].sem, c["pv_mm"].at(b, 0))
                    act.activation(v_hi[:, 2 * g:2 * g + 2, :].rearrange("p i d -> p (i d)"), ps[:TT, g, :], ACT.Copy)\
                       .then_inc(c["v_hi"].sem, 1)

                def exps(i):
                    act.wait_ge(c["neg_max"].sem, c["neg_max"].at(b, i + 1))
                    if i < 2:
                        act.wait_ge(c["pT_mm"].sem, c["pT_mm"].at(b, 0))
                    else:
                        act.wait_ge(c["pT_mm"].sem, c["pT_mm"].at(b, i - 1))
                    act.activation(probs[:, i % 2, 0:width(i)], flat(2 * (i % 2))[:TT, 0:width(i)], ACT.Exp,
                                   bias=neg_max[:, i:i + 1], accum_out=denom[:, i:i + 1]).then_inc(c["exp"].sem, 1)

                def turned_hi(i):
                    act.wait_ge(c["pT_mm"].sem, c["pT_mm"].at(b, i + 1))
                    if i < 2:
                        act.wait_ge(c["pv_mm"].sem, c["pv_mm"].at(b, 0))
                    else:
                        act.wait_ge(c["pv_mm"].sem, c["pv_mm"].at(b, i - 1))
                    n = width(i) // TT
                    act.activation(pT_hi[:, i % 2, 0:n, :],
                                   flat(4).rearrange("p (j q) -> p j q", q=P)[:TT, 0:n, 0:TT], ACT.Copy)\
                       .then_inc(c["pT_hi"].sem, 1)

                exps(0)
                for i in range(NT):
                    if i + 1 < NT:
                        exps(i + 1)
                    turned_hi(i)

        @block.gpsimd
        def _(pool):
            pool.memset(decay[:], 0.9).then_inc(set_const, 1)
            pool.wait_ge(load, loads)
            pool.tensor_scalar(w_raw[:, 0], w_raw[:, 0], float(D) ** -0.5, None, ALU.mult).then_inc(set_scale, 1)
            with pool.Fori(0, B) as b:
                pool.wait_ge(c["ve"].sem, c["ve"].at(b))
                pool.tensor_tensor(rstd[:], rstd[:], half[:], ALU.pow).then_inc(c["rstd"].sem, 1)
                for n in range(2):
                    pool.wait_ge(c["rope_mul"].sem, c["rope_mul"].at(b, 4 * n + 4))
                    if n == 0:
                        pool.wait_ge(c["qk_lo"].sem, c["qk_lo"].at(b, 0))
                    pool.tensor_tensor(rot[:, n, 0], prod[:, 0], prod[:, 1], ALU.subtract)\
                        .then_inc(c["rope_sum"].sem, 1)
                    pool.tensor_tensor(rot[:, n, 1], prod[:, 2], prod[:, 3], ALU.add)\
                        .then_inc(c["rope_sum"].sem, 1)

        @block.vector
        def _(dve):
            dve.wait_ge(set_wT, 1)
            dve.tensor_scalar(tok_wT[:], ps[:, 0, 0:D], 0.5, None, ALU.mult)
            for n in range(3):
                dve.wait_ge(set_hi, n + 1)
                dve.tensor_tensor(w_lo[:, n].rearrange("p k e -> p (k e)"), ps[:, 1 + n, :],
                                  w_hi[:, n].bitcast(F32).rearrange("p k e -> p (k e)"), ALU.subtract)\
                   .then_inc(set_lo, 1)
            dve.wait_ge(set_const, 1)
            with dve.Fori(0, B) as b:
                dve.tensor_scalar(xs[:], x_sb[:, b, :], 0.1, None, ALU.mult).then_inc(c["xs"].sem, 1)
                dve.wait_ge(c["xs"].sem, c["xs"].at(b))
                dve.tensor_tensor_scan(fwd[:], decay[:], xs[:], x_sb[:, b, 0:1], ALU.mult, ALU.add)\
                   .then_inc(c["scan"].sem, 1)
                dve.tensor_tensor_scan(bwd[:, ::-1], decay[:], xs[:, ::-1], x_sb[:, b, T - 1:T], ALU.mult, ALU.add)\
                   .then_inc(c["scan"].sem, 1)
                dve.wait_ge(c["scan"].sem, c["scan"].at(b))
                dve.wait_ge(c["tok_mm"].sem, c["tok_mm"].at(b, 0))
                dve.tensor_tensor(ew[:], fwd[:], bwd[:], ALU.add).then_inc(c["ew"].sem, 1)
                for g in range(3):
                    dve.wait_ge(c["tok_mm"].sem, c["tok_mm"].at(b, g + 1))
                    dve.tensor_tensor(h[:, bass.ds(b * NT + 2 * g, 2), :],
                                      ps[:TT, g, :].rearrange("p (i d) -> p i d", d=D), bias[:], ALU.add)\
                       .then_inc(c["h"].sem, 1)
                    dve.wait_ge(c["h"].sem, c["h"].at(b, g + 1))
                    dve.memset(waiter[:], 0.0)
                    for i in (2 * g, 2 * g + 1):
                        dve.bn_stats(stats[:, i], h[:, b * NT + i, :]).then_inc(c["stats"].sem, 1)
                dve.wait_ge(c["stats"].sem, c["stats"].at(b))
                dve.memset(waiter[:], 0.0)
                for i in range(NT):
                    dve.bn_aggr(mv[:, i], stats[:, i]).then_inc(c["mv"].sem, 1)
                dve.wait_ge(c["mv"].sem, c["mv"].at(b))
                dve.tensor_scalar(rstd[:], mv[:, :, 1], LN_EPS, None, ALU.add).then_inc(c["ve"].sem, 1)
                dve.wait_ge(c["rstd"].sem, c["rstd"].at(b))
                for i in range(NT):
                    if i == 0:
                        dve.wait_ge(c["uT_mm"].sem, c["uT_mm"].at(b, 0))
                    dve.tensor_scalar(u[:, i], h[:, b * NT + i, :], mv[:, i, 0:1], rstd[:, i:i + 1],
                                      ALU.subtract, ALU.mult).then_inc(c["u"].sem, 1)
                for g, (i0, i1) in enumerate(((0, 4), (4, 6))):
                    dve.wait_ge(c["uT_hi"].sem, c["uT_hi"].at(b, g + 1))
                    dve.tensor_tensor(uT_lo[:, :, i0 * TT:i1 * TT], ps[:, 4 + 2 * g:6 + 2 * g, 0:(i1 - i0) * TT],
                                      uT_hi[:, :, i0 * TT:i1 * TT].bitcast(F32), ALU.subtract)\
                       .then_inc(c["uT_lo"].sem, 1)
                for n in range(2):
                    dve.wait_ge(c["qk_mm"].sem, c["qk_mm"].at(b, n + 1))
                    if n == 0:
                        dve.wait_ge(c["rope_sum"].sem, c["rope_sum"].at(b, 0))
                    else:
                        dve.wait_ge(c["rope_sum"].sem, c["rope_sum"].at(b, 2))
                    even, odd = flat(4 * n)[:, 0:T], flat(4 * n + 2)[:, 0:T]
                    for k, (part, table) in enumerate(((even, cos), (odd, sin), (even, sin), (odd, cos))):
                        dve.tensor_tensor(prod[:, k], part, table[:], ALU.mult).then_inc(c["rope_mul"].sem, 1)
                for n in range(2):
                    dve.wait_ge(c["qk_hi"].sem, c["qk_hi"].at(b, n + 1))
                    dve.tensor_tensor(qk_lo[:, n], rot[:, n], qk_hi[:, n].bitcast(F32), ALU.subtract)\
                       .then_inc(c["qk_lo"].sem, 1)
                for g in range(3):
                    dve.wait_ge(c["v_hi"].sem, c["v_hi"].at(b, g + 1))
                    dve.tensor_tensor(v_lo[:, 2 * g:2 * g + 2, :].rearrange("p i d -> p (i d)"), ps[:TT, g, :],
                                      v_hi[:, 2 * g:2 * g + 2, :].bitcast(F32).rearrange("p i d -> p (i d)"),
                                      ALU.subtract).then_inc(c["v_lo"].sem, 1)

                def row_max(i):
                    dve.wait_ge(c["s_mm"].sem, c["s_mm"].at(b, i + 1))
                    dve.tensor_reduce(neg_max[:, i:i + 1], flat(2 * (i % 2))[:TT, 0:width(i)], AX_X, ALU.max,
                                      negate=True).then_inc(c["neg_max"].sem, 1)

                def turned_lo(i):
                    dve.wait_ge(c["pT_hi"].sem, c["pT_hi"].at(b, i + 1))
                    n = width(i) // TT
                    dve.tensor_tensor(pT_lo[:, i % 2, 0:n, :],
                                      flat(4).rearrange("p (j q) -> p j q", q=P)[:TT, 0:n, 0:TT],
                                      pT_hi[:, i % 2, 0:n, :].bitcast(F32), ALU.subtract)\
                       .then_inc(c["pT_lo"].sem, 1)
                    dve.wait_ge(c["exp"].sem, c["exp"].at(b, i + 1))
                    dve.reciprocal(rden[:, i:i + 1], denom[:, i:i + 1]).then_inc(c["rden"].sem, 1)

                def add_out(i):
                    dve.wait_ge(c["pv_mm"].sem, c["pv_mm"].at(b, i + 1))
                    dve.wait_ge(c["rden"].sem, c["rden"].at(b, i + 1))
                    dve.scalar_tensor_tensor(h[:, b * NT + i, :], ps[:TT, 6 + i % 2, 0:D], rden[:, i:i + 1],
                                             h[:, b * NT + i, :], ALU.mult, ALU.add).then_inc(c["h_upd"].sem, 1)

                row_max(0)
                for i in range(NT):
                    if i + 1 < NT:
                        row_max(i + 1)
                    turned_lo(i)
                    if i >= 1:
                        add_out(i - 1)
                add_out(NT - 1)
                dve.wait_ge(c["h_upd"].sem, c["h_upd"].at(b))
        keep.shared.close(c)


H, HD = 16, 16
HG = 4
GROUPS = H // HG
SLOTS = ((0, 0), (0, 1), (1, 0), (1, 1), (0, 2), (2, 0))
STACK = len(SLOTS) * HD
ROWS = STACK + 3
E_N = 8
WINDOW = 128


def stage_heads(nc, keep, io, h, ident, identb, local, route=None, scratch=None):
    L = "d" if local else "b"
    with ExitStack() as stack:
        m = Memory(nc, stack, keep)
        w_hi = m.sb(f"{L}_w_hi", [P, 3, KC, D], F32R)
        w_lo = m.sb(f"{L}_w_lo", [P, 3, KC, D], F32R)
        wo = m.sb(f"{L}_wo", [P, KC, D], F32)
        mask_w = 2 * TT + 2 if local else TT
        mask_q = m.sb(f"{L}_mask_q", [TT, mask_w], BF16)
        mask_k = m.sb(f"{L}_mask_k", [TT, mask_w], BF16)
        half = m.sb(f"{L}_half", [TT, NT], F32)
        stats = m.sb(f"{L}_stats", [TT, NT, 6], F32)
        waiter = m.sb(f"{L}_waiter", [TT, 1], F32)
        one = m.sb(f"{L}_one", [P, 1], F32)
        mv = m.sb(f"{L}_mv", [TT, NT, 2], F32)
        rstd = m.sb(f"{L}_rstd", [TT, NT], F32)
        u = m.sb(f"{L}_u", [TT, NT, D], F32)
        uT_hi = m.sb(f"{L}_uT_hi", [P, KC, T], F32R)
        uT_lo = m.sb(f"{L}_uT_lo", [P, KC, T], F32R)
        part = [m.sb(f"{L}_part{k}", [P, 2, KC, T], BF16) for k in range(3)]
        rest = m.sb(f"{L}_rest", [P, KC, T], F32)
        q_st = m.sb(f"{L}_q_st", [ROWS, H, T], BF16)
        k_st = m.sb(f"{L}_k_st", [ROWS, H, T], BF16)
        v_ext = m.sb(f"{L}_v_ext", [TT, NT, H, 2 * HD], F32)
        neg = m.sb(f"{L}_neg", [TT, NT, H], F32)
        neg_b = m.sb(f"{L}_neg_b", [TT, 2, H], F32)
        negp = [m.sb(f"{L}_negp{k}", [HG, T], BF16) for k in range(3)]
        neg_rest = m.sb(f"{L}_neg_rest", [HG, T], F32)
        pw = 2 * TT + 2 if local else T
        probs = m.sb(f"{L}_probs", [TT, 2, HG, pw], F32)
        pv_sb = m.sb(f"{L}_pv_sb", [P, GROUPS, T], F32)
        rden = m.sb(f"{L}_rden", [TT, NT, H], F32)
        o_full = m.sb(f"{L}_o", [P, NT, D], F32)
        o = o_full[:TT]
        oT = m.sb(f"{L}_oT", [P, 2, KC, TT], F32)
        ps = m.ps(f"{L}_ps", [P, 8, BANK])
        if local:
            prod = m.sb(f"{L}_prod", [P, 4, T], F32)
            rot = m.sb(f"{L}_rot", [P, KC, T], F32)
            cos = m.sb(f"{L}_cos", [P, T], F32)
            sin = m.sb(f"{L}_sin", [P, T], F32)
        else:
            r_raw = m.sb("b_r_raw", [P, KC, E_N], F32)
            r_hi = m.sb("b_r_hi", [P, KC, E_N], F32R)
            r_lo = m.sb("b_r_lo", [P, KC, E_N], F32R)
            norm_w = m.sb("b_norm_w", [TT, D], F32)
            junk = m.sb("b_junk", [TT, D], F32)
            ss = m.sb("b_ss", [TT, NT], F32)
            rms = m.sb("b_rms", [TT, NT], F32)
            hd = o
            hdT_hi = m.sb("b_hdT_hi", [P, 2, KC, TT], F32R)
            hdT_lo = m.sb("b_hdT_lo", [P, 2, KC, TT], F32R)
            r_max = m.sb("b_r_max", [TT, NT], F32)
            r_sum = m.sb("b_r_sum", [TT, NT], F32)
            r_inv = m.sb("b_r_inv", [TT, NT], F32)
            r_sub = m.sb("b_r_sub", [TT, NT, E_N], F32)
            r_exp = m.sb("b_r_exp", [TT, NT, E_N], F32)
            r_prob = m.sb("b_r_prob", [TT, NT, E_N], F32)
            top_v = m.sb("b_top_v", [TT, NT, E_N], F32)
            top_i = m.sb("b_top_i", [TT, NT, E_N], U32)
            top_f = m.sb("b_top_f", [TT, NT, E_N], F32)
            pick = m.sb("b_pick", [TT, 2, NT, E_N], F32)
            iota = m.sb("b_iota", [TT, E_N], F32)

        def flat(bank, n=2):
            return ps[:, bank:bank + n, :].rearrange("p b n -> p (b n)")

        def chunks(n):
            return ps[:, 4 * n:4 * n + 4, :].rearrange("p (c b) n -> p c (b n)", c=KC)[:, :, 0:T]

        firsts = []
        for i in range(NT):
            if local:
                k0 = max(0, i * TT - WINDOW + 1)
                segs = [(0, k0, (i + 1) * TT - k0, WINDOW - 1 - i * TT + k0)]
            elif i < 4:
                segs = [(0, 0, (i + 1) * TT, None)]
            else:
                segs = [(0, 0, 4 * TT, None), (1, 4 * TT, (i - 3) * TT, None)]
            for seg, k0, n, mc in segs:
                per = max(1, min(HG, BANK // n))
                for h0 in range(0, HG, per):
                    firsts.append((i, seg, h0, per, k0, n, mc))
        N_SIDE = len(firsts) + 2

        seconds = []
        for j in range(NT):
            n = min(pw, T - j * TT)
            per = max(1, min(HG, BANK // n))
            banks = 1 if per == HG else 2
            step = 1 if n > BANK else per * banks
            for h0 in range(0, HG, step):
                seconds.append((j, h0, step, per if n <= BANK else 1, n))
        N_SEC = len(seconds)

        load = m.sem(f"{L}_load")
        set_w = m.sem(f"{L}_set_w")
        set_hi = m.sem(f"{L}_set_hi")
        set_const = m.sem(f"{L}_set_const")
        c = m.counts(stats=NT, mv=NT, ve=1, rstd=1, u=NT, uT_mm=2, uT_hi=2, uT_lo=2, qk_mm=2, rope_mul=8,
                     rope_sum=4, part0=2, rest=2, part1=2, part2=2, parts_out=96, stacked=16 * (4 if local else 2) * len(SLOTS), v_mm=3, v=3,
                     side_mm=GROUPS * N_SIDE, side=GROUPS * N_SIDE, neg=GROUPS, neg0=2 * GROUPS,
                     neg1=GROUPS, neg2=GROUPS, neg_in=48 * GROUPS, sec_mm=GROUPS * N_SEC, exp=GROUPS * N_SEC,
                     pv_mm=GROUPS * NT, pv_sb=GROUPS, back_mm=NT, rden=NT, o=NT, oT_mm=NT, oT=NT, wo_mm=NT, h=NT,
                     router_mm=1, r_max=1, r_sub=1, r_exp=1, r_sum=1, r_inv=1, r_prob=1, top_v=NT, top_i=NT,
                     top_f=1, pick=2 * NT, route=1, ss=NT, rms_ve=1, rms=1, hd_t=NT, hd=NT, hdT_mm=NT, hdT_hi=NT,
                     hdT_lo=NT, uT_out=32, hdT_out0=16 * NT, hdT_out1=16 * NT)

        def second_out(x, unit):
            j, h0, nh, per, n = unit
            b0 = 2 * (x % 2)
            if n > BANK:
                return flat(b0)[:TT, 0:n]
            nb = nh // per
            return ps[:TT, b0:b0 + nb, 0:per * n].rearrange("p b (m n) -> p b m n", n=n)

        with ExitStack() as inner:
            raw = pv_sb[:].rearrange("p g t -> p (g t)")[:, 0:3 * KC * D].rearrange("p (n k e) -> p n k e", n=3, k=KC)
            rawp = o_full[:].rearrange("p (n k) e -> p n k e", k=KC)
            names = ("L0_ffn_wq", "L0_ffn_wk", "L0_ffn_wv")
            block = inner.enter_context(nc.Block())
            n_loads = 16 * (9 if local else 10)

            @block.sync
            def _(sp):
                for n in range(3):
                    src = io["L1_attn_Wqkv"][:, n * D:(n + 1) * D] if local else io[names[n]]
                    sp.dma_start(raw[:, n], src.rearrange("(k p) e -> p k e", p=P)).then_inc(load, 16)
                src = io["L1_attn_Wout" if local else "L0_ffn_wo"]
                sp.dma_start(wo[:], src.rearrange("(k p) e -> p k e", p=P)).then_inc(load, 16)
                sp.dma_start(mask_q[:], io["mask_window_q" if local else "mask_causal_q"]).then_inc(load, 16)
                sp.dma_start(mask_k[:], io["mask_window_k" if local else "mask_causal_k"]).then_inc(load, 16)
                sp.dma_start(half[:], io["minus_half"]).then_inc(load, 16)
                if local:
                    sp.dma_start(cos[:], io["cos_heads"]).then_inc(load, 16)
                    sp.dma_start(sin[:], io["sin_heads"]).then_inc(load, 16)
                else:
                    sp.dma_start(r_raw[:], io["L0_ffn_router_w"].rearrange("(k p) e -> p k e", p=P)).then_inc(load, 16)
                    sp.dma_start(norm_w[:], io["L0_ffn_attn_norm_w"].rearrange("(a d) -> a d", a=1)
                                 .to_broadcast([TT, D])).then_inc(load, 16)
                    sp.dma_start(iota[:], io["expert_iota"]).then_inc(load, 16)
                sp.wait_ge(load, n_loads)

            @block.gpsimd
            def _(pool):
                pool.wait_ge(load, n_loads)
                for n in range(3):
                    for k in range(KC):
                        src, dst = raw[:, n, k], rawp[:, n, k]
                        if local and n < 2:
                            src = src.rearrange("p (h a f) -> p a h f", a=2, f=HD // 2)
                            dst = dst.rearrange("p (a h f) -> p a h f", a=2, f=HD // 2)
                        mm = pool.tensor_scalar(dst, src, float(HD) ** -0.5 if n == 0 else 1.0, None, ALU.mult)
                    mm.then_inc(set_w, 1)
                pool.memset(one[:], 1.0)
                pool.memset(v_ext[:], 0.0).then_inc(set_const, 1)
                pool.wait_ge(set_const, 1)
                pool.memset(k_st[96:ROWS], 1.0).then_inc(set_const, 1)
                pool.wait_ge(set_const, 2)
                pool.memset(v_ext[:, :, :, HD:HD + 1], 1.0).then_inc(set_const, 1)

            @block.scalar
            def _(act):
                for n in range(3):
                    act.wait_ge(set_w, n + 1)
                    act.activation(w_hi[:, n], rawp[:, n], ACT.Copy).then_inc(set_hi, 1)
                if not local:
                    act.wait_ge(load, n_loads)
                    act.activation(r_hi[:], r_raw[:], ACT.Copy).then_inc(set_hi, 1)

            @block.vector
            def _(dve):
                for n in range(3):
                    dve.wait_ge(set_hi, n + 1)
                    dve.tensor_tensor(w_lo[:, n], rawp[:, n], w_hi[:, n].bitcast(F32), ALU.subtract)
                if not local:
                    dve.wait_ge(set_hi, 4)
                    dve.tensor_tensor(r_lo[:], r_raw[:], r_hi[:].bitcast(F32), ALU.subtract)

        block = stack.enter_context(nc.Block())

        @block.sync
        def _(sp):
            with sp.Fori(0, B) as b:
                if not local:
                    sp.wait_ge(c["uT_lo"].sem, c["uT_lo"].at(b))
                    for k, t in enumerate((uT_hi, uT_lo)):
                        sp.dma_start(scratch["uT"][k, :, :, bass.ds(b * T, T)], t[:].bitcast(F32))\
                          .then_inc(c["uT_out"].sem, 16)
                for n, dst in enumerate((q_st, k_st)):
                    for k in range(3):
                        sp.wait_ge(c[f"part{k}"].sem, c[f"part{k}"].at(b, n + 1))
                        sp.dma_start(scratch["parts"][n, k].rearrange("(c p) t -> p c t", p=P), part[k][:, n])\
                          .then_inc(c["parts_out"].sem, 16)
                    if n == 0:
                        sp.wait_ge(c["sec_mm"].sem, c["sec_mm"].at(b, 0))
                    sp.wait_ge(c["parts_out"].sem, c["parts_out"].at(b, 48 * (n + 1)))
                    for s, slot in enumerate(SLOTS):
                        src = scratch["parts"][n, slot[n]]
                        if local:
                            src = src.rearrange("(a h f) t -> a f h t", a=2, h=H)
                            for a in range(2):
                                r0 = s * HD + a * (HD // 2)
                                sp.dma_start(dst[r0:r0 + HD // 2], src[a]).then_inc(c["stacked"].sem, 16)
                        else:
                            sp.dma_start(dst[s * HD:(s + 1) * HD], src.rearrange("(h d) t -> d h t", d=HD))\
                              .then_inc(c["stacked"].sem, 16)
                for g in range(GROUPS):
                    sp.wait_ge(c["neg2"].sem, c["neg2"].at(b, g + 1))
                    for k in range(3):
                        sp.dma_start(q_st[STACK + k:STACK + k + 1, g * HG:(g + 1) * HG, :], negp[k][:]).then_inc(c["neg_in"].sem, 16)
                if not local:
                    for i in range(NT):
                        sp.wait_ge(c["hdT_lo"].sem, c["hdT_lo"].at(b, i + 1))
                        for k, t in enumerate((hdT_hi, hdT_lo)):
                            sp.dma_start(scratch["hdT"][k, :, :, bass.ds(b * T + i * TT, TT)],
                                         t[:, i % 2].bitcast(F32)).then_inc(c[f"hdT_out{i % 2}"].sem, 16)
            if not local:
                sp.wait_ge(c["uT_out"].sem, c["uT_out"].at(B - 1))
                for k in range(2):
                    sp.wait_ge(c[f"hdT_out{k}"].sem, c[f"hdT_out{k}"].at(B - 1))

        @block.tensor
        def _(pe):
            with pe.Fori(0, B) as b:
                for i in range(NT):
                    pe.wait_ge(c["u"].sem, c["u"].at(b, i + 1))
                    if i == 0:
                        pe.wait_ge(c["oT"].sem, c["oT"].at(b, 0))
                        if not local:
                            pe.wait_ge(c["hdT_lo"].sem, c["hdT_lo"].at(b, 0))
                    for kc in range(KC):
                        mm = pe.transpose(ps[:, 4 + kc + 2 * (i // 4), (i % 4) * TT:(i % 4 + 1) * TT],
                                          u[:, i, kc * P:(kc + 1) * P], ident[:TT, :TT])
                    if i in (3, 5):
                        mm.then_inc(c["uT_mm"].sem, 1)
                pe.wait_ge(c["uT_lo"].sem, c["uT_lo"].at(b))
                pe.wait_ge(c["h"].sem, c["h"].at(b, 0))
                for n in range(2):
                    for ec in range(KC):
                        for s0, s1 in SEGS:
                            for kc in range(KC):
                                mm = split3(pe, flat(4 * n + 2 * ec)[:, s0:s1],
                                            [w[:, n, kc, ec * P:(ec + 1) * P] for w in (w_hi, w_lo)],
                                            [t[:, kc, s0:s1] for t in (uT_hi, uT_lo)], kc == 0, kc == KC - 1)
                    mm.then_inc(c["qk_mm"].sem, 1)
                if local:
                    pe.wait_ge(c["rope_mul"].sem, c["rope_mul"].at(b, 4))
                else:
                    pe.wait_ge(c["rest"].sem, c["rest"].at(b, 1))
                for g in range(3):
                    for i in (2 * g, 2 * g + 1):
                        for kc in range(KC):
                            mm = split3(pe, ps[:TT, g, (i % 2) * D:(i % 2 + 1) * D],
                                        [t[:, kc, i * TT:(i + 1) * TT] for t in (uT_hi, uT_lo)],
                                        [w[:, 2, kc, :] for w in (w_hi, w_lo)], kc == 0, kc == KC - 1)
                    mm.then_inc(c["v_mm"].sem, 1)
                if not local:
                    for i in range(NT):
                        for kc in range(KC):
                            mm = split3(pe, ps[:TT, 3, i * E_N:(i + 1) * E_N],
                                        [t[:, kc, i * TT:(i + 1) * TT] for t in (uT_hi, uT_lo)],
                                        [w[:, kc, :] for w in (r_hi, r_lo)], kc == 0, kc == KC - 1)
                    mm.then_inc(c["router_mm"].sem, 1)

                side = [0]

                def side_bank():
                    x = side[0]
                    side[0] += 1
                    if x >= 2:
                        pe.wait_ge(c["side"].sem, c["side"].at(b, x - 1))
                    elif x == 0:
                        if local:
                            pe.wait_ge(c["rope_mul"].sem, c["rope_mul"].at(b))
                        else:
                            pe.wait_ge(c["rest"].sem, c["rest"].at(b))
                        pe.wait_ge(c["stacked"].sem, c["stacked"].at(b))
                    return 6 + x % 2

                def first(g, unit):
                    i, seg, h0, per, k0, n, mc = unit
                    bank = side_bank()
                    for k in range(per):
                        hh = g * HG + h0 + k
                        out = ps[:TT, bank, k * n:(k + 1) * n]
                        mm = pe.matmul(out, q_st[0:STACK, hh, i * TT:(i + 1) * TT], k_st[0:STACK, hh, k0:k0 + n],
                                       start=True, stop=True)
                        if local:
                            mm = pe.matmul(out, identb[:TT, :TT], mask_q[:, mc:mc + n], start=False, stop=True,
                                           skip_group_check=True)
                        elif k0 + n == (i + 1) * TT:
                            mm = pe.matmul(out[:, n - TT:n], identb[:TT, :TT], mask_q[:], start=False, stop=True,
                                           skip_group_check=True)
                    mm.then_inc(c["side_mm"].sem, 1)

                def turn_max(g):
                    pe.wait_ge(c["neg"].sem, c["neg"].at(b, g + 1))
                    for t0, t1 in ((0, 4), (4, 6)):
                        bank = side_bank()
                        for i in range(t0, t1):
                            mm = pe.transpose(ps[:HG, bank, (i - t0) * TT:(i - t0 + 1) * TT],
                                              neg[:, i, g * HG:(g + 1) * HG], ident[:TT, :TT])
                        mm.then_inc(c["side_mm"].sem, 1)

                def second(g, k):
                    x = g * N_SEC + k
                    j, h0, nh, per, n = seconds[k]
                    if x >= 2:
                        pe.wait_ge(c["exp"].sem, c["exp"].at(b, x - 1))
                    elif x == 0:
                        pe.wait_ge(c["v"].sem, c["v"].at(b))
                        if not local:
                            pe.wait_ge(c["r_sub"].sem, c["r_sub"].at(b))
                    pe.wait_ge(c["neg_in"].sem, c["neg_in"].at(b, 48 * (g + 1)))
                    for e in range(nh):
                        hh = g * HG + h0 + e
                        out = flat(2 * (x % 2))[:TT, 0:n] if n > BANK else \
                            ps[:TT, 2 * (x % 2) + e // per, (e % per) * n:(e % per + 1) * n]
                        for s0 in range(0, n, BANK):
                            s1 = min(n, s0 + BANK)
                            mm = pe.matmul(out[:, s0:s1], k_st[0:ROWS, hh, j * TT:(j + 1) * TT],
                                           q_st[0:ROWS, hh, j * TT + s0:j * TT + s1], start=True, stop=True)
                        w = min(mask_w, n)
                        mm = pe.matmul(out[:, 0:w], identb[:TT, :TT], mask_k[:, 0:w], start=False, stop=True,
                                       skip_group_check=True)
                    mm.then_inc(c["sec_mm"].sem, 1)

                def weigh(g, j):
                    last = g * N_SEC + max(k for k, s in enumerate(seconds) if s[0] == j)
                    pe.wait_ge(c["exp"].sem, c["exp"].at(b, last + 1))
                    if j == 0 and g >= 1:
                        pe.wait_ge(c["pv_sb"].sem, c["pv_sb"].at(b, g))
                    q0, q1 = j * TT, min(T, j * TT + pw)
                    for bank, (s0, s1) in enumerate(SEGS):
                        a0, a1 = max(q0, s0), min(q1, s1)
                        if a0 >= a1:
                            continue
                        opens = not any(jj * TT < s1 and min(T, jj * TT + pw) > s0 for jj in range(j))
                        for e in range(HG):
                            mm = pe.matmul(ps[32 * e:32 * e + 32, 4 + bank, a0 - s0:a1 - s0],
                                           v_ext[:, j, g * HG + e, :],
                                           probs[:, (g * NT + j) % 2, e, a0 - q0:a1 - q0],
                                           start=opens, stop=True, skip_group_check=not opens)
                    mm.then_inc(c["pv_mm"].sem, 1)

                for unit in firsts:
                    first(0, unit)
                turn_max(0)
                share = -(-len(firsts) // 4)
                for g in range(GROUPS):
                    for j in range(NT):
                        for k in range(N_SEC):
                            if seconds[k][0] == j:
                                second(g, k)
                        if j >= 1:
                            weigh(g, j - 1)
                        if g + 1 < GROUPS:
                            if j < 4:
                                for unit in firsts[j * share:(j + 1) * share]:
                                    first(g + 1, unit)
                            elif j == 4:
                                turn_max(g + 1)
                    weigh(g, NT - 1)
                pe.wait_ge(c["pv_sb"].sem, c["pv_sb"].at(b))
                pe.wait_ge(c["exp"].sem, c["exp"].at(b))

                def project(i):
                    pe.wait_ge(c["oT"].sem, c["oT"].at(b, i + 1))
                    for kc in range(KC):
                        mm = pe.matmul(ps[:TT, i, 0:D], oT[:, i % 2, kc, :], wo[:, kc, :],
                                       start=kc == 0, stop=kc == KC - 1)
                    mm.then_inc(c["wo_mm"].sem, 1)

                for i in range(NT):
                    for g in range(GROUPS):
                        mm = pe.transpose(ps[:TT, i, g * P:(g + 1) * P], pv_sb[:, g, i * TT:(i + 1) * TT], ident[:])
                    mm.then_inc(c["back_mm"].sem, 1)
                for i in range(NT):
                    pe.wait_ge(c["o"].sem, c["o"].at(b, i + 1))
                    if i >= 2:
                        pe.wait_ge(c["oT"].sem, c["oT"].at(b, i - 1))
                    else:
                        pe.wait_ge(c["side"].sem, c["side"].at(b))
                    for kc in range(KC):
                        mm = pe.transpose(ps[:, 6 + i % 2, kc * TT:(kc + 1) * TT], o[:, i, kc * P:(kc + 1) * P],
                                          ident[:TT, :TT])
                    mm.then_inc(c["oT_mm"].sem, 1)
                    if i >= 1:
                        project(i - 1)
                project(NT - 1)
                if not local:
                    for i in range(NT):
                        pe.wait_ge(c["hd"].sem, c["hd"].at(b, i + 1))
                        if i >= 2:
                            pe.wait_ge(c["hdT_lo"].sem, c["hdT_lo"].at(b, i - 1))
                        else:
                            pe.wait_ge(c["oT"].sem, c["oT"].at(b))
                        for kc in range(KC):
                            mm = pe.transpose(ps[:, 6 + i % 2, kc * TT:(kc + 1) * TT], hd[:, i, kc * P:(kc + 1) * P],
                                              ident[:TT, :TT])
                        mm.then_inc(c["hdT_mm"].sem, 1)

        @block.scalar
        def _(act):
            with act.Fori(0, B) as b:
                for g, (i0, i1) in enumerate(((0, 4), (4, 6))):
                    act.wait_ge(c["uT_mm"].sem, c["uT_mm"].at(b, g + 1))
                    if g == 0:
                        if local:
                            act.wait_ge(c["v_mm"].sem, c["v_mm"].at(b, 0))
                        else:
                            act.wait_ge(c["router_mm"].sem, c["router_mm"].at(b, 0))
                            act.wait_ge(c["uT_out"].sem, c["uT_out"].at(b, 0))
                    act.activation(uT_hi[:, :, i0 * TT:i1 * TT],
                                   ps[:, 4 + 2 * g:6 + 2 * g, 0:(i1 - i0) * TT], ACT.Copy).then_inc(c["uT_hi"].sem, 1)
                for n in range(2):
                    if n == 0:
                        act.wait_ge(c["stacked"].sem, c["stacked"].at(b, 0))
                    if local:
                        act.wait_ge(c["rope_sum"].sem, c["rope_sum"].at(b, 2 * n + 2))
                        src = rot[:]
                    else:
                        act.wait_ge(c["qk_mm"].sem, c["qk_mm"].at(b, n + 1))
                        src = chunks(n)
                    act.activation(part[0][:, n], src, ACT.Copy).then_inc(c["part0"].sem, 1)
                for g in range(3):
                    act.wait_ge(c["v_mm"].sem, c["v_mm"].at(b, g + 1))
                    if g == 0:
                        act.wait_ge(c["pv_mm"].sem, c["pv_mm"].at(b, 0))
                    for i in (2 * g, 2 * g + 1):
                        a = act.activation(v_ext[:, i, :, 0:HD],
                                           ps[:TT, g, (i % 2) * D:(i % 2 + 1) * D].rearrange("p (h d) -> p h d", d=HD),
                                           ACT.Copy)
                    a.then_inc(c["v"].sem, 1)
                if not local:
                    act.wait_ge(c["r_sub"].sem, c["r_sub"].at(b))
                    act.activation(r_exp[:], r_sub[:], ACT.Exp).then_inc(c["r_exp"].sem, 1)

                def max_part(g):
                    for k, (t0, t1) in enumerate(((0, 4), (4, 6))):
                        x = g * N_SIDE + len(firsts) + k
                        act.wait_ge(c["side_mm"].sem, c["side_mm"].at(b, x + 1))
                        if k == 0:
                            if g == 0:
                                act.wait_ge(c["neg_in"].sem, c["neg_in"].at(b, 0))
                            else:
                                act.wait_ge(c["neg_in"].sem, c["neg_in"].at(b, 48 * g))
                        act.activation(negp[0][:, t0 * TT:t1 * TT], ps[:HG, 6 + x % 2, 0:(t1 - t0) * TT], ACT.Copy)\
                           .then_inc(c["neg0"].sem, 1)

                max_part(0)
                for g in range(GROUPS):
                    for k, unit in enumerate(seconds):
                        j, h0, nh, per, n = unit
                        x = g * N_SEC + k
                        if k and j == NT - 1 and seconds[k - 1][0] == NT - 2 and g + 1 < GROUPS:
                            max_part(g + 1)
                        act.wait_ge(c["sec_mm"].sem, c["sec_mm"].at(b, x + 1))
                        s = g * NT + j
                        act.wait_ge(c["pv_mm"].sem, c["pv_mm"].at(b, max(0, s - 1)))
                        dst = probs[:, s % 2, h0, 0:n] if n > BANK else \
                            probs[:, s % 2, h0:h0 + nh, 0:n].rearrange("p (b m) n -> p b m n", m=per)
                        act.activation(dst, second_out(x, unit), ACT.Exp).then_inc(c["exp"].sem, 1)
                for i in range(NT):
                    act.wait_ge(c["oT_mm"].sem, c["oT_mm"].at(b, i + 1))
                    act.wait_ge(c["wo_mm"].sem, c["wo_mm"].at(b, max(0, i - 1)))
                    act.activation(oT[:, i % 2].rearrange("p k q -> p (k q)"), ps[:, 6 + i % 2, 0:KC * TT], ACT.Copy)\
                       .then_inc(c["oT"].sem, 1)
                if not local:
                    for i in range(NT):
                        act.wait_ge(c["wo_mm"].sem, c["wo_mm"].at(b, i + 1))
                        if i:
                            act.wait_ge(c["ss"].sem, c["ss"].at(b, i))
                        act.activation(junk[:], ps[:TT, i, 0:D], ACT.Square, accum_out=ss[:, i:i + 1])\
                           .then_inc(c["ss"].sem, 1)
                    for i in range(NT):
                        act.wait_ge(c["hdT_mm"].sem, c["hdT_mm"].at(b, i + 1))
                        act.wait_ge(c[f"hdT_out{i % 2}"].sem, c["hdT_out0"].at(b, 32 * (i // 2)))
                        act.activation(hdT_hi[:, i % 2].rearrange("p k q -> p (k q)"), ps[:, 6 + i % 2, 0:KC * TT],
                                       ACT.Copy).then_inc(c["hdT_hi"].sem, 1)

        @block.gpsimd
        def _(pool):
            with pool.Fori(0, B) as b:
                pool.wait_ge(c["ve"].sem, c["ve"].at(b))
                pool.tensor_tensor(rstd[:], rstd[:], half[:], ALU.pow).then_inc(c["rstd"].sem, 1)
                for n in range(2):
                    if local:
                        pool.wait_ge(c["rope_mul"].sem, c["rope_mul"].at(b, 4 * n + 4))
                        if n == 0:
                            pool.wait_ge(c["rest"].sem, c["rest"].at(b, 0))
                        else:
                            pool.wait_ge(c["rest"].sem, c["rest"].at(b, 1))
                        pool.tensor_tensor(rot[:, 0], prod[:, 0], prod[:, 1], ALU.subtract)\
                            .then_inc(c["rope_sum"].sem, 1)
                        pool.tensor_tensor(rot[:, 1], prod[:, 2], prod[:, 3], ALU.add).then_inc(c["rope_sum"].sem, 1)
                    pool.wait_ge(c["rest"].sem, c["rest"].at(b, n + 1))
                    pool.tensor_tensor(part[1][:, n], rest[:], one[:].unsqueeze(2).to_broadcast([P, KC, T]),
                                       ALU.mult).then_inc(c["part1"].sem, 1)
                    pool.wait_ge(c["part1"].sem, c["part1"].at(b, n + 1))
                    pool.tensor_tensor(part[2][:, n], rest[:], part[1][:, n], ALU.subtract).then_inc(c["part2"].sem, 1)
                for g in range(GROUPS):
                    pool.wait_ge(c["side"].sem, c["side"].at(b, (g + 1) * N_SIDE))
                    pool.tensor_tensor(negp[1][:], neg_rest[:], one[:HG].to_broadcast([HG, T]), ALU.mult).then_inc(c["neg1"].sem, 1)
                    pool.wait_ge(c["neg1"].sem, c["neg1"].at(b, g + 1))
                    pool.tensor_tensor(negp[2][:], neg_rest[:], negp[1][:], ALU.subtract).then_inc(c["neg2"].sem, 1)
                if not local:
                    pool.wait_ge(c["rms_ve"].sem, c["rms_ve"].at(b))
                    pool.tensor_tensor(rms[:], rms[:], half[:], ALU.pow).then_inc(c["rms"].sem, 1)

        @block.vector
        def _(dve):
            with dve.Fori(0, B) as b:
                for i in range(NT):
                    dve.bn_stats(stats[:, i], h[:, b * NT + i, :]).then_inc(c["stats"].sem, 1)
                dve.wait_ge(c["stats"].sem, c["stats"].at(b))
                dve.memset(waiter[:], 0.0)
                for i in range(NT):
                    dve.bn_aggr(mv[:, i], stats[:, i]).then_inc(c["mv"].sem, 1)
                dve.wait_ge(c["mv"].sem, c["mv"].at(b))
                dve.tensor_scalar(rstd[:], mv[:, :, 1], LN_EPS, None, ALU.add).then_inc(c["ve"].sem, 1)
                dve.wait_ge(c["rstd"].sem, c["rstd"].at(b))
                for i in range(NT):
                    dve.tensor_scalar(u[:, i], h[:, b * NT + i, :], mv[:, i, 0:1], rstd[:, i:i + 1],
                                      ALU.subtract, ALU.mult).then_inc(c["u"].sem, 1)
                for g, (i0, i1) in enumerate(((0, 4), (4, 6))):
                    dve.wait_ge(c["uT_hi"].sem, c["uT_hi"].at(b, g + 1))
                    dve.tensor_tensor(uT_lo[:, :, i0 * TT:i1 * TT], ps[:, 4 + 2 * g:6 + 2 * g, 0:(i1 - i0) * TT],
                                      uT_hi[:, :, i0 * TT:i1 * TT].bitcast(F32), ALU.subtract)\
                       .then_inc(c["uT_lo"].sem, 1)

                def remainder(n):
                    dve.wait_ge(c["part0"].sem, c["part0"].at(b, n + 1))
                    dve.wait_ge(c["part2"].sem, c["part2"].at(b, n))
                    dve.tensor_tensor(rest[:], rot[:] if local else chunks(n), part[0][:, n], ALU.subtract)\
                       .then_inc(c["rest"].sem, 1)

                for n in range(2):
                    if local:
                        dve.wait_ge(c["qk_mm"].sem, c["qk_mm"].at(b, n + 1))
                        dve.wait_ge(c["rope_sum"].sem, c["rope_sum"].at(b, 2 * n))
                        one, two = chunks(n)[:, 0], chunks(n)[:, 1]
                        for k, (src, table) in enumerate(((one, cos), (two, sin), (one, sin), (two, cos))):
                            dve.tensor_tensor(prod[:, k], src, table[:], ALU.mult).then_inc(c["rope_mul"].sem, 1)
                    remainder(n)
                if not local:
                    logits = ps[:TT, 3, 0:NT * E_N].rearrange("p (i e) -> p i e", e=E_N)
                    dve.wait_ge(c["router_mm"].sem, c["router_mm"].at(b))
                    dve.tensor_reduce(r_max[:], logits, AX_X, ALU.max).then_inc(c["r_max"].sem, 1)
                    dve.wait_ge(c["r_max"].sem, c["r_max"].at(b))
                    dve.tensor_tensor(r_sub[:], logits, r_max[:].unsqueeze(2).to_broadcast([TT, NT, E_N]),
                                      ALU.subtract).then_inc(c["r_sub"].sem, 1)
                    dve.wait_ge(c["r_exp"].sem, c["r_exp"].at(b))
                    dve.tensor_reduce(r_sum[:], r_exp[:], AX_X, ALU.add).then_inc(c["r_sum"].sem, 1)
                    dve.wait_ge(c["r_sum"].sem, c["r_sum"].at(b))
                    dve.reciprocal(r_inv[:], r_sum[:]).then_inc(c["r_inv"].sem, 1)
                    dve.wait_ge(c["r_inv"].sem, c["r_inv"].at(b))
                    dve.tensor_tensor(r_prob[:], r_exp[:], r_inv[:].unsqueeze(2).to_broadcast([TT, NT, E_N]),
                                      ALU.mult).then_inc(c["r_prob"].sem, 1)
                    dve.wait_ge(c["r_prob"].sem, c["r_prob"].at(b))
                    dve.memset(waiter[:], 0.0)
                    for i in range(NT):
                        dve.max(top_v[:, i], r_prob[:, i]).then_inc(c["top_v"].sem, 1)
                    dve.wait_ge(c["top_v"].sem, c["top_v"].at(b))
                    dve.memset(waiter[:], 0.0)
                    for i in range(NT):
                        dve.max_index(top_i[:, i], top_v[:, i], r_prob[:, i]).then_inc(c["top_i"].sem, 1)
                    dve.wait_ge(c["top_i"].sem, c["top_i"].at(b))
                    dve.tensor_copy(top_f[:], top_i[:]).then_inc(c["top_f"].sem, 1)
                    dve.wait_ge(c["top_f"].sem, c["top_f"].at(b))
                    for i in range(NT):
                        for k in range(2):
                            dve.tensor_scalar(pick[:, k, i], iota[:], top_f[:, i, k:k + 1], top_v[:, i, k:k + 1],
                                              ALU.is_equal, ALU.mult).then_inc(c["pick"].sem, 1)
                    dve.wait_ge(c["pick"].sem, c["pick"].at(b))
                    dve.tensor_tensor(route[:, bass.ds(b * NT, NT), :], pick[:, 0], pick[:, 1], ALU.add)\
                       .then_inc(c["route"].sem, 1)

                def side(g, k):
                    x = g * N_SIDE + k
                    dve.wait_ge(c["side_mm"].sem, c["side_mm"].at(b, x + 1))
                    if k < len(firsts):
                        i, seg, h0, per, k0, n, mc = firsts[k]
                        dst = (neg_b[:, i - 4] if seg else neg[:, i])[:, g * HG + h0:g * HG + h0 + per]
                        dve.tensor_reduce(dst, ps[:TT, 6 + x % 2, 0:per * n].rearrange("p (m n) -> p m n", n=n),
                                          AX_X, ALU.max, negate=True).then_inc(c["side"].sem, 1)
                        if k == len(firsts) - 1:
                            dve.wait_ge(c["side"].sem, c["side"].at(b, x + 1))
                            lo = 4 if not local else NT - 1
                            part_neg = neg[:, lo:NT, g * HG:(g + 1) * HG]
                            other = neg_b[:, :, g * HG:(g + 1) * HG] if not local else part_neg
                            dve.tensor_tensor(part_neg, part_neg, other, ALU.min).then_inc(c["neg"].sem, 1)
                    else:
                        t0, t1 = ((0, 4), (4, 6))[k - len(firsts)]
                        dve.wait_ge(c["neg0"].sem, c["neg0"].at(b, 2 * g + k - len(firsts) + 1))
                        dve.wait_ge(c["neg2"].sem, c["neg2"].at(b, g))
                        dve.tensor_tensor(neg_rest[:, t0 * TT:t1 * TT], ps[:HG, 6 + x % 2, 0:(t1 - t0) * TT],
                                          negp[0][:, t0 * TT:t1 * TT], ALU.subtract).then_inc(c["side"].sem, 1)

                for k in range(N_SIDE):
                    side(0, k)
                for g in range(GROUPS):
                    if g + 1 < GROUPS:
                        for k in range(N_SIDE):
                            side(g + 1, k)
                    dve.wait_ge(c["pv_mm"].sem, c["pv_mm"].at(b, (g + 1) * NT))
                    if g == 0:
                        dve.wait_ge(c["back_mm"].sem, c["back_mm"].at(b, 0))
                    dve.tensor_copy(pv_sb[:, g, :], flat(4)[:, 0:T]).then_inc(c["pv_sb"].sem, 1)
                for i in range(NT):
                    dve.wait_ge(c["back_mm"].sem, c["back_mm"].at(b, i + 1))
                    rows = ps[:TT, i, :].rearrange("p (h w) -> p h w", w=2 * HD)
                    dve.reciprocal(rden[:, i], rows[:, :, HD]).then_inc(c["rden"].sem, 1)
                    dve.wait_ge(c["rden"].sem, c["rden"].at(b, i + 1))
                    dve.tensor_tensor(o[:, i].rearrange("p (h d) -> p h d", d=HD), rows[:, :, 0:HD],
                                      rden[:, i].unsqueeze(2).to_broadcast([TT, H, HD]), ALU.mult)\
                       .then_inc(c["o"].sem, 1)
                if local:
                    for i in range(NT):
                        dve.wait_ge(c["wo_mm"].sem, c["wo_mm"].at(b, i + 1))
                        dve.tensor_tensor(h[:, b * NT + i, :], ps[:TT, i, 0:D], h[:, b * NT + i, :], ALU.add)\
                           .then_inc(c["h"].sem, 1)
                else:
                    dve.wait_ge(c["ss"].sem, c["ss"].at(b))
                    dve.tensor_scalar(rms[:], ss[:], 1.0 / D, LN_EPS, ALU.mult, ALU.add).then_inc(c["rms_ve"].sem, 1)
                    dve.wait_ge(c["rms"].sem, c["rms"].at(b))
                    for i in range(NT):
                        dve.scalar_tensor_tensor(hd[:, i], ps[:TT, i, 0:D], rms[:, i:i + 1], norm_w[:],
                                                 ALU.mult, ALU.mult).then_inc(c["hd_t"].sem, 1)
                        dve.wait_ge(c["hd_t"].sem, c["hd_t"].at(b, i + 1))
                        dve.tensor_tensor(hd[:, i], hd[:, i], u[:, i], ALU.add).then_inc(c["hd"].sem, 1)
                        dve.wait_ge(c["hd"].sem, c["hd"].at(b, i + 1))
                        dve.tensor_tensor(h[:, b * NT + i, :], hd[:, i], h[:, b * NT + i, :], ALU.add)\
                           .then_inc(c["h"].sem, 1)
                    for i in range(NT):
                        dve.wait_ge(c["hdT_hi"].sem, c["hdT_hi"].at(b, i + 1))
                        dve.tensor_tensor(hdT_lo[:, i % 2].rearrange("p k q -> p (k q)"),
                                          ps[:, 6 + i % 2, 0:KC * TT],
                                          hdT_hi[:, i % 2].bitcast(F32).rearrange("p k q -> p (k q)"), ALU.subtract)\
                           .then_inc(c["hdT_lo"].sem, 1)
                dve.wait_ge(c["h"].sem, c["h"].at(b))
        keep.shared.close(c)


E_H = 256
FF = 1024
CT = 4
CN = CT * TT
NCH = B * T // CN
PAIRS = E_N // 2
NALL = E_N + FF // E_H


def stage_experts(nc, keep, io, h, route, scratch):
    with ExitStack() as stack:
        m = Memory(nc, stack, keep)
        uT = m.sb("c_uT", [P, 2, KC, B * T], F32R)
        hdT = m.sb("c_hdT", [P, 2, KC, B * T], F32R)
        acc = m.sb("c_acc", [TT, NTILES, D], F32)
        raw = [m.sb(f"c_raw{k}", [P, 3, KC, E_H], F32) for k in range(2)]
        w_hi = [m.sb(f"c_w_hi{k}", [P, 3, KC, E_H], F32R) for k in range(2)]
        w_lo = [m.sb(f"c_w_lo{k}", [P, 3, KC, E_H], F32R) for k in range(2)]
        act_a = m.sb("c_act_a", [P, 2, CN], F32)
        g = m.sb("c_g", [P, 2, CN], F32)
        g_hi = m.sb("c_g_hi", [P, 2, CN], F32R)
        g_lo = m.sb("c_g_lo", [P, 2, CN], F32R)
        norm_w = m.sb("c_norm_w", [TT, 2, D], F32)
        half = m.sb("c_half", [TT, NT], F32)
        junk = m.sb("c_junk", [TT, D], F32)
        ss = m.sb("c_ss", [TT, NTILES], F32)
        rms_p = m.sb("c_rms", [TT, CT], F32)
        t = m.sb("c_t", [TT, CT, D], F32)
        ps = m.ps("c_ps", [P, 8, BANK])

        const_in = m.sem("c_const_in")
        zeroed = m.sem("c_zeroed")
        x_in, hd_in = m.sem("c_x_in"), m.sem("c_hd_in")
        raw_in = [m.sem(f"c_raw_in{k}") for k in range(2)]
        made_hi, made_lo = m.sem("c_made_hi"), m.sem("c_made_lo")
        up_mm, down_mm = m.sem("c_up_mm"), m.sem("c_down_mm")
        silu, gated, gated_hi, gated_lo = m.sem("c_silu"), m.sem("c_gated"), m.sem("c_gated_hi"), m.sem("c_gated_lo")
        added = m.sem("c_added")
        sq, ve, rms_ok, scaled, h_upd = m.sem("c_sq"), m.sem("c_ve"), m.sem("c_rms_ok"), m.sem("c_scaled"), m.sem("c_h")

        def walk(eng, prepare, head, tail):

            def expert(e, par, last=False, before_dense=False, dense=False, final=None, opens=False):
                n0 = e * NCH
                if not last:
                    prepare(e + 1, 1 - par)
                with eng.Fori(1, NCH) as k:
                    head(par, k, n0 + k, dense)
                    tail(par, k - 1, n0 + k - 1, e, dense, final, opens)
                if not last:
                    head(1 - par, 0, n0 + NCH, dense or before_dense)
                tail(par, NCH - 1, n0 + NCH - 1, e, dense, final, opens)

            prepare(0, 0)
            head(0, 0, 0, False)
            with eng.Fori(0, PAIRS - 1) as pair:
                for par in range(2):
                    expert(pair * 2 + par, par)
            expert(E_N - 2, 0)
            expert(E_N - 1, 1, before_dense=True, final=0)
            for e in range(E_N, NALL):
                expert(e, e % 2, last=e == NALL - 1, dense=True, final=1 if e == NALL - 1 else None, opens=e == E_N)

        def skip(*_):
            return

        def raw_count(e, par):
            return (e - par) * 24 + 48

        def tile_of(buf, c, i):
            return buf[:, c * CT + i, :]

        def column_of(buf, c, i):
            return buf[:, bass.ds(c * CT + i, 1)]

        block = stack.enter_context(nc.Block())

        @block.sync
        def _(sp):
            def weights(e, par, dense):
                for k, name in enumerate(("1", "3", "2")):
                    if not dense:
                        src = io[f"L0_ffn_ew{name}"][bass.ds(e, 1), :, :].rearrange("a (k p) n -> p (a k) n", p=P)
                    elif name == "2":
                        s = e - E_N
                        src = io["L0_ffn_w2"][s * E_H:(s + 1) * E_H, :].rearrange("(k p) n -> p k n", p=P)
                    else:
                        s = e - E_N
                        src = io[f"L0_ffn_w{name}"][:, s * E_H:(s + 1) * E_H].rearrange("(k p) n -> p k n", p=P)
                    sp.dma_start(raw[par][:, k], src).then_inc(raw_in[par], 16)

            def rows(c, name, dst, sem):
                for k in range(2):
                    sp.dma_start(dst[:, k, :, c * CN:(c + 1) * CN].bitcast(F32),
                                 scratch[name][k, :, :, c * CN:(c + 1) * CN]).then_inc(sem, 16)
                sp.wait_ge(sem, 32 * (c + 1))

            weights(0, 0, False)
            rows(0, "uT", uT, x_in)
            weights(1, 1, False)
            for k, name in enumerate(("moe_norm_w", "ff_norm_w")):
                sp.dma_start(norm_w[:, k], io[f"L0_ffn_{name}"].rearrange("(a d) -> a d", a=1).to_broadcast([TT, D]))\
                  .then_inc(const_in, 16)
            sp.dma_start(half[:], io["minus_half"]).then_inc(const_in, 16)
            for c in range(1, NCH):
                rows(c, "uT", uT, x_in)
            for c in range(NCH):
                rows(c, "hdT", hdT, hd_in)
            with sp.Fori(1, PAIRS) as pair:
                for par in range(2):
                    sp.wait_ge(made_lo, pair * 2 + par - 1)
                    weights(pair * 2 + par, par, False)
            for e in range(E_N, NALL):
                sp.wait_ge(made_lo, e - 1)
                weights(e, e % 2, True)

        @block.tensor
        def _(pe):
            def prepare(e, par):
                if isinstance(e, int) and e == 0:
                    pe.wait_ge(made_lo, 1)

            def head(par, c, n, dense):
                if isinstance(c, int):
                    pe.wait_ge(made_lo, n // NCH + 1 if isinstance(n, int) else next_expert[0] + 1)
                pe.wait_ge(hd_in if dense else x_in, c * 32 + 32)
                pe.wait_ge(gated, n * 2)
                x = hdT if dense else uT
                for hc in range(2):
                    for k in range(2):
                        for kc in range(KC):
                            mm = split3(pe, ps[:, 2 * hc + k, 0:CN],
                                        [w[par][:, k, kc, hc * P:(hc + 1) * P] for w in (w_hi, w_lo)],
                                        [x[:, s, kc, bass.ds(c * CN, CN)] for s in range(2)], kc == 0, kc == KC - 1)
                    mm.then_inc(up_mm, 1)

            def tail(par, c, n, e, dense, final, opens):
                pe.wait_ge(gated_lo, n * 2 + 2)
                pe.wait_ge(added, n * 4)
                for i in range(CT):
                    for hc in range(2):
                        mm = split3(pe, ps[:TT, 4 + i, 0:D], [x[:, hc, i * TT:(i + 1) * TT] for x in (g_hi, g_lo)],
                                    [w[par][:, 2, hc, :] for w in (w_hi, w_lo)], hc == 0, hc == 1)
                    mm.then_inc(down_mm, 1)

            next_expert = [0]

            def note(e, par):
                next_expert[0] = e

            walk(pe, note, head, tail)

        @block.scalar
        def _(act):
            def prepare(e, par):
                act.wait_ge(raw_in[par], raw_count(e, par))
                if not (isinstance(e, int) and e == 0):
                    act.wait_ge(down_mm, (e - 1) * (CT * NCH))
                act.activation(w_hi[par][:], raw[par][:], ACT.Copy).then_inc(made_hi, 1)

            def head(par, c, n, dense):
                for hc in range(2):
                    act.wait_ge(up_mm, n * 2 + hc + 1)
                    act.wait_ge(gated, n * 2)
                    act.activation(act_a[:, hc], ps[:, 2 * hc, 0:CN], ACT.Silu).then_inc(silu, 1)
                for hc in range(2):
                    act.wait_ge(gated, n * 2 + hc + 1)
                    act.wait_ge(down_mm, n * CT)
                    act.activation(g_hi[:, hc], g[:, hc], ACT.Copy).then_inc(gated_hi, 1)

            def tail(par, c, n, e, dense, final, opens):
                if final is None:
                    return
                for i in range(CT):
                    act.wait_ge(added, n * CT + i + 1)
                    act.wait_ge(sq, c * CT + (final * NTILES + i))
                    act.activation(junk[:], tile_of(acc, c, i), ACT.Square, accum_out=column_of(ss, c, i))\
                       .then_inc(sq, 1)

            walk(act, prepare, head, tail)

        @block.gpsimd
        def _(pool):
            def prepare(e, par):
                pool.wait_ge(made_hi, e + 1)
                pool.tensor_tensor(w_lo[par][:], raw[par][:], w_hi[par][:].bitcast(F32), ALU.subtract)\
                    .then_inc(made_lo, 1)

            def head(par, c, n, dense):
                for hc in range(2):
                    pool.wait_ge(gated_hi, n * 2 + hc + 1)
                    pool.tensor_tensor(g_lo[:, hc], g[:, hc], g_hi[:, hc].bitcast(F32), ALU.subtract)\
                        .then_inc(gated_lo, 1)

            def tail(par, c, n, e, dense, final, opens):
                if final is None:
                    return
                pool.wait_ge(ve, c + (final * NCH + 1))
                pool.tensor_tensor(rms_p[:], rms_p[:], half[:, 0:CT], ALU.pow).then_inc(rms_ok, 1)

            pool.wait_ge(const_in, 48)
            pool.memset(acc[:], 0.0).then_inc(zeroed, 1)
            pool.wait_ge(zeroed, 1)
            walk(pool, prepare, head, tail)

        @block.vector
        def _(dve):
            def head(par, c, n, dense):
                for hc in range(2):
                    dve.wait_ge(silu, n * 2 + hc + 1)
                    dve.wait_ge(gated_lo, n * 2)
                    dve.tensor_tensor(g[:, hc], act_a[:, hc], ps[:, 2 * hc + 1, 0:CN], ALU.mult).then_inc(gated, 1)

            def tail(par, c, n, e, dense, final, opens):
                for i in range(CT):
                    dve.wait_ge(down_mm, n * CT + i + 1)
                    a, out = tile_of(acc, c, i), ps[:TT, 4 + i, 0:D]
                    if opens:
                        dve.wait_ge(scaled, c * CT + CT)
                        dve.tensor_copy(a, out).then_inc(added, 1)
                    elif dense:
                        dve.tensor_tensor(a, out, a, ALU.add).then_inc(added, 1)
                    else:
                        dve.scalar_tensor_tensor(a, out, route[:, c * CT + i, bass.ds(e, 1)], a, ALU.mult, ALU.add)\
                           .then_inc(added, 1)
                if final is not None:
                    dve.wait_ge(sq, c * CT + (final * NTILES + CT))
                    dve.tensor_scalar(rms_p[:], ss[:, bass.ds(c * CT, CT)], 1.0 / D, LN_EPS, ALU.mult, ALU.add)\
                       .then_inc(ve, 1)
                    dve.wait_ge(rms_ok, c + (final * NCH + 1))
                    for i in range(CT):
                        dve.scalar_tensor_tensor(t[:, i], tile_of(acc, c, i), rms_p[:, i:i + 1], norm_w[:, final],
                                                 ALU.mult, ALU.mult).then_inc(scaled, 1)
                    for i in range(CT):
                        dve.wait_ge(scaled, c * CT + (final * NTILES + i + 1))
                        dve.tensor_tensor(tile_of(h, c, i), tile_of(h, c, i), t[:, i], ALU.add).then_inc(h_upd, 1)

            dve.wait_ge(zeroed, 1)
            walk(dve, skip, head, tail)
            dve.wait_ge(h_upd, 2 * NTILES)


FH = 1024
FC = FH // P
QP, MIN_RANGE = 127.0, 1e-6
ROUND = 1.5 * 2.0 ** 23


def stage_quantised(nc, keep, io, h, ident):
    with ExitStack() as stack:
        m = Memory(nc, stack, keep)
        hid = m.sb("e_hid", [P, FC, B * T], F32)
        flat_hid = hid[:].rearrange("p c t -> p (c t)")
        w1 = flat_hid[:, 0:FC * D].rearrange("p (c d) -> p c d", c=FC)
        w2 = flat_hid[:, FC * D:FC * D + KC * FH].rearrange("p (c f) -> p c f", c=KC)
        w1T = m.sb("e_w1T", [P, KC, FC, P], BF16)
        w2T = m.sb("e_w2T", [P, FC, D], BF16)
        b1 = m.sb("e_b1", [P, FC], F32)
        b2 = m.sb("e_b2", [TT, D], F32)
        half = m.sb("e_half", [TT, NT], F32)
        stats = m.sb("e_stats", [TT, NTILES, 6], F32)
        mv = m.sb("e_mv", [TT, NTILES, 2], F32)
        rstd = m.sb("e_rstd", [TT, NTILES], F32)
        u = m.sb("e_u", [TT, NTILES, D], F32)
        uT = m.sb("e_uT", [P, KC, B * T], BF16)
        qh = m.sb("e_qh", [P, 2, FC, CN], BF16)
        peak = m.sb("e_peak", [P, 3], F32)
        peak_u = m.sb("e_peak_u", [TT, NTILES], F32)
        peak_h = m.sb("e_peak_h", [P, NCH * FC], F32)
        top = m.sb("e_top", [P, 4], F32)
        peak_p = m.sb("e_peak_p", [P, 1], F32)
        scale = m.sb("e_scale", [P, 4], F32)
        inv = m.sb("e_inv", [P, 4], F32)
        out_scale = m.sb("e_out_scale", [P, 2], F32)
        b1s = m.sb("e_b1s", [P, FC], F32)
        b2s = m.sb("e_b2s", [TT, D], F32)
        ps = m.ps("e_ps", [P, 8, BANK])

        loaded = m.sem("e_loaded")
        stat, agg, ve, rstd_ok, norm = (m.sem(f"e_{n}") for n in ("stat", "agg", "ve", "rstd_ok", "norm"))
        peaked, topped, scaled = m.sem("e_peaked"), m.sem("e_topped"), m.sem("e_scaled")
        w_shift, w_int, w_turned, w_ready = (m.sem(f"e_{n}") for n in ("w_shift", "w_int", "w_turned", "w_ready"))
        u_shift, u_int, u_turned, u_ready = (m.sem(f"e_{n}") for n in ("u_shift", "u_int", "u_turned", "u_ready"))
        zero_p = m.sem("e_zero_p")
        up_mm, gelu, hid_peak = m.sem("e_up_mm"), m.sem("e_gelu"), m.sem("e_hid_peak")
        q_shift, q_ready, down_mm, added, biased = (m.sem(f"e_{n}") for n in
                                                    ("q_shift", "q_ready", "down_mm", "added", "biased"))
        W1, W2, U, HID = range(4)

        block = stack.enter_context(nc.Block())

        @block.sync
        def _(sp):
            sp.dma_start(w1, io["L1_ffn_w1"].rearrange("(p c) d -> p c d", c=FC)).then_inc(loaded, 16)
            sp.dma_start(w2, io["L1_ffn_w2"].rearrange("(c p) f -> p c f", p=P)).then_inc(loaded, 16)
            sp.dma_start(b1[:], io["L1_ffn_b1"].rearrange("(p c) -> p c", c=FC)).then_inc(loaded, 16)
            sp.dma_start(b2[:], io["L1_ffn_b2"].rearrange("(a d) -> a d", a=1).to_broadcast([TT, D])).then_inc(loaded, 16)
            sp.dma_start(half[:], io["minus_half"]).then_inc(loaded, 16)

        @block.gpsimd
        def _(pool):
            reduce_max = bass.bass_isa.ReduceOp.max

            def over_rows(k, src):
                pool.partition_all_reduce(top[:, k:k + 1], src, P, reduce_max).then_inc(topped, 1)

            pool.memset(peak_p[:], 0.0).then_inc(zero_p, 1)
            pool.wait_ge(loaded, 80)
            for b in range(B):
                cols = slice(b * NT, (b + 1) * NT)
                pool.wait_ge(agg, (b + 1) * NT)
                pool.tensor_scalar(rstd[:, cols], mv[:, cols, 1], LN_EPS, None, ALU.add).then_inc(ve, 1)
                pool.wait_ge(ve, b + 1)
                pool.tensor_tensor(rstd[:, cols], rstd[:, cols], half[:], ALU.pow).then_inc(rstd_ok, 1)
                if b == 0:
                    for k in (W1, W2):
                        pool.wait_ge(peaked, k + 1)
                        over_rows(k, peak[:, k:k + 1])
            pool.wait_ge(peaked, U + 1)
            over_rows(U, peak_p[:])
            pool.wait_ge(peaked, HID + 1)
            over_rows(HID, peak[:, 2:3])

        @block.scalar
        def _(act):
            for k, w in ((W1, w1), (W2, w2)):
                act.wait_ge(scaled, k + 1)
                act.activation(w, w, ACT.Copy, scale=inv[:, k:k + 1], bias=ROUND).then_inc(w_shift, 1)
            for n in range(8):
                act.wait_ge(w_turned, n + 1)
                src = ps[:, n % 4, :].rearrange("p (c q) -> p c q", q=P)
                dst = w1T[:, n // 2, 4 * (n % 2):4 * (n % 2) + 4, :] if n < 4 else \
                    w2T[:, 2 * (n - 4):2 * (n - 4) + 2, :].rearrange("p c (k q) -> p (c k) q", q=P)
                act.activation(dst, src, ACT.Copy).then_inc(w_ready, 1)
            act.wait_ge(scaled, U + 1)
            for c in range(NCH):
                rows = u[:, c * CT:(c + 1) * CT, :]
                act.activation(rows, rows, ACT.Copy, scale=inv[:TT, U:U + 1], bias=ROUND).then_inc(u_shift, 1)
            for c in range(NCH):
                act.wait_ge(u_turned, c + 1)
                act.activation(uT[:, :, c * CN:(c + 1) * CN], ps[:, 4 + 2 * (c % 2):6 + 2 * (c % 2), 0:CN], ACT.Copy)\
                   .then_inc(u_ready, 1)
            act.wait_ge(biased, 1)
            with act.Fori(0, NCH) as c:
                for k in range(FC):
                    act.wait_ge(up_mm, c * FC + k + 1)
                    act.activation(hid[:, k, bass.ds(c * CN, CN)], ps[:, k, 0:CN], ACT.Gelu,
                                   scale=out_scale[:, 0:1], bias=b1s[:, k:k + 1]).then_inc(gelu, 1)
            act.wait_ge(scaled, HID + 1)
            with act.Fori(0, NCH) as c:
                rows = hid[:, :, bass.ds(c * CN, CN)]
                act.activation(rows, rows, ACT.Copy, scale=inv[:, HID:HID + 1], bias=ROUND).then_inc(q_shift, 1)

        @block.tensor
        def _(pe):
            pe.wait_ge(w_int, 1)
            for n in range(4):
                for k in range(4):
                    mm = pe.transpose(ps[:, n, k * P:(k + 1) * P],
                                      w1[:, 4 * (n % 2) + k, (n // 2) * P:(n // 2 + 1) * P], ident[:])
                mm.then_inc(w_turned, 1)
            pe.wait_ge(w_int, 2)
            for n in range(4):
                pe.wait_ge(w_ready, n + 1)
                for k in range(4):
                    f = 2 * n + k // 2
                    mm = pe.transpose(ps[:, n, k * P:(k + 1) * P], w2[:, k % 2, f:FH:FC], ident[:])
                mm.then_inc(w_turned, 1)
            for c in range(NCH):
                pe.wait_ge(u_int, c + 1)
                if c >= 2:
                    pe.wait_ge(u_ready, c - 1)
                for i in range(CT):
                    for kc in range(KC):
                        mm = pe.transpose(ps[:, 4 + 2 * (c % 2) + kc, i * TT:(i + 1) * TT],
                                          u[:, c * CT + i, kc * P:(kc + 1) * P], ident[:TT, :TT])
                mm.then_inc(u_turned, 1)
            pe.wait_ge(u_ready, NCH)
            pe.wait_ge(w_ready, 8)
            with pe.Fori(0, NCH) as c:
                for k in range(FC):
                    pe.wait_ge(gelu, c * FC)
                    for kc in range(KC):
                        mm = pe.matmul(ps[:, k, 0:CN], w1T[:, kc, k, :], uT[:, kc, bass.ds(c * CN, CN)],
                                       start=kc == 0, stop=kc == KC - 1)
                    mm.then_inc(up_mm, 1)
            with pe.Fori(0, NCH // 2) as c2:
                for par in range(2):
                    pe.wait_ge(q_ready, c2 * 2 + par + 1)
                    for i in range(CT):
                        pe.wait_ge(added, c2 * 8)
                        for k in range(FC):
                            mm = pe.matmul(ps[:TT, 4 * par + i, 0:D], qh[:, par, k, i * TT:(i + 1) * TT], w2T[:, k, :],
                                           start=k == 0, stop=k == FC - 1)
                        mm.then_inc(down_mm, 1)

        @block.vector
        def _(dve):
            chain = m.sem("e_chain")
            links = [0]

            def link(ins):
                links[0] += 1
                ins.then_inc(chain, 1)
                dve.wait_ge(chain, links[0])

            def scale_of(k):
                dve.wait_ge(topped, k + 1)
                col = slice(k, k + 1)
                link(dve.tensor_scalar(scale[:, col], top[:, col], MIN_RANGE, 1.0 / QP, ALU.max, ALU.mult))
                dve.reciprocal(inv[:, col], scale[:, col]).then_inc(scaled, 1)

            dve.wait_ge(loaded, 80)
            dve.tensor_reduce(peak[:, 0:1], flat_hid[:, 0:FC * D], AX_X, ALU.max, apply_absolute_value=True)\
               .then_inc(peaked, 1)
            dve.tensor_reduce(peak[:, 1:2], flat_hid[:, FC * D:2 * FC * D], AX_X, ALU.max, apply_absolute_value=True)\
               .then_inc(peaked, 1)
            for b in range(B):
                for i in range(b * NT, (b + 1) * NT):
                    dve.bn_stats(stats[:, i], h[:, i, :]).then_inc(stat, 1)
                for i in range(b * NT, (b + 1) * NT):
                    dve.wait_ge(stat, i + 1)
                    dve.bn_aggr(mv[:, i], stats[:, i]).then_inc(agg, 1)
            for b in range(B):
                dve.wait_ge(rstd_ok, b + 1)
                for i in range(b * NT, (b + 1) * NT):
                    dve.tensor_scalar(u[:, i], h[:, i, :], mv[:, i, 0:1], rstd[:, i:i + 1], ALU.subtract, ALU.mult)\
                       .then_inc(norm, 1)
                dve.wait_ge(norm, (b + 1) * NT)
                link(dve.tensor_reduce(peak_u[:, b * NT:(b + 1) * NT], u[:, b * NT:(b + 1) * NT, :], AX_X, ALU.max,
                                       apply_absolute_value=True))
            dve.wait_ge(zero_p, 1)
            dve.tensor_reduce(peak_p[:TT], peak_u[:], AX_X, ALU.max).then_inc(peaked, 1)
            scale_of(W1)
            scale_of(W2)
            for k, w in ((W1, flat_hid[:, 0:FC * D]), (W2, flat_hid[:, FC * D:2 * FC * D])):
                dve.wait_ge(w_shift, k + 1)
                dve.tensor_scalar(w, w, -ROUND, None, ALU.add).then_inc(w_int, 1)
            scale_of(U)
            for c in range(NCH):
                dve.wait_ge(u_shift, c + 1)
                rows = u[:, c * CT:(c + 1) * CT, :]
                dve.tensor_scalar(rows, rows, -ROUND, None, ALU.add).then_inc(u_int, 1)
            dve.wait_ge(scaled, 3)
            link(dve.tensor_tensor(out_scale[:, 0:1], scale[:, W1:W1 + 1], scale[:, U:U + 1], ALU.mult))
            dve.tensor_scalar(b1s[:], b1[:], out_scale[:, 0:1], None, ALU.mult).then_inc(biased, 1)
            with dve.Fori(0, NCH) as c:
                for k in range(FC):
                    dve.wait_ge(gelu, c * FC + k + 1)
                    dve.tensor_reduce(peak_h[:, bass.ds(c * FC + k, 1)], hid[:, k, bass.ds(c * CN, CN)], AX_X, ALU.max,
                                      apply_absolute_value=True).then_inc(hid_peak, 1)
            dve.wait_ge(hid_peak, NCH * FC)
            dve.tensor_reduce(peak[:, 2:3], peak_h[:], AX_X, ALU.max).then_inc(peaked, 1)
            scale_of(HID)
            dve.wait_ge(scaled, 4)
            link(dve.tensor_tensor(out_scale[:, 1:2], scale[:, W2:W2 + 1], scale[:, HID:HID + 1], ALU.mult))
            link(dve.tensor_scalar(b2s[:], b2[:], out_scale[:TT, 1:2], None, ALU.mult))
            link(dve.tensor_tensor(h[:], h[:], b2s[:].unsqueeze(1).to_broadcast([TT, NTILES, D]), ALU.add))
            with dve.Fori(0, NCH // 2) as c2:
                for par in range(2):
                    dve.wait_ge(q_shift, c2 * 2 + par + 1)
                    dve.wait_ge(down_mm, c2 * 8)
                    dve.tensor_scalar(qh[:, par], hid[:, :, bass.ds(c2 * (2 * CN) + par * CN, CN)], -ROUND, None, ALU.add)\
                       .then_inc(q_ready, 1)
                for par in range(2):
                    for i in range(CT):
                        tile = c2 * 8 + (par * CT + i)
                        dve.wait_ge(down_mm, c2 * 8 + (par * CT + i + 1))
                        dve.scalar_tensor_tensor(h[:, tile, :], ps[:TT, 4 * par + i, 0:D], out_scale[:TT, 1:2],
                                                 h[:, tile, :], ALU.mult, ALU.add).then_inc(added, 1)
            dve.wait_ge(added, NTILES)


def audio_tower(nc, io, out):
    with ExitStack() as stack:
        keep = Memory(nc, stack)
        h = keep.sb("h", [TT, NTILES, D], F32)
        ident = keep.sb("ident", [P, P], F32)
        identb = keep.sb("identb", [P, P], BF16)
        ready = keep.sem("const_ready")
        stored = keep.sem("stored")
        with nc.Block() as block:
            @block.gpsimd
            def _(pool):
                for k, t in enumerate((ident, identb)):
                    pool.memset(t[:], 0.0).then_inc(ready, 1)
                    pool.wait_ge(ready, 2 * k + 1)
                    pool.affine_select(out=t[:], in_=t[:], compare_op=ALU.not_equal, fill=1.0, base=0,
                                       pattern=[[-1, P]], channel_multiplier=1).then_inc(ready, 1)
                pool.wait_ge(ready, 4)
        route = keep.sb("route", [TT, NTILES, E_N], F32)
        scratch = {name: nc.dram_tensor(f"scratch_{name}", (2, P, KC, B * T), F32, kind="Internal").ap()
                   for name in ("uT", "hdT")}
        scratch["parts"] = nc.dram_tensor("scratch_parts", (2, 3, D, T), BF16, kind="Internal").ap()
        stage_tok_attn(nc, keep, io, h, ident, identb)
        stage_heads(nc, keep, io, h, ident, identb, False, route, scratch)
        stage_experts(nc, keep, io, h, route, scratch)
        stage_heads(nc, keep, io, h, ident, identb, True, None, scratch)
        stage_quantised(nc, keep, io, h, ident)
        with nc.Block() as block:
            @block.sync
            def _(sp):
                sp.dma_start(out.rearrange("b (i p) d -> p (b i) d", p=TT), h[:].rearrange("p (b i) d -> p (b i) d", b=B))\
                  .then_inc(stored, 16)
                sp.wait_ge(stored, 16)


def shape_constants():
    pos = np.arange(T, dtype=np.float32)
    theta = np.power(np.float32(10000.0), (np.float32(-2.0) * np.arange(D // 2, dtype=np.float32) / np.float32(D))
                     .astype(np.float32)).astype(np.float32)
    ang = (theta[:, None] * pos[None, :]).astype(np.float32)
    bf = mybir.dt.np(BF16)
    p, o = np.arange(TT)[:, None], np.arange(2 * TT)[None, :]
    freq = (np.float32(1.0) / np.power(np.float32(10000.0), np.arange(HD // 2, dtype=np.float32) / np.float32(HD // 2)))
    ang_h = (np.tile(freq.astype(np.float32), H)[:, None] * pos[None, :]).astype(np.float32)
    ow = np.arange(2 * TT + 2)[None, :]
    oc = np.arange(TT)[None, :]
    return {
        "cos_heads": np.cos(ang_h).astype(np.float32),
        "sin_heads": np.sin(ang_h).astype(np.float32),
        "mask_causal_q": np.where(oc <= p, 0.0, NEG).astype(bf),
        "mask_causal_k": np.where(oc >= p, 0.0, NEG).astype(bf),
        "mask_window_q": np.where((ow >= p) & (ow <= p + WINDOW - 1), 0.0, NEG).astype(bf),
        "mask_window_k": np.where((ow >= p) & (ow <= p + WINDOW - 1), 0.0, NEG).astype(bf),
        "expert_iota": np.tile(np.arange(E_N, dtype=np.float32), (TT, 1)),
        "cos_one": np.cos(ang).astype(np.float32),
        "sin_one": np.sin(ang).astype(np.float32),
        "mask_next": np.where(o <= p + 1, 0.0, NEG).astype(bf),
        "minus_half": np.full((TT, NT), -0.5, np.float32),
    }


_OUT = ("out_0_dram", (B, T, D), "float32")


def kernel(**inputs):
    import numpy as _np
    import concourse.bacc as _bacc
    from concourse import mybir as _mybir
    from concourse.bass_utils import run_bass_kernel_spmd as _run

    nc = _bacc.Bacc("TRN2", target_bir_lowering=False, num_devices=1)
    arrays, io = {}, {}
    for name, a in (dict(inputs) | shape_constants()).items():
        a = _np.ascontiguousarray(a)
        arrays[f"in_{name}_dram"] = a
        io[name] = nc.dram_tensor(f"in_{name}_dram", a.shape, _mybir.dt.from_np(a.dtype), kind="ExternalInput").ap()
    name, shape, dtype = _OUT
    out = nc.dram_tensor(name, shape, _mybir.dt.from_np(_np.dtype(dtype)), kind="ExternalOutput").ap()
    audio_tower(nc, io, out)
    r = _run(nc, [arrays], core_ids=[0])
    return r.results[0][name]
```

```python
from contextlib import ExitStack

import concourse.bass as bass
from concourse import mybir
import numpy as np

F32 = mybir.dt.float32
F32R = mybir.dt.float32r
BF16 = mybir.dt.bfloat16
U32 = mybir.dt.uint32
ACT = mybir.ActivationFunctionType
ALU = mybir.AluOpType
AX_X = mybir.AxisListType.X

P = 128
B, C_IN, T = 4, 128, 750
D, KC = 256, 2
TT, NT = 125, 6
NTILES = B * NT
BANK = 512
LN_EPS = 1e-5
FIRST = 1
SEGS = ((0, BANK), (BANK, T))
NEG = -1e30


class Count:

    def __init__(self, shared, name, per):
        self.shared, self.name, self.per, self.used = shared, name, per, False

    @property
    def sem(self):
        self.used = True
        return self.shared.get(self.name)

    def at(self, i, k=None):
        return i * self.per + (self.per if k is None else k) + self.shared.left.get(self.name, FIRST)


class SharedSemaphores:

    def __init__(self, nc, stack):
        self.nc, self.stack, self.held, self.left, self.started = nc, stack, {}, {}, set()

    def get(self, name):
        if name not in self.held:
            self.held[name] = self.stack.enter_context(self.nc.semaphore(name))
        return self.held[name]

    def start(self, pool, counts):
        for c in counts.values():
            if c.name not in self.started:
                self.started.add(c.name)
                pool.sem_inc(self.get(c.name), FIRST)

    def close(self, counts):
        for c in counts.values():
            if c.used:
                self.left[c.name] = self.left.get(c.name, FIRST) + B * c.per


class Memory:

    def __init__(self, nc, stack, keep=None):
        self.nc, self.stack, self.keep = nc, stack, keep.keep if keep else stack
        self.shared = keep.shared if keep else SharedSemaphores(nc, stack)

    def sb(self, name, shape, dt):
        return self.stack.enter_context(self.nc.sbuf_tensor(name, shape, dt))

    def ps(self, name, shape):
        return self.stack.enter_context(self.nc.psum_tensor(name, shape, F32))

    def sem(self, name):
        return self.keep.enter_context(self.nc.semaphore(name))

    def counts(self, **per):
        return {k: Count(self.shared, k, n) for k, n in per.items()}


def split3(eng, out, lhs, rhs, first=True, last=True):
    eng.matmul(out, lhs[0], rhs[0], start=first, stop=False)
    eng.matmul(out, lhs[0], rhs[1], start=False, stop=False)
    return eng.matmul(out, lhs[1], rhs[0], start=False, stop=last)


def stage_tok_attn(nc, keep, io, h, ident, identb):
    with ExitStack() as stack:
        m = Memory(nc, stack, keep)
        x_sb = m.sb("a_x", [P, B, T], F32)
        w_raw = m.sb("a_w_raw", [P, 3, KC, D], F32)
        wt_raw = m.sb("a_wt_raw", [P, KC, P], F32)
        tok_wT = m.sb("a_tok_wT", [P, D], F32)
        bias = m.sb("a_bias", [TT, 2, D], F32)
        w_hi = m.sb("a_w_hi", [P, 3, KC, D], F32R)
        w_lo = m.sb("a_w_lo", [P, 3, KC, D], F32R)
        cos = m.sb("a_cos", [P, T], F32)
        sin = m.sb("a_sin", [P, T], F32)
        mask = m.sb("a_mask", [TT, 2 * TT], BF16)
        decay = m.sb("a_decay", [P, T], F32)
        xs = m.sb("a_xs", [P, T], F32)
        fwd = m.sb("a_fwd", [P, T], F32)
        bwd = m.sb("a_bwd", [P, T], F32)
        ew = m.sb("a_ew", [P, T], F32)
        stats = m.sb("a_stats", [TT, NT, 6], F32)
        waiter = m.sb("a_waiter", [TT, 1], F32)
        mv = m.sb("a_mv", [TT, NT, 2], F32)
        rstd = m.sb("a_rstd", [TT, NT], F32)
        half = m.sb("a_half", [TT, NT], F32)
        u = m.sb("a_u", [TT, NT, D], F32)
        uT_hi = m.sb("a_uT_hi", [P, KC, T], F32R)
        uT_lo = m.sb("a_uT_lo", [P, KC, T], F32R)
        prod = m.sb("a_prod", [P, 4, T], F32)
        rot = m.sb("a_rot", [P, 2, KC, T], F32)
        qk_hi = m.sb("a_qk_hi", [P, 2, KC, T], F32R)
        qk_lo = m.sb("a_qk_lo", [P, 2, KC, T], F32R)
        v_hi = m.sb("a_v_hi", [TT, NT, D], F32R)
        v_lo = m.sb("a_v_lo", [TT, NT, D], F32R)
        neg_max = m.sb("a_neg_max", [TT, NT], F32)
        denom = m.sb("a_denom", [TT, NT], F32)
        rden = m.sb("a_rden", [TT, NT], F32)
        probs = m.sb("a_probs", [TT, 2, T], F32)
        pT_hi = m.sb("a_pT_hi", [TT, 2, NT, TT], F32R)
        pT_lo = m.sb("a_pT_lo", [TT, 2, NT, TT], F32R)
        ps = m.ps("a_ps", [P, 8, BANK])

        load = m.sem("a_load")
        set_wT = m.sem("a_set_wT")
        set_hi = m.sem("a_set_hi")
        set_lo = m.sem("a_set_lo")
        set_scale = m.sem("a_set_scale")
        set_const = m.sem("a_set_const")
        c = m.counts(xs=1, scan=2, ew=1, tok_mm=3, h=3, stats=6, mv=6, ve=1, rstd=1, u=6, uT_mm=2,
                     uT_hi=2, uT_lo=2, qk_mm=2, rope_mul=8, rope_sum=4, qk_hi=2, qk_lo=2, v_mm=3, v_hi=3,
                     v_lo=3, s_mm=6, neg_max=6, exp=6, pT_mm=6, pT_hi=6, pT_lo=6, rden=6, pv_mm=6, h_upd=6)

        def flat(bank):
            return ps[:, bank:bank + 2, :].rearrange("p b n -> p (b n)")

        def width(i):
            return min(T, (i + 2) * TT)

        block = stack.enter_context(nc.Block())
        loads = 16 * 11

        @block.sync
        def _(sp):
            sp.dma_start(wt_raw[:], io["L0_tok_W"].rearrange("(c p) d -> p c d", p=P)).then_inc(load, 16)
            sp.dma_start(x_sb[:], io["x"].rearrange("b c t -> c b t")).then_inc(load, 16)
            for n, name in enumerate(("L0_attn_Wq", "L0_attn_Wk")):
                sp.dma_start(w_raw[:, n], io[name].rearrange("(p c) d -> p c d", c=KC)).then_inc(load, 16)
            sp.dma_start(w_raw[:, 2], io["L0_attn_Wv"].rearrange("(c p) d -> p c d", p=P)).then_inc(load, 16)
            for k in range(2):
                sp.dma_start(bias[:, k], io["L0_tok_b"].rearrange("(a d) -> a d", a=1).to_broadcast([TT, D]))\
                  .then_inc(load, 16)
            sp.dma_start(cos[:], io["cos_one"]).then_inc(load, 16)
            sp.dma_start(sin[:], io["sin_one"]).then_inc(load, 16)
            sp.dma_start(mask[:], io["mask_next"]).then_inc(load, 16)
            sp.dma_start(half[:], io["minus_half"]).then_inc(load, 16)

        @block.tensor
        def _(pe):
            pe.wait_ge(load, loads)
            for ec in range(KC):
                mm = pe.transpose(ps[:, 0, ec * P:(ec + 1) * P], wt_raw[:, ec, :], ident[:])
            mm.then_inc(set_wT, 1)
            pe.wait_ge(set_scale, 1)
            for n in range(3):
                for kc in range(KC):
                    for ec in range(KC):
                        mm = pe.transpose(ps[:, 1 + n, (kc * KC + ec) * P:(kc * KC + ec + 1) * P],
                                          w_raw[:, n, ec, kc * P:(kc + 1) * P], ident[:])
                mm.then_inc(set_wT, 1)
            pe.wait_ge(set_lo, 3)
            with pe.Fori(0, B) as b:
                pe.wait_ge(c["ew"].sem, c["ew"].at(b))
                for g in range(3):
                    for i in (2 * g, 2 * g + 1):
                        mm = pe.matmul(ps[:TT, g, (i % 2) * D:(i % 2 + 1) * D], ew[:, i * TT:(i + 1) * TT],
                                       tok_wT[:], start=True, stop=True)
                    mm.then_inc(c["tok_mm"].sem, 1)
                for i in range(NT):
                    pe.wait_ge(c["u"].sem, c["u"].at(b, i + 1))
                    if i == 0:
                        pe.wait_ge(c["h_upd"].sem, c["h_upd"].at(b, 0))
                    for kc in range(KC):
                        mm = pe.transpose(ps[:, 4 + kc + 2 * (i // 4), (i % 4) * TT:(i % 4 + 1) * TT],
                                          u[:, i, kc * P:(kc + 1) * P], ident[:TT, :TT])
                    if i in (3, 5):
                        mm.then_inc(c["uT_mm"].sem, 1)
                pe.wait_ge(c["uT_lo"].sem, c["uT_lo"].at(b))
                pe.wait_ge(c["h"].sem, c["h"].at(b))
                for n in range(2):
                    for ec in range(KC):
                        for s0, s1 in SEGS:
                            for kc in range(KC):
                                mm = split3(pe, flat(4 * n + 2 * ec)[:, s0:s1],
                                            [w[:, n, kc, ec * P:(ec + 1) * P] for w in (w_hi, w_lo)],
                                            [t[:, kc, s0:s1] for t in (uT_hi, uT_lo)], kc == 0, kc == KC - 1)
                    mm.then_inc(c["qk_mm"].sem, 1)
                pe.wait_ge(c["rope_mul"].sem, c["rope_mul"].at(b, 4))
                for g in range(3):
                    for i in (2 * g, 2 * g + 1):
                        for kc in range(KC):
                            mm = split3(pe, ps[:TT, g, (i % 2) * D:(i % 2 + 1) * D],
                                        [t[:, kc, i * TT:(i + 1) * TT] for t in (uT_hi, uT_lo)],
                                        [w[:, 2, kc, :] for w in (w_hi, w_lo)], kc == 0, kc == KC - 1)
                    mm.then_inc(c["v_mm"].sem, 1)

                def scores(i):
                    pe.wait_ge(c["qk_lo"].sem, c["qk_lo"].at(b))
                    if i < 2:
                        pe.wait_ge(c["v_lo"].sem, c["v_lo"].at(b))
                    else:
                        pe.wait_ge(c["exp"].sem, c["exp"].at(b, i - 1))
                    out = flat(2 * (i % 2))
                    for s0 in range(0, width(i), BANK):
                        s1 = min(s0 + BANK, width(i))
                        s2 = s1 + (s1 - s0) % 2
                        for kc in range(KC):
                            mm = split3(pe, out[:TT, s0:s2], [t[:, 0, kc, i * TT:(i + 1) * TT] for t in (qk_hi, qk_lo)],
                                        [t[:, 1, kc, s0:s2] for t in (qk_hi, qk_lo)], kc == 0, kc == KC - 1)
                            m0 = max(s0, i * TT)
                            if kc == 0 and m0 < s1:
                                pe.matmul(out[:TT, m0:s1], identb[:TT, :TT], mask[:, m0 - i * TT:s1 - i * TT],
                                          start=False, stop=False)
                    mm.then_inc(c["s_mm"].sem, 1)

                def turn_probs(i):
                    pe.wait_ge(c["exp"].sem, c["exp"].at(b, i + 1))
                    if i == 0:
                        pe.wait_ge(c["rope_mul"].sem, c["rope_mul"].at(b))
                    else:
                        pe.wait_ge(c["pT_lo"].sem, c["pT_lo"].at(b, i))
                    for j in range(width(i) // TT):
                        mm = pe.transpose(ps[:TT, 4 + j // 4, (j % 4) * P:(j % 4) * P + TT],
                                          probs[:, i % 2, j * TT:(j + 1) * TT], ident[:TT, :TT])
                    mm.then_inc(c["pT_mm"].sem, 1)

                def weigh(i):
                    pe.wait_ge(c["pT_lo"].sem, c["pT_lo"].at(b, i + 1))
                    if i >= 2:
                        pe.wait_ge(c["h_upd"].sem, c["h_upd"].at(b, i - 1))
                    n = width(i) // TT
                    for j in range(n):
                        mm = split3(pe, ps[:TT, 6 + i % 2, 0:D], [t[:, i % 2, j, :] for t in (pT_hi, pT_lo)],
                                    [t[:, j, :] for t in (v_hi, v_lo)], j == 0, j == n - 1)
                    mm.then_inc(c["pv_mm"].sem, 1)

                scores(0)
                for i in range(NT):
                    if i + 1 < NT:
                        scores(i + 1)
                    turn_probs(i)
                    if i >= 1:
                        weigh(i - 1)
                weigh(NT - 1)

        @block.scalar
        def _(act):
            for n in range(3):
                act.wait_ge(set_wT, n + 2)
                act.activation(w_hi[:, n].rearrange("p k e -> p (k e)"), ps[:, 1 + n, :], ACT.Copy)\
                   .then_inc(set_hi, 1)
            with act.Fori(0, B) as b:
                for g, (i0, i1) in enumerate(((0, 4), (4, 6))):
                    act.wait_ge(c["uT_mm"].sem, c["uT_mm"].at(b, g + 1))
                    if g == 0:
                        act.wait_ge(c["v_mm"].sem, c["v_mm"].at(b, 0))
                    act.activation(uT_hi[:, :, i0 * TT:i1 * TT],
                                   ps[:, 4 + 2 * g:6 + 2 * g, 0:(i1 - i0) * TT], ACT.Copy).then_inc(c["uT_hi"].sem, 1)
                for n in range(2):
                    act.wait_ge(c["rope_sum"].sem, c["rope_sum"].at(b, 2 * n + 2))
                    if n == 0:
                        act.wait_ge(c["s_mm"].sem, c["s_mm"].at(b, 0))
                    act.activation(qk_hi[:, n], rot[:, n], ACT.Copy).then_inc(c["qk_hi"].sem, 1)
                for g in range(3):
                    act.wait_ge(c["v_mm"].sem, c["v_mm"].at(b, g + 1))
                    if g == 0:
                        act.wait_ge(c["pv_mm"].sem, c["pv_mm"].at(b, 0))
                    act.activation(v_hi[:, 2 * g:2 * g + 2, :].rearrange("p i d -> p (i d)"), ps[:TT, g, :], ACT.Copy)\
                       .then_inc(c["v_hi"].sem, 1)

                def exps(i):
                    act.wait_ge(c["neg_max"].sem, c["neg_max"].at(b, i + 1))
                    if i < 2:
                        act.wait_ge(c["pT_mm"].sem, c["pT_mm"].at(b, 0))
                    else:
                        act.wait_ge(c["pT_mm"].sem, c["pT_mm"].at(b, i - 1))
                    act.activation(probs[:, i % 2, 0:width(i)], flat(2 * (i % 2))[:TT, 0:width(i)], ACT.Exp,
                                   bias=neg_max[:, i:i + 1], accum_out=denom[:, i:i + 1]).then_inc(c["exp"].sem, 1)

                def turned_hi(i):
                    act.wait_ge(c["pT_mm"].sem, c["pT_mm"].at(b, i + 1))
                    if i < 2:
                        act.wait_ge(c["pv_mm"].sem, c["pv_mm"].at(b, 0))
                    else:
                        act.wait_ge(c["pv_mm"].sem, c["pv_mm"].at(b, i - 1))
                    n = width(i) // TT
                    act.activation(pT_hi[:, i % 2, 0:n, :],
                                   flat(4).rearrange("p (j q) -> p j q", q=P)[:TT, 0:n, 0:TT], ACT.Copy)\
                       .then_inc(c["pT_hi"].sem, 1)

                exps(0)
                for i in range(NT):
                    if i + 1 < NT:
                        exps(i + 1)
                    turned_hi(i)

        @block.gpsimd
        def _(pool):
            keep.shared.start(pool, c)
            pool.memset(decay[:], 0.9).then_inc(set_const, 1)
            pool.wait_ge(load, loads)
            pool.tensor_scalar(w_raw[:, 0], w_raw[:, 0], float(D) ** -0.5, None, ALU.mult).then_inc(set_scale, 1)
            with pool.Fori(0, B) as b:
                pool.wait_ge(c["ve"].sem, c["ve"].at(b))
                pool.tensor_tensor(rstd[:], rstd[:], half[:], ALU.pow).then_inc(c["rstd"].sem, 1)
                for n in range(2):
                    pool.wait_ge(c["rope_mul"].sem, c["rope_mul"].at(b, 4 * n + 4))
                    if n == 0:
                        pool.wait_ge(c["qk_lo"].sem, c["qk_lo"].at(b, 0))
                    pool.tensor_tensor(rot[:, n, 0], prod[:, 0], prod[:, 1], ALU.subtract)\
                        .then_inc(c["rope_sum"].sem, 1)
                    pool.tensor_tensor(rot[:, n, 1], prod[:, 2], prod[:, 3], ALU.add)\
                        .then_inc(c["rope_sum"].sem, 1)

        @block.vector
        def _(dve):
            dve.wait_ge(set_wT, 1)
            dve.tensor_scalar(tok_wT[:], ps[:, 0, 0:D], 0.5, None, ALU.mult)
            for n in range(3):
                dve.wait_ge(set_hi, n + 1)
                dve.tensor_tensor(w_lo[:, n].rearrange("p k e -> p (k e)"), ps[:, 1 + n, :],
                                  w_hi[:, n].bitcast(F32).rearrange("p k e -> p (k e)"), ALU.subtract)\
                   .then_inc(set_lo, 1)
            dve.wait_ge(set_const, 1)
            with dve.Fori(0, B) as b:
                dve.tensor_scalar(xs[:], x_sb[:, b, :], 0.1, None, ALU.mult).then_inc(c["xs"].sem, 1)
                dve.wait_ge(c["xs"].sem, c["xs"].at(b))
                dve.tensor_tensor_scan(fwd[:], decay[:], xs[:], x_sb[:, b, 0:1], ALU.mult, ALU.add)\
                   .then_inc(c["scan"].sem, 1)
                dve.tensor_tensor_scan(bwd[:, ::-1], decay[:], xs[:, ::-1], x_sb[:, b, T - 1:T], ALU.mult, ALU.add)\
                   .then_inc(c["scan"].sem, 1)
                dve.wait_ge(c["scan"].sem, c["scan"].at(b))
                dve.wait_ge(c["tok_mm"].sem, c["tok_mm"].at(b, 0))
                dve.tensor_tensor(ew[:], fwd[:], bwd[:], ALU.add).then_inc(c["ew"].sem, 1)
                for g in range(3):
                    dve.wait_ge(c["tok_mm"].sem, c["tok_mm"].at(b, g + 1))
                    dve.tensor_tensor(h[:, bass.ds(b * NT + 2 * g, 2), :],
                                      ps[:TT, g, :].rearrange("p (i d) -> p i d", d=D), bias[:], ALU.add)\
                       .then_inc(c["h"].sem, 1)
                    dve.wait_ge(c["h"].sem, c["h"].at(b, g + 1))
                    dve.memset(waiter[:], 0.0)
                    for i in (2 * g, 2 * g + 1):
                        dve.bn_stats(stats[:, i], h[:, b * NT + i, :]).then_inc(c["stats"].sem, 1)
                dve.wait_ge(c["stats"].sem, c["stats"].at(b))
                dve.memset(waiter[:], 0.0)
                for i in range(NT):
                    dve.bn_aggr(mv[:, i], stats[:, i]).then_inc(c["mv"].sem, 1)
                dve.wait_ge(c["mv"].sem, c["mv"].at(b))
                dve.tensor_scalar(rstd[:], mv[:, :, 1], LN_EPS, None, ALU.add).then_inc(c["ve"].sem, 1)
                dve.wait_ge(c["rstd"].sem, c["rstd"].at(b))
                for i in range(NT):
                    if i == 0:
                        dve.wait_ge(c["uT_mm"].sem, c["uT_mm"].at(b, 0))
                    dve.tensor_scalar(u[:, i], h[:, b * NT + i, :], mv[:, i, 0:1], rstd[:, i:i + 1],
                                      ALU.subtract, ALU.mult).then_inc(c["u"].sem, 1)
                for g, (i0, i1) in enumerate(((0, 4), (4, 6))):
                    dve.wait_ge(c["uT_hi"].sem, c["uT_hi"].at(b, g + 1))
                    dve.tensor_tensor(uT_lo[:, :, i0 * TT:i1 * TT], ps[:, 4 + 2 * g:6 + 2 * g, 0:(i1 - i0) * TT],
                                      uT_hi[:, :, i0 * TT:i1 * TT].bitcast(F32), ALU.subtract)\
                       .then_inc(c["uT_lo"].sem, 1)
                for n in range(2):
                    dve.wait_ge(c["qk_mm"].sem, c["qk_mm"].at(b, n + 1))
                    if n == 0:
                        dve.wait_ge(c["rope_sum"].sem, c["rope_sum"].at(b, 0))
                    else:
                        dve.wait_ge(c["rope_sum"].sem, c["rope_sum"].at(b, 2))
                    even, odd = flat(4 * n)[:, 0:T], flat(4 * n + 2)[:, 0:T]
                    for k, (part, table) in enumerate(((even, cos), (odd, sin), (even, sin), (odd, cos))):
                        dve.tensor_tensor(prod[:, k], part, table[:], ALU.mult).then_inc(c["rope_mul"].sem, 1)
                for n in range(2):
                    dve.wait_ge(c["qk_hi"].sem, c["qk_hi"].at(b, n + 1))
                    dve.tensor_tensor(qk_lo[:, n], rot[:, n], qk_hi[:, n].bitcast(F32), ALU.subtract)\
                       .then_inc(c["qk_lo"].sem, 1)
                for g in range(3):
                    dve.wait_ge(c["v_hi"].sem, c["v_hi"].at(b, g + 1))
                    dve.tensor_tensor(v_lo[:, 2 * g:2 * g + 2, :].rearrange("p i d -> p (i d)"), ps[:TT, g, :],
                                      v_hi[:, 2 * g:2 * g + 2, :].bitcast(F32).rearrange("p i d -> p (i d)"),
                                      ALU.subtract).then_inc(c["v_lo"].sem, 1)

                def row_max(i):
                    dve.wait_ge(c["s_mm"].sem, c["s_mm"].at(b, i + 1))
                    dve.tensor_reduce(neg_max[:, i:i + 1], flat(2 * (i % 2))[:TT, 0:width(i)], AX_X, ALU.max,
                                      negate=True).then_inc(c["neg_max"].sem, 1)

                def turned_lo(i):
                    dve.wait_ge(c["pT_hi"].sem, c["pT_hi"].at(b, i + 1))
                    n = width(i) // TT
                    dve.tensor_tensor(pT_lo[:, i % 2, 0:n, :],
                                      flat(4).rearrange("p (j q) -> p j q", q=P)[:TT, 0:n, 0:TT],
                                      pT_hi[:, i % 2, 0:n, :].bitcast(F32), ALU.subtract)\
                       .then_inc(c["pT_lo"].sem, 1)
                    dve.wait_ge(c["exp"].sem, c["exp"].at(b, i + 1))
                    dve.reciprocal(rden[:, i:i + 1], denom[:, i:i + 1]).then_inc(c["rden"].sem, 1)

                def add_out(i):
                    dve.wait_ge(c["pv_mm"].sem, c["pv_mm"].at(b, i + 1))
                    dve.wait_ge(c["rden"].sem, c["rden"].at(b, i + 1))
                    dve.scalar_tensor_tensor(h[:, b * NT + i, :], ps[:TT, 6 + i % 2, 0:D], rden[:, i:i + 1],
                                             h[:, b * NT + i, :], ALU.mult, ALU.add).then_inc(c["h_upd"].sem, 1)

                row_max(0)
                for i in range(NT):
                    if i + 1 < NT:
                        row_max(i + 1)
                    turned_lo(i)
                    if i >= 1:
                        add_out(i - 1)
                add_out(NT - 1)
                dve.wait_ge(c["h_upd"].sem, c["h_upd"].at(b))
        keep.shared.close(c)


H, HD = 16, 16
HG = 4
GROUPS = H // HG
SLOTS = ((0, 0), (0, 1), (1, 0), (1, 1), (0, 2), (2, 0))
STACK = len(SLOTS) * HD
ROWS = STACK + 3
E_N = 8
WINDOW = 128


def stage_heads(nc, keep, io, h, ident, identb, local, route=None, scratch=None):
    L = "d" if local else "b"
    with ExitStack() as stack:
        m = Memory(nc, stack, keep)
        w_hi = m.sb(f"{L}_w_hi", [P, 3, KC, D], F32R)
        w_lo = m.sb(f"{L}_w_lo", [P, 3, KC, D], F32R)
        wo = m.sb(f"{L}_wo", [P, KC, D], F32)
        mask_w = 2 * TT + 2 if local else TT
        mask_q = m.sb(f"{L}_mask_q", [TT, mask_w], BF16)
        mask_k = m.sb(f"{L}_mask_k", [TT, mask_w], BF16)
        half = m.sb(f"{L}_half", [TT, NT], F32)
        stats = m.sb(f"{L}_stats", [TT, NT, 6], F32)
        waiter = m.sb(f"{L}_waiter", [TT, 1], F32)
        one = m.sb(f"{L}_one", [P, 1], F32)
        mv = m.sb(f"{L}_mv", [TT, NT, 2], F32)
        rstd = m.sb(f"{L}_rstd", [TT, NT], F32)
        u = m.sb(f"{L}_u", [TT, NT, D], F32)
        uT_hi = m.sb(f"{L}_uT_hi", [P, KC, T], F32R)
        uT_lo = m.sb(f"{L}_uT_lo", [P, KC, T], F32R)
        part = [m.sb(f"{L}_part{k}", [P, 2, KC, T], BF16) for k in range(3)]
        rest = m.sb(f"{L}_rest", [P, KC, T], F32)
        q_st = m.sb(f"{L}_q_st", [ROWS, H, T], BF16)
        k_st = m.sb(f"{L}_k_st", [ROWS, H, T], BF16)
        v_ext = m.sb(f"{L}_v_ext", [TT, NT, H, 2 * HD], F32)
        neg = m.sb(f"{L}_neg", [TT, NT, H], F32)
        neg_b = m.sb(f"{L}_neg_b", [TT, 2, H], F32)
        neg_part = m.sb(f"{L}_neg_part", [TT, NT, 3, HG], BF16)
        neg_rest = m.sb(f"{L}_neg_rest", [TT, NT, HG], F32)
        negT = m.sb(f"{L}_negT", [3 * HG, T], BF16)
        pw = 2 * TT + 2 if local else T
        probs = m.sb(f"{L}_probs", [TT, 2, HG, pw], F32)
        pv_sb = m.sb(f"{L}_pv_sb", [P, GROUPS, T], F32)
        rden = m.sb(f"{L}_rden", [TT, NT, H], F32)
        o_full = m.sb(f"{L}_o", [P, NT, D], F32)
        o = o_full[:TT]
        oT = m.sb(f"{L}_oT", [P, 2, KC, TT], F32)
        ps = m.ps(f"{L}_ps", [P, 8, BANK])
        if local:
            prod = m.sb(f"{L}_prod", [P, 4, T], F32)
            rot = m.sb(f"{L}_rot", [P, KC, T], F32)
            cos = m.sb(f"{L}_cos", [P, T], F32)
            sin = m.sb(f"{L}_sin", [P, T], F32)
        else:
            r_raw = m.sb("b_r_raw", [P, KC, E_N], F32)
            r_hi = m.sb("b_r_hi", [P, KC, E_N], F32R)
            r_lo = m.sb("b_r_lo", [P, KC, E_N], F32R)
            norm_w = m.sb("b_norm_w", [TT, D], F32)
            junk = m.sb("b_junk", [TT, D], F32)
            ss = m.sb("b_ss", [TT, NT], F32)
            rms = m.sb("b_rms", [TT, NT], F32)
            hd = o
            u_kept = m.sb("b_u_kept", [TT, NT, D], F32)
            hdT_hi = m.sb("b_hdT_hi", [P, 2, KC, TT], F32R)
            hdT_lo = m.sb("b_hdT_lo", [P, 2, KC, TT], F32R)
            r_max = m.sb("b_r_max", [TT, NT], F32)
            r_sum = m.sb("b_r_sum", [TT, NT], F32)
            r_inv = m.sb("b_r_inv", [TT, NT], F32)
            r_sub = m.sb("b_r_sub", [TT, NT, E_N], F32)
            r_exp = m.sb("b_r_exp", [TT, NT, E_N], F32)
            r_prob = m.sb("b_r_prob", [TT, NT, E_N], F32)
            top_v = m.sb("b_top_v", [TT, NT, E_N], F32)
            top_i = m.sb("b_top_i", [TT, NT, E_N], U32)
            top_f = m.sb("b_top_f", [TT, NT, E_N], F32)
            pick = m.sb("b_pick", [TT, 2, NT, E_N], F32)
            iota = m.sb("b_iota", [TT, E_N], F32)

        def flat(bank, n=2):
            return ps[:, bank:bank + n, :].rearrange("p b n -> p (b n)")

        firsts = []
        for i in range(NT):
            if local:
                k0 = max(0, i * TT - WINDOW + 1)
                segs = [(0, k0, (i + 1) * TT - k0, WINDOW - 1 - i * TT + k0)]
            elif i < 4:
                segs = [(0, 0, (i + 1) * TT, None)]
            else:
                segs = [(0, 0, 4 * TT, None), (1, 4 * TT, (i - 3) * TT, None)]
            for seg, k0, n, mc in segs:
                per = max(1, min(HG, BANK // n))
                for h0 in range(0, HG, per):
                    firsts.append((i, seg, h0, per, k0, n, mc))
        seconds = []
        for j in range(NT):
            n = min(pw, T - j * TT)
            per = max(1, min(HG, BANK // n))
            banks = 1 if per == HG else 2
            step = 1 if n > BANK else per * banks
            for h0 in range(0, HG, step):
                seconds.append((j, h0, step, per if n <= BANK else 1, n))
        N_SEC = len(seconds)

        load = m.sem(f"{L}_load")
        set_w = m.sem(f"{L}_set_w")
        set_hi = m.sem(f"{L}_set_hi")
        set_const = m.sem(f"{L}_set_const")
        UT = ((0, 2), (2, 4), (4, 6)) if local else ((0, 2), (2, 4), (4, 5), (5, 6))
        HALF = T // 2 + T // 2 % 2
        HALVES = ((0, HALF), (HALF, T))
        AHEAD, FIRSTS_BY, TURN_AT, MAX_IN_AT = (0.45, 0.80, 1.00, 1.15) if local else (0.25, 0.60, 0.75, 0.90)
        FRONT_AT, KEEP_AT, ROWS_OUT_BY, NORMED_BY = (0.0, 0.0, 1.4, 0.0) if local else (1.38, 1.36, 0.95, 1.35)
        UNITS = {"uT", "qk", "router", "v", "first", "turn", "back", "oT", "wo", "hdT"}
        def over(t0, t1, steps):
            return [(t0 + (t1 - t0) * (i + 0.5) / len(steps), s) for i, s in enumerate(steps)]

        def weigh_group(g):
            steps, at_col = [], 0
            for j in range(NT):
                for k, (jj, h0, nh, per, n) in enumerate(seconds):
                    if jj == j:
                        steps.append((at_col, ("second", (g, k))))
                        at_col += nh * (n + TT)
                if j >= 1:
                    steps.append((at_col, ("weigh", (g, j - 1))))
                    at_col += HG * min(pw, T - (j - 1) * TT)
            steps.append((at_col, ("weigh", (g, NT - 1))))
            at_col += HG * TT
            return [(g + 0.999 * a / at_col, s) for a, s in steps] + [(g + 0.9995, ("weighed", (g,)))]

        rows_out = []
        for i in range(NT + 2):
            rows_out += [(name, (i - lag,)) for name, lag in (("back", 0), ("oT", 1), ("wo", 2)) if 0 <= i - lag < NT]
        steps_of_batch = []
        if not local:
            steps_of_batch += [(GROUPS + ROWS_OUT_BY, ("rms", ()))]
            steps_of_batch += over(GROUPS + ROWS_OUT_BY, GROUPS + NORMED_BY,
                                   [(name, (i,)) for name in ("hd", "hdT") for i in range(NT)])
            steps_of_batch += [(KEEP_AT - GROUPS + 0.001, ("keep", ()))]
        steps_of_batch += over(GROUPS, GROUPS + ROWS_OUT_BY, rows_out)
        steps_of_batch += [(FRONT_AT - GROUPS, ("norm", ()))]
        steps_of_batch += over(FRONT_AT + 0.14 - GROUPS, FRONT_AT + 0.30 - GROUPS, [("uT", (k,)) for k in range(len(UT))])
        for n in range(2):
            t0 = FRONT_AT + 0.36 - GROUPS + 0.35 * n
            steps_of_batch += over(t0, t0 + 0.30, [("qk", (n, ec, s)) for s in range(2) for ec in range(KC)])
            steps_of_batch += [(t0 + 0.33, ("cut", (n,)))]
        if not local:
            steps_of_batch += over(FRONT_AT + 1.1 - GROUPS, FRONT_AT + 1.2 - GROUPS, [("router", ()), ("route", ())])
        steps_of_batch += [(-4e-4 + 1e-4 * k, ("v", (k,))) for k in range(3)]
        for g in range(GROUPS):
            steps_of_batch += weigh_group(g)
            t0 = g - 1 - AHEAD
            steps_of_batch += over(t0, t0 + FIRSTS_BY, [("first", (g, k)) for k in range(len(firsts))])
            steps_of_batch += [(t0 + FIRSTS_BY, ("maxima", (g,)))]
            steps_of_batch += over(t0 + TURN_AT, t0 + TURN_AT + 0.04, [("turn", (g, k)) for k in range(2)])
            steps_of_batch += [(t0 + MAX_IN_AT, ("max_in", (g,)))]

        def plan_of(t0, batches):
            found = [(at + GROUPS * w, (name, w, args)) for at, (name, args) in steps_of_batch for w in batches
                     if t0 <= at + GROUPS * w < t0 + GROUPS]
            return numbered([s for _, s in sorted(found, key=lambda x: x[0])])

        def numbered(steps):
            out, p = [], 0
            for kind, which, args in steps:
                out.append((kind, which, args, p))
                p += kind in UNITS
            return out

        def units_of(steps):
            return sum(kind in UNITS for kind, _, _, _ in steps)

        before = plan_of(0, (1,))
        plans = {"first": plan_of(0, (0, 1)), "middle": plan_of(0, (-1, 0, 1)), "last": plan_of(0, (-1, 0))}
        after = plan_of(0, (-1,))
        PER = units_of(plans["middle"])
        AT_0, AT_1 = units_of(before), units_of(before) + units_of(plans["first"]) - PER
        assert PER % 2 == 0 and AT_1 + (B - 1) * PER + units_of(plans["last"]) + units_of(after) == B * PER

        def unit_no(t, p):
            if isinstance(t, int):
                return 0, {-1: 0, 0: AT_0, B - 1: AT_1 + (B - 1) * PER, B: B * PER - units_of(after)}[t] + p
            return t, AT_1 + p

        def run(eng, step):
            for t, plan in ((-1, before), (0, plans["first"])):
                for s in plan:
                    step(t, *s)
            with eng.Fori(1, B - 1) as t:
                for s in plans["middle"]:
                    step(t, *s)
            for t, plan in ((B - 1, plans["last"]), (B, after)):
                for s in plan:
                    step(t, *s)

        SPLITS = 1 if local else KC * 2
        LOADS = len(SLOTS) * (4 if local else 2)
        c = m.counts(stats=NT, mv=NT, ve=1, rstd=1, u=NT, uT_hi=len(UT), uT_lo=len(UT), rope_mul=16, rope_sum=4,
                     part0=2 * SPLITS, rest=2 * SPLITS, part1=2, part2=2, parts_out=96,
                     stacked0=16 * LOADS, stacked1=16 * LOADS, stacked2=16 * LOADS, stacked3=16 * LOADS, v=3,
                     unit_mm=PER, free0=PER // 2, free1=PER // 2, neg=GROUPS, neg_part=4 * GROUPS, negT=2 * GROUPS,
                     neg_in=48 * GROUPS, sec_mm=GROUPS * N_SEC, exp=GROUPS * N_SEC, pv_mm=GROUPS * NT, pv_sb=GROUPS,
                     rden=NT, o=NT, oT=NT, h=NT, r_max=1, r_sub=1, r_exp=1, r_sum=1, r_inv=1, r_prob=1, top_v=NT,
                     top_i=NT, top_f=1, pick=2 * NT, route=1, hd_raw=NT, ss=NT, rms_ve=1, rms=1, hd_t=NT,
                     hd=NT, hdT_hi=NT, hdT_lo=NT, uT_out=32, hdT_out0=16 * NT, hdT_out1=16 * NT)

        def at(name, t, which, k=None):
            n = c[name]
            return n.at(t, which * n.per + (n.per if k is None else k))

        def unit_done(t, p):
            trips, units = unit_no(t, p)
            return c["unit_mm"].at(trips, units + 1)

        def bank_of(t, p):
            return 6 + unit_no(t, p)[1] % 2

        def free_sem(t, p):
            return c[f"free{bank_of(t, p) - 6}"].sem

        def tile_no(t, which, i):
            return t * NT + (which * NT + i)

        def second_out(x, unit):
            j, h0, nh, per, n = unit
            b0 = 2 * (x % 2)
            if n > BANK:
                return flat(b0)[:TT, 0:n]
            nb = nh // per
            return ps[:TT, b0:b0 + nb, 0:per * n].rearrange("p b (m n) -> p b m n", n=n)

        with ExitStack() as inner:
            raw = pv_sb[:].rearrange("p g t -> p (g t)")[:, 0:3 * KC * D].rearrange("p (n k e) -> p n k e", n=3, k=KC)
            rawp = o_full[:].rearrange("p (n k) e -> p n k e", k=KC)
            names = ("L0_ffn_wq", "L0_ffn_wk", "L0_ffn_wv")
            block = inner.enter_context(nc.Block())
            n_loads = 16 * (9 if local else 10)

            @block.sync
            def _(sp):
                for n in range(3):
                    src = io["L1_attn_Wqkv"][:, n * D:(n + 1) * D] if local else io[names[n]]
                    sp.dma_start(raw[:, n], src.rearrange("(k p) e -> p k e", p=P)).then_inc(load, 16)
                src = io["L1_attn_Wout" if local else "L0_ffn_wo"]
                sp.dma_start(wo[:], src.rearrange("(k p) e -> p k e", p=P)).then_inc(load, 16)
                sp.dma_start(mask_q[:], io["mask_window_q" if local else "mask_causal_q"]).then_inc(load, 16)
                sp.dma_start(mask_k[:], io["mask_window_k" if local else "mask_causal_k"]).then_inc(load, 16)
                sp.dma_start(half[:], io["minus_half"]).then_inc(load, 16)
                if local:
                    sp.dma_start(cos[:], io["cos_heads"]).then_inc(load, 16)
                    sp.dma_start(sin[:], io["sin_heads"]).then_inc(load, 16)
                else:
                    sp.dma_start(r_raw[:], io["L0_ffn_router_w"].rearrange("(k p) e -> p k e", p=P)).then_inc(load, 16)
                    sp.dma_start(norm_w[:], io["L0_ffn_attn_norm_w"].rearrange("(a d) -> a d", a=1)
                                 .to_broadcast([TT, D])).then_inc(load, 16)
                    sp.dma_start(iota[:], io["expert_iota"]).then_inc(load, 16)
                sp.wait_ge(load, n_loads)

            @block.gpsimd
            def _(pool):
                pool.wait_ge(load, n_loads)
                for n in range(3):
                    for k in range(KC):
                        src, dst = raw[:, n, k], rawp[:, n, k]
                        if local and n < 2:
                            src = src.rearrange("p (h a f) -> p a h f", a=2, f=HD // 2)
                            dst = dst.rearrange("p (a h f) -> p a h f", a=2, f=HD // 2)
                        mm = pool.tensor_scalar(dst, src, float(HD) ** -0.5 if n == 0 else 1.0, None, ALU.mult)
                    mm.then_inc(set_w, 1)
                pool.memset(one[:], 1.0)
                pool.memset(v_ext[:], 0.0).then_inc(set_const, 1)
                pool.wait_ge(set_const, 1)
                pool.memset(k_st[96:ROWS], 1.0).then_inc(set_const, 1)
                pool.wait_ge(set_const, 2)
                pool.memset(v_ext[:, :, :, HD:HD + 1], 1.0).then_inc(set_const, 1)

            @block.scalar
            def _(act):
                for n in range(3):
                    act.wait_ge(set_w, n + 1)
                    act.activation(w_hi[:, n], rawp[:, n], ACT.Copy).then_inc(set_hi, 1)
                if not local:
                    act.wait_ge(load, n_loads)
                    act.activation(r_hi[:], r_raw[:], ACT.Copy).then_inc(set_hi, 1)

            @block.vector
            def _(dve):
                for n in range(3):
                    dve.wait_ge(set_hi, n + 1)
                    dve.tensor_tensor(w_lo[:, n], rawp[:, n], w_hi[:, n].bitcast(F32), ALU.subtract)
                if not local:
                    dve.wait_ge(set_hi, 4)
                    dve.tensor_tensor(r_lo[:], r_raw[:], r_hi[:].bitcast(F32), ALU.subtract)

        block = stack.enter_context(nc.Block())

        @block.sync
        def _(sp):
            def load_group(t, g):
                if not (isinstance(t, int) and t == -1):
                    sp.wait_ge(c["sec_mm"].sem, at("sec_mm", t, 0, (g + 1) * N_SEC))
                for n, dst in enumerate((q_st, k_st)):
                    for s, slot in enumerate(SLOTS):
                        src = scratch["parts"][n, slot[n]]
                        heads = slice(g * HG, (g + 1) * HG)
                        if local:
                            src = src.rearrange("(a h f) t -> a f h t", a=2, h=H)
                            for a in range(2):
                                r0 = s * HD + a * (HD // 2)
                                sp.dma_start(dst[r0:r0 + HD // 2, heads], src[a][:, heads])\
                                  .then_inc(c[f"stacked{g}"].sem, 16)
                        else:
                            src = src.rearrange("(h d) t -> d h t", d=HD)
                            sp.dma_start(dst[s * HD:(s + 1) * HD, heads], src[:, heads])\
                              .then_inc(c[f"stacked{g}"].sem, 16)

            def step(t, kind, which, args, p):
                if kind == "uT" and args[0] == len(UT) - 1 and not local:
                    sp.wait_ge(c["uT_lo"].sem, at("uT_lo", t, which))
                    for k, x in enumerate((uT_hi, uT_lo)):
                        sp.dma_start(scratch["uT"][k, :, :, bass.ds(t * T + which * T, T)], x[:].bitcast(F32))\
                          .then_inc(c["uT_out"].sem, 16)
                elif kind == "cut":
                    (n,) = args
                    if n == 0:
                        for g in range(GROUPS):
                            sp.wait_ge(c[f"stacked{g}"].sem, at(f"stacked{g}", t, which, 0))
                    for k in range(3):
                        full = (n + 1) * (SPLITS if k == 0 else 1)
                        sp.wait_ge(c[f"part{k}"].sem, at(f"part{k}", t, which, full))
                        sp.dma_start(scratch["parts"][n, k].rearrange("(c p) t -> p c t", p=P), part[k][:, n])\
                          .then_inc(c["parts_out"].sem, 16)
                    if n == 1:
                        sp.wait_ge(c["parts_out"].sem, at("parts_out", t, which))
                        for g in range(GROUPS if isinstance(t, int) and t == -1 else 2):
                            load_group(t, g)
                elif kind == "weighed" and args[0] >= 2 and not (isinstance(t, int) and t == B - 1):
                    load_group(t, args[0])
                elif kind == "hdT":
                    (i,) = args
                    sp.wait_ge(c["hdT_lo"].sem, at("hdT_lo", t, which, i + 1))
                    for k, x in enumerate((hdT_hi, hdT_lo)):
                        sp.dma_start(scratch["hdT"][k, :, :, bass.ds(t * T + (which * T + i * TT), TT)],
                                     x[:, i % 2].bitcast(F32)).then_inc(c[f"hdT_out{i % 2}"].sem, 16)

            run(sp, step)
            if not local:
                sp.wait_ge(c["uT_out"].sem, c["uT_out"].at(B - 1))
                for k in range(2):
                    sp.wait_ge(c[f"hdT_out{k}"].sem, c[f"hdT_out{k}"].at(B - 1))

        @block.tensor
        def _(pe):
            def side(t, p):
                trips, units = unit_no(t, p)
                if not (isinstance(trips, int) and trips == 0 and units < 2):
                    n = c[f"free{units % 2}"]
                    pe.wait_ge(free_sem(t, p), n.at(trips, units // 2))
                return 6 + units % 2

            def step(t, kind, which, args, p):
                if kind == "uT":
                    t0, t1 = UT[args[0]]
                    pe.wait_ge(c["u"].sem, at("u", t, which, t1))
                    bank = side(t, p)
                    for kc in range(KC):
                        for i in range(t0, t1):
                            col = (kc * (t1 - t0) + i - t0) * TT
                            mm = pe.transpose(ps[:, bank, col:col + TT], u[:, i, kc * P:(kc + 1) * P],
                                              ident[:TT, :TT])
                    mm.then_inc(c["unit_mm"].sem, 1)
                elif kind == "qk":
                    n, ec, s = args
                    s0, s1 = HALVES[s]
                    pe.wait_ge(c["uT_lo"].sem, at("uT_lo", t, which))
                    bank = side(t, p)
                    for kc in range(KC):
                        mm = split3(pe, ps[:, bank, 0:s1 - s0], [w[:, n, kc, ec * P:(ec + 1) * P] for w in (w_hi, w_lo)],
                                    [x[:, kc, s0:s1] for x in (uT_hi, uT_lo)], kc == 0, kc == KC - 1)
                    mm.then_inc(c["unit_mm"].sem, 1)
                elif kind == "v":
                    bank = side(t, p)
                    for i in range(2):
                        cols = slice((2 * args[0] + i) * TT, (2 * args[0] + i + 1) * TT)
                        for kc in range(KC):
                            mm = split3(pe, ps[:TT, bank, i * D:(i + 1) * D], [x[:, kc, cols] for x in (uT_hi, uT_lo)],
                                        [w[:, 2, kc, :] for w in (w_hi, w_lo)], kc == 0, kc == KC - 1)
                    mm.then_inc(c["unit_mm"].sem, 1)
                elif kind == "router":
                    bank = side(t, p)
                    for i in range(NT):
                        for kc in range(KC):
                            mm = split3(pe, ps[:TT, bank, i * E_N:(i + 1) * E_N],
                                        [x[:, kc, i * TT:(i + 1) * TT] for x in (uT_hi, uT_lo)],
                                        [w[:, kc, :] for w in (r_hi, r_lo)], kc == 0, kc == KC - 1)
                    mm.then_inc(c["unit_mm"].sem, 1)
                elif kind == "first":
                    g, unit = args[0], firsts[args[1]]
                    i, seg, h0, per, k0, n, mc = unit
                    if args[1] == 0:
                        pe.wait_ge(c[f"stacked{g}"].sem, at(f"stacked{g}", t, which))
                    bank = side(t, p)
                    for k in range(per):
                        hh = g * HG + h0 + k
                        out = ps[:TT, bank, k * n:(k + 1) * n]
                        mm = pe.matmul(out, q_st[0:STACK, hh, i * TT:(i + 1) * TT], k_st[0:STACK, hh, k0:k0 + n],
                                       start=True, stop=True)
                        if local:
                            mm = pe.matmul(out, identb[:TT, :TT], mask_q[:, mc:mc + n], start=False, stop=True,
                                           skip_group_check=True)
                        elif k0 + n == (i + 1) * TT:
                            mm = pe.matmul(out[:, n - TT:n], identb[:TT, :TT], mask_q[:], start=False, stop=True,
                                           skip_group_check=True)
                    mm.then_inc(c["unit_mm"].sem, 1)
                elif kind == "turn":
                    g, k = args
                    t0, t1 = ((0, 4), (4, 6))[k]
                    if k == 0:
                        pe.wait_ge(c["neg_part"].sem, at("neg_part", t, which, 4 * (g + 1)))
                    bank = side(t, p)
                    for i in range(t0, t1):
                        mm = pe.matmul(ps[:3 * HG, bank, (i - t0) * TT:(i - t0 + 1) * TT],
                                       neg_part[:, i].rearrange("p k h -> p (k h)"), identb[:TT, :TT],
                                       start=True, stop=True)
                    mm.then_inc(c["unit_mm"].sem, 1)
                elif kind == "second":
                    g, k = args
                    x = g * N_SEC + k
                    j, h0, nh, per, n = seconds[k]
                    if x >= 2 or not (isinstance(t, int) and t == 0):
                        pe.wait_ge(c["exp"].sem, at("exp", t, which, x - 1))
                    if k == 0:
                        pe.wait_ge(c["neg_in"].sem, at("neg_in", t, which, 48 * (g + 1)))
                    for e in range(nh):
                        hh = g * HG + h0 + e
                        out = flat(2 * (x % 2))[:TT, 0:n] if n > BANK else \
                            ps[:TT, 2 * (x % 2) + e // per, (e % per) * n:(e % per + 1) * n]
                        for s0 in range(0, n, BANK):
                            s1 = min(n, s0 + BANK)
                            mm = pe.matmul(out[:, s0:s1], k_st[0:ROWS, hh, j * TT:(j + 1) * TT],
                                           q_st[0:ROWS, hh, j * TT + s0:j * TT + s1], start=True, stop=True)
                        w = min(mask_w, n)
                        mm = pe.matmul(out[:, 0:w], identb[:TT, :TT], mask_k[:, 0:w], start=False, stop=True,
                                       skip_group_check=True)
                    mm.then_inc(c["sec_mm"].sem, 1)
                elif kind == "weigh":
                    g, j = args
                    last = g * N_SEC + max(k for k, s in enumerate(seconds) if s[0] == j)
                    pe.wait_ge(c["exp"].sem, at("exp", t, which, last + 1))
                    if g == 0:
                        pe.wait_ge(c["v"].sem, at("v", t, which, j // 2 + 1))
                    if j == 0 and (g >= 1 or not (isinstance(t, int) and t == 0)):
                        pe.wait_ge(c["pv_sb"].sem, at("pv_sb", t, which, g))
                    q0, q1 = j * TT, min(T, j * TT + pw)
                    for bank, (s0, s1) in enumerate(SEGS):
                        a0, a1 = max(q0, s0), min(q1, s1)
                        if a0 >= a1:
                            continue
                        opens = not any(jj * TT < s1 and min(T, jj * TT + pw) > s0 for jj in range(j))
                        for e in range(HG):
                            mm = pe.matmul(ps[32 * e:32 * e + 32, 4 + bank, a0 - s0:a1 - s0],
                                           v_ext[:, j, g * HG + e, :],
                                           probs[:, (g * NT + j) % 2, e, a0 - q0:a1 - q0],
                                           start=opens, stop=True, skip_group_check=not opens)
                    mm.then_inc(c["pv_mm"].sem, 1)
                elif kind == "back":
                    (i,) = args
                    if i == 0:
                        pe.wait_ge(c["pv_sb"].sem, at("pv_sb", t, which))
                    bank = side(t, p)
                    for g in range(GROUPS):
                        mm = pe.transpose(ps[:TT, bank, g * P:(g + 1) * P], pv_sb[:, g, i * TT:(i + 1) * TT], ident[:])
                    mm.then_inc(c["unit_mm"].sem, 1)
                elif kind == "oT":
                    (i,) = args
                    pe.wait_ge(c["o"].sem, at("o", t, which, i + 1))
                    bank = side(t, p)
                    for kc in range(KC):
                        mm = pe.transpose(ps[:, bank, kc * TT:(kc + 1) * TT], o[:, i, kc * P:(kc + 1) * P],
                                          ident[:TT, :TT])
                    mm.then_inc(c["unit_mm"].sem, 1)
                elif kind == "wo":
                    (i,) = args
                    pe.wait_ge(c["oT"].sem, at("oT", t, which, i + 1))
                    bank = side(t, p)
                    for kc in range(KC):
                        mm = pe.matmul(ps[:TT, bank, 0:D], oT[:, i % 2, kc, :], wo[:, kc, :],
                                       start=kc == 0, stop=kc == KC - 1)
                    mm.then_inc(c["unit_mm"].sem, 1)
                elif kind == "hdT":
                    (i,) = args
                    pe.wait_ge(c["hd"].sem, at("hd", t, which, i + 1))
                    bank = side(t, p)
                    for kc in range(KC):
                        mm = pe.transpose(ps[:, bank, kc * TT:(kc + 1) * TT], hd[:, i, kc * P:(kc + 1) * P],
                                          ident[:TT, :TT])
                    mm.then_inc(c["unit_mm"].sem, 1)

            run(pe, step)

        @block.scalar
        def _(act):
            def step(t, kind, which, args, p):
                bank = bank_of(t, p)
                if kind == "uT":
                    k = args[0]
                    t0, t1 = UT[k]
                    act.wait_ge(c["unit_mm"].sem, unit_done(t, p))
                    if k == 0 and not local:
                        act.wait_ge(c["uT_out"].sem, at("uT_out", t, which, 0))
                    act.activation(uT_hi[:, :, t0 * TT:t1 * TT],
                                   ps[:, bank, 0:KC * (t1 - t0) * TT].rearrange("p (k q) -> p k q", k=KC), ACT.Copy)\
                       .then_inc(c["uT_hi"].sem, 1)
                elif kind == "qk" and not local:
                    n, ec, s = args
                    s0, s1 = HALVES[s]
                    act.wait_ge(c["unit_mm"].sem, unit_done(t, p))
                    if (n, ec, s) == (0, 0, 0):
                        act.wait_ge(c["parts_out"].sem, at("parts_out", t, which, 0))
                    act.activation(part[0][:, n, ec, s0:s1], ps[:, bank, 0:s1 - s0], ACT.Copy)\
                       .then_inc(c["part0"].sem, 1)
                elif kind == "cut" and local:
                    (n,) = args
                    act.wait_ge(c["rope_sum"].sem, at("rope_sum", t, which, 2 * n + 2))
                    if n == 0:
                        act.wait_ge(c["parts_out"].sem, at("parts_out", t, which, 0))
                    act.activation(part[0][:, n], rot[:], ACT.Copy).then_inc(c["part0"].sem, 1)
                elif kind == "v":
                    act.wait_ge(c["unit_mm"].sem, unit_done(t, p))
                    for i in range(2):
                        a = act.activation(v_ext[:, 2 * args[0] + i, :, 0:HD],
                                           ps[:TT, bank, i * D:(i + 1) * D].rearrange("p (h d) -> p h d", d=HD),
                                           ACT.Copy)
                        if i == 0:
                            continue
                        a.then_inc(c["v"].sem, 1)
                    act.wait_ge(c["v"].sem, at("v", t, which, args[0] + 1))
                    act.sem_inc(free_sem(t, p), 1)
                elif kind == "route":
                    act.wait_ge(c["r_sub"].sem, at("r_sub", t, which))
                    act.activation(r_exp[:], r_sub[:], ACT.Exp).then_inc(c["r_exp"].sem, 1)
                elif kind == "max_in":
                    (g,) = args
                    act.wait_ge(c["negT"].sem, at("negT", t, which, 2 * g + 2))
                    for k in range(3):
                        act.dma_start(q_st[STACK + k:STACK + k + 1, g * HG:(g + 1) * HG, :],
                                      negT[k * HG:(k + 1) * HG]).then_inc(c["neg_in"].sem, 16)
                elif kind == "second":
                    g, k = args
                    unit = seconds[k]
                    j, h0, nh, per, n = unit
                    x = g * N_SEC + k
                    act.wait_ge(c["sec_mm"].sem, at("sec_mm", t, which, x + 1))
                    s = g * NT + j
                    if s >= 2:
                        act.wait_ge(c["pv_mm"].sem, at("pv_mm", t, which, s - 1))
                    else:
                        act.wait_ge(c["pv_mm"].sem, at("pv_mm", t, which, 0))
                    dst = probs[:, s % 2, h0, 0:n] if n > BANK else \
                        probs[:, s % 2, h0:h0 + nh, 0:n].rearrange("p (b m) n -> p b m n", m=per)
                    act.activation(dst, second_out(x, unit), ACT.Exp).then_inc(c["exp"].sem, 1)
                elif kind == "oT":
                    act.wait_ge(c["unit_mm"].sem, unit_done(t, p))
                    act.activation(oT[:, args[0] % 2].rearrange("p k q -> p (k q)"), ps[:, bank, 0:KC * TT], ACT.Copy)\
                       .then_inc(c["oT"].sem, 1)
                    act.wait_ge(c["oT"].sem, at("oT", t, which, args[0] + 1))
                    act.sem_inc(free_sem(t, p), 1)
                elif kind == "rms":
                    for i in range(NT):
                        act.wait_ge(c["hd_raw"].sem, at("hd_raw", t, which, i + 1))
                        if i:
                            act.wait_ge(c["ss"].sem, at("ss", t, which, i))
                        act.activation(junk[:], hd[:, i], ACT.Square, accum_out=ss[:, i:i + 1])\
                           .then_inc(c["ss"].sem, 1)
                elif kind == "hdT":
                    (i,) = args
                    act.wait_ge(c["unit_mm"].sem, unit_done(t, p))
                    act.wait_ge(c[f"hdT_out{i % 2}"].sem, at("hdT_out0", t, which, 32 * (i // 2)))
                    act.activation(hdT_hi[:, i % 2].rearrange("p k q -> p (k q)"), ps[:, bank, 0:KC * TT],
                                   ACT.Copy).then_inc(c["hdT_hi"].sem, 1)

            run(act, step)

        @block.gpsimd
        def _(pool):
            keep.shared.start(pool, c)

            def step(t, kind, which, args, p):
                if kind == "norm":
                    pool.wait_ge(c["ve"].sem, at("ve", t, which))
                    pool.tensor_tensor(rstd[:], rstd[:], half[:], ALU.pow).then_inc(c["rstd"].sem, 1)
                elif kind == "cut":
                    (n,) = args
                    if local:
                        pool.wait_ge(c["rope_mul"].sem, at("rope_mul", t, which, 8 * n + 8))
                        if n == 0:
                            pool.wait_ge(c["rest"].sem, at("rest", t, which, 0))
                        else:
                            pool.wait_ge(c["rest"].sem, at("rest", t, which, 1))
                        pool.tensor_tensor(rot[:, 0], prod[:, 0], prod[:, 1], ALU.subtract)\
                            .then_inc(c["rope_sum"].sem, 1)
                        pool.tensor_tensor(rot[:, 1], prod[:, 2], prod[:, 3], ALU.add).then_inc(c["rope_sum"].sem, 1)
                    pool.wait_ge(c["rest"].sem, at("rest", t, which, SPLITS * (n + 1)))
                    pool.tensor_tensor(part[1][:, n], rest[:], one[:].unsqueeze(2).to_broadcast([P, KC, T]),
                                       ALU.mult).then_inc(c["part1"].sem, 1)
                    pool.wait_ge(c["part1"].sem, at("part1", t, which, n + 1))
                    pool.tensor_tensor(part[2][:, n], rest[:], part[1][:, n], ALU.subtract).then_inc(c["part2"].sem, 1)
                elif kind == "rms":
                    pool.wait_ge(c["rms_ve"].sem, at("rms_ve", t, which))
                    pool.tensor_tensor(rms[:], rms[:], half[:], ALU.pow).then_inc(c["rms"].sem, 1)

            run(pool, step)

        @block.vector
        def _(dve):
            def step(t, kind, which, args, p):
                bank = bank_of(t, p)
                if kind in UNITS and kind not in ("v", "oT"):
                    dve.wait_ge(c["unit_mm"].sem, unit_done(t, p))
                if kind == "keep":
                    if not (isinstance(t, int) and t == -1):
                        dve.tensor_copy(u_kept[:], u[:])
                elif kind == "norm":
                    for i in range(NT):
                        dve.bn_stats(stats[:, i], h[:, tile_no(t, which, i), :]).then_inc(c["stats"].sem, 1)
                    dve.wait_ge(c["stats"].sem, at("stats", t, which))
                    dve.memset(waiter[:], 0.0)
                    for i in range(NT):
                        dve.bn_aggr(mv[:, i], stats[:, i]).then_inc(c["mv"].sem, 1)
                    dve.wait_ge(c["mv"].sem, at("mv", t, which))
                    dve.tensor_scalar(rstd[:], mv[:, :, 1], LN_EPS, None, ALU.add).then_inc(c["ve"].sem, 1)
                    dve.wait_ge(c["rstd"].sem, at("rstd", t, which))
                    for i in range(NT):
                        dve.tensor_scalar(u[:, i], h[:, tile_no(t, which, i), :], mv[:, i, 0:1], rstd[:, i:i + 1],
                                          ALU.subtract, ALU.mult).then_inc(c["u"].sem, 1)
                elif kind == "uT":
                    k = args[0]
                    t0, t1 = UT[k]
                    dve.wait_ge(c["uT_hi"].sem, at("uT_hi", t, which, k + 1))
                    dve.tensor_tensor(uT_lo[:, :, t0 * TT:t1 * TT],
                                      ps[:, bank, 0:KC * (t1 - t0) * TT].rearrange("p (k q) -> p k q", k=KC),
                                      uT_hi[:, :, t0 * TT:t1 * TT].bitcast(F32), ALU.subtract)\
                       .then_inc(c["uT_lo"].sem, 1)
                    dve.wait_ge(c["uT_lo"].sem, at("uT_lo", t, which, k + 1))
                    dve.sem_inc(free_sem(t, p), 1)
                elif kind == "qk" and local:
                    n, ec, s = args
                    s0, s1 = HALVES[s]
                    if (ec, s) == (0, 0):
                        dve.wait_ge(c["rope_sum"].sem, at("rope_sum", t, which, 2 * n))
                    for k, table in (((0, cos), (2, sin)), ((1, sin), (3, cos)))[ec]:
                        dve.tensor_tensor(prod[:, k, s0:s1], ps[:, bank, 0:s1 - s0], table[:, s0:s1], ALU.mult)\
                           .then_inc(c["rope_mul"].sem, 1)
                    dve.wait_ge(c["rope_mul"].sem, at("rope_mul", t, which, 8 * n + 4 * s + 2 * ec + 2))
                    dve.sem_inc(free_sem(t, p), 1)
                elif kind == "qk":
                    n, ec, s = args
                    s0, s1 = HALVES[s]
                    unit = 4 * n + 2 * s + ec
                    dve.wait_ge(c["part0"].sem, at("part0", t, which, unit + 1))
                    if (ec, s) == (0, 0):
                        dve.wait_ge(c["part2"].sem, at("part2", t, which, n))
                    dve.tensor_tensor(rest[:, ec, s0:s1], ps[:, bank, 0:s1 - s0], part[0][:, n, ec, s0:s1],
                                      ALU.subtract).then_inc(c["rest"].sem, 1)
                    dve.wait_ge(c["rest"].sem, at("rest", t, which, unit + 1))
                    dve.sem_inc(free_sem(t, p), 1)
                elif kind == "cut" and local:
                    (n,) = args
                    dve.wait_ge(c["part0"].sem, at("part0", t, which, n + 1))
                    dve.wait_ge(c["part2"].sem, at("part2", t, which, n))
                    dve.tensor_tensor(rest[:], rot[:], part[0][:, n], ALU.subtract).then_inc(c["rest"].sem, 1)
                elif kind == "router":
                    logits = ps[:TT, bank, 0:NT * E_N].rearrange("p (i e) -> p i e", e=E_N)
                    dve.tensor_reduce(r_max[:], logits, AX_X, ALU.max).then_inc(c["r_max"].sem, 1)
                    dve.wait_ge(c["r_max"].sem, at("r_max", t, which))
                    dve.tensor_tensor(r_sub[:], logits, r_max[:].unsqueeze(2).to_broadcast([TT, NT, E_N]),
                                      ALU.subtract).then_inc(c["r_sub"].sem, 1)
                    dve.wait_ge(c["r_sub"].sem, at("r_sub", t, which))
                    dve.sem_inc(free_sem(t, p), 1)
                elif kind == "route":
                    dve.wait_ge(c["r_exp"].sem, at("r_exp", t, which))
                    dve.tensor_reduce(r_sum[:], r_exp[:], AX_X, ALU.add).then_inc(c["r_sum"].sem, 1)
                    dve.wait_ge(c["r_sum"].sem, at("r_sum", t, which))
                    dve.reciprocal(r_inv[:], r_sum[:]).then_inc(c["r_inv"].sem, 1)
                    dve.wait_ge(c["r_inv"].sem, at("r_inv", t, which))
                    dve.tensor_tensor(r_prob[:], r_exp[:], r_inv[:].unsqueeze(2).to_broadcast([TT, NT, E_N]),
                                      ALU.mult).then_inc(c["r_prob"].sem, 1)
                    dve.wait_ge(c["r_prob"].sem, at("r_prob", t, which))
                    dve.memset(waiter[:], 0.0)
                    for i in range(NT):
                        dve.max(top_v[:, i], r_prob[:, i]).then_inc(c["top_v"].sem, 1)
                    dve.wait_ge(c["top_v"].sem, at("top_v", t, which))
                    dve.memset(waiter[:], 0.0)
                    for i in range(NT):
                        dve.max_index(top_i[:, i], top_v[:, i], r_prob[:, i]).then_inc(c["top_i"].sem, 1)
                    dve.wait_ge(c["top_i"].sem, at("top_i", t, which))
                    dve.tensor_copy(top_f[:], top_i[:]).then_inc(c["top_f"].sem, 1)
                    dve.wait_ge(c["top_f"].sem, at("top_f", t, which))
                    for i in range(NT):
                        for k in range(2):
                            dve.tensor_scalar(pick[:, k, i], iota[:], top_f[:, i, k:k + 1], top_v[:, i, k:k + 1],
                                              ALU.is_equal, ALU.mult).then_inc(c["pick"].sem, 1)
                    dve.wait_ge(c["pick"].sem, at("pick", t, which))
                    dve.tensor_tensor(route[:, bass.ds(tile_no(t, which, 0), NT), :], pick[:, 0], pick[:, 1], ALU.add)\
                       .then_inc(c["route"].sem, 1)
                elif kind == "first":
                    g, unit = args[0], firsts[args[1]]
                    i, seg, h0, per, k0, n, mc = unit
                    dst = (neg_b[:, i - 4] if seg else neg[:, i])[:, g * HG + h0:g * HG + h0 + per]
                    dve.tensor_reduce(dst, ps[:TT, bank, 0:per * n].rearrange("p (m n) -> p m n", n=n),
                                      AX_X, ALU.max, negate=True).then_inc(free_sem(t, p), 1)
                elif kind == "maxima":
                    (g,) = args
                    trips, units = unit_no(t, p)
                    for back in (1, 2):
                        dve.wait_ge(c[f"free{(units - back) % 2}"].sem,
                                    c[f"free{(units - back) % 2}"].at(trips, (units - back) // 2 + 1))
                    heads = slice(g * HG, (g + 1) * HG)
                    lo = 4 if not local else NT - 1
                    part_neg = neg[:, lo:NT, heads]
                    other = neg_b[:, :, heads] if not local else part_neg
                    dve.tensor_tensor(part_neg, part_neg, other, ALU.min).then_inc(c["neg"].sem, 1)
                    dve.wait_ge(c["neg"].sem, at("neg", t, which, g + 1))
                    dve.tensor_copy(neg_part[:, :, 0], neg[:, :, heads]).then_inc(c["neg_part"].sem, 1)
                    dve.wait_ge(c["neg_part"].sem, at("neg_part", t, which, 4 * g + 1))
                    dve.tensor_tensor(neg_rest[:], neg[:, :, heads], neg_part[:, :, 0], ALU.subtract)\
                       .then_inc(c["neg_part"].sem, 1)
                    dve.wait_ge(c["neg_part"].sem, at("neg_part", t, which, 4 * g + 2))
                    dve.tensor_copy(neg_part[:, :, 1], neg_rest[:]).then_inc(c["neg_part"].sem, 1)
                    dve.wait_ge(c["neg_part"].sem, at("neg_part", t, which, 4 * g + 3))
                    dve.tensor_tensor(neg_part[:, :, 2], neg_rest[:], neg_part[:, :, 1], ALU.subtract)\
                       .then_inc(c["neg_part"].sem, 1)
                elif kind == "turn":
                    g, k = args
                    t0, t1 = ((0, 4), (4, 6))[k]
                    if k == 0:
                        dve.wait_ge(c["neg_in"].sem, at("neg_in", t, which, 48 * g))
                    dve.tensor_copy(negT[:, t0 * TT:t1 * TT], ps[:3 * HG, bank, 0:(t1 - t0) * TT])\
                       .then_inc(c["negT"].sem, 1)
                    dve.wait_ge(c["negT"].sem, at("negT", t, which, 2 * g + k + 1))
                    dve.sem_inc(free_sem(t, p), 1)
                elif kind == "weighed":
                    (g,) = args
                    dve.wait_ge(c["pv_mm"].sem, at("pv_mm", t, which, (g + 1) * NT))
                    dve.tensor_copy(pv_sb[:, g, :], flat(4)[:, 0:T]).then_inc(c["pv_sb"].sem, 1)
                elif kind == "back":
                    (i,) = args
                    rows = ps[:TT, bank, :].rearrange("p (h w) -> p h w", w=2 * HD)
                    dve.reciprocal(rden[:, i], rows[:, :, HD]).then_inc(c["rden"].sem, 1)
                    dve.wait_ge(c["rden"].sem, at("rden", t, which, i + 1))
                    dve.tensor_tensor(o[:, i].rearrange("p (h d) -> p h d", d=HD), rows[:, :, 0:HD],
                                      rden[:, i].unsqueeze(2).to_broadcast([TT, H, HD]), ALU.mult)\
                       .then_inc(c["o"].sem, 1)
                    dve.wait_ge(c["o"].sem, at("o", t, which, i + 1))
                    dve.sem_inc(free_sem(t, p), 1)
                elif kind == "wo" and local:
                    (i,) = args
                    tile = tile_no(t, which, i)
                    dve.tensor_tensor(h[:, tile, :], ps[:TT, bank, 0:D], h[:, tile, :], ALU.add)\
                       .then_inc(c["h"].sem, 1)
                    dve.wait_ge(c["h"].sem, at("h", t, which, i + 1))
                    dve.sem_inc(free_sem(t, p), 1)
                elif kind == "wo":
                    (i,) = args
                    dve.tensor_copy(hd[:, i], ps[:TT, bank, 0:D]).then_inc(c["hd_raw"].sem, 1)
                    dve.wait_ge(c["hd_raw"].sem, at("hd_raw", t, which, i + 1))
                    dve.sem_inc(free_sem(t, p), 1)
                elif kind == "rms":
                    dve.wait_ge(c["ss"].sem, at("ss", t, which))
                    dve.tensor_scalar(rms[:], ss[:], 1.0 / D, LN_EPS, ALU.mult, ALU.add).then_inc(c["rms_ve"].sem, 1)
                elif kind == "hd":
                    (i,) = args
                    tile = tile_no(t, which, i)
                    if i == 0:
                        dve.wait_ge(c["rms"].sem, at("rms", t, which))
                    dve.scalar_tensor_tensor(hd[:, i], hd[:, i], rms[:, i:i + 1], norm_w[:], ALU.mult, ALU.mult)\
                       .then_inc(c["hd_t"].sem, 1)
                    dve.wait_ge(c["hd_t"].sem, at("hd_t", t, which, i + 1))
                    dve.tensor_tensor(hd[:, i], hd[:, i], rows_of(t)[:, i], ALU.add).then_inc(c["hd"].sem, 1)
                    dve.wait_ge(c["hd"].sem, at("hd", t, which, i + 1))
                    dve.tensor_tensor(h[:, tile, :], hd[:, i], h[:, tile, :], ALU.add).then_inc(c["h"].sem, 1)
                elif kind == "hdT":
                    (i,) = args
                    dve.wait_ge(c["hdT_hi"].sem, at("hdT_hi", t, which, i + 1))
                    dve.tensor_tensor(hdT_lo[:, i % 2].rearrange("p k q -> p (k q)"), ps[:, bank, 0:KC * TT],
                                      hdT_hi[:, i % 2].bitcast(F32).rearrange("p k q -> p (k q)"), ALU.subtract)\
                       .then_inc(c["hdT_lo"].sem, 1)
                    dve.wait_ge(c["hdT_lo"].sem, at("hdT_lo", t, which, i + 1))
                    dve.sem_inc(free_sem(t, p), 1)

            def rows_of(t):
                return u if isinstance(t, int) and t == B else u_kept

            run(dve, step)
            dve.wait_ge(c["h"].sem, c["h"].at(B - 1))
        keep.shared.close(c)


E_H = 256
FF = 1024
CT = 4
CN = CT * TT
NCH = B * T // CN
PAIRS = E_N // 2
NALL = E_N + FF // E_H


def stage_experts(nc, keep, io, h, route, scratch):
    with ExitStack() as stack:
        m = Memory(nc, stack, keep)
        uT = m.sb("c_uT", [P, 2, KC, B * T], F32R)
        hdT = m.sb("c_hdT", [P, 2, KC, B * T], F32R)
        acc = m.sb("c_acc", [TT, NTILES, D], F32)
        raw = [m.sb(f"c_raw{k}", [P, 3, KC, E_H], F32) for k in range(2)]
        w_hi = [m.sb(f"c_w_hi{k}", [P, 3, KC, E_H], F32R) for k in range(2)]
        w_lo = [m.sb(f"c_w_lo{k}", [P, 3, KC, E_H], F32R) for k in range(2)]
        act_a = m.sb("c_act_a", [P, 2, CN], F32)
        g = m.sb("c_g", [P, 2, CN], F32)
        g_hi = m.sb("c_g_hi", [P, 2, CN], F32R)
        g_lo = m.sb("c_g_lo", [P, 2, CN], F32R)
        norm_w = m.sb("c_norm_w", [TT, 2, D], F32)
        half = m.sb("c_half", [TT, NT], F32)
        junk = m.sb("c_junk", [TT, D], F32)
        ss = m.sb("c_ss", [TT, NTILES], F32)
        rms_p = m.sb("c_rms", [TT, CT], F32)
        t = m.sb("c_t", [TT, CT, D], F32)
        ps = m.ps("c_ps", [P, 8, BANK])

        const_in = m.sem("c_const_in")
        zeroed = m.sem("c_zeroed")
        x_in, hd_in = m.sem("c_x_in"), m.sem("c_hd_in")
        raw_in = [m.sem(f"c_raw_in{k}") for k in range(2)]
        made_hi, made_lo = m.sem("c_made_hi"), m.sem("c_made_lo")
        up_mm, down_mm = m.sem("c_up_mm"), m.sem("c_down_mm")
        silu, gated, gated_hi, gated_lo = m.sem("c_silu"), m.sem("c_gated"), m.sem("c_gated_hi"), m.sem("c_gated_lo")
        added = m.sem("c_added")
        sq, ve, rms_ok, scaled, h_upd = m.sem("c_sq"), m.sem("c_ve"), m.sem("c_rms_ok"), m.sem("c_scaled"), m.sem("c_h")

        def walk(eng, prepare, head, tail):

            def expert(e, par, last=False, before_dense=False, dense=False, final=None, opens=False):
                n0 = e * NCH
                if not last:
                    prepare(e + 1, 1 - par)
                with eng.Fori(1, NCH) as k:
                    head(par, k, n0 + k, dense)
                    tail(par, k - 1, n0 + k - 1, e, dense, final, opens)
                if not last:
                    head(1 - par, 0, n0 + NCH, dense or before_dense)
                tail(par, NCH - 1, n0 + NCH - 1, e, dense, final, opens)

            prepare(0, 0)
            head(0, 0, 0, False)
            with eng.Fori(0, PAIRS - 1) as pair:
                for par in range(2):
                    expert(pair * 2 + par, par)
            expert(E_N - 2, 0)
            expert(E_N - 1, 1, before_dense=True, final=0)
            for e in range(E_N, NALL):
                expert(e, e % 2, last=e == NALL - 1, dense=True, final=1 if e == NALL - 1 else None, opens=e == E_N)

        def skip(*_):
            return

        def raw_count(e, par):
            return (e - par) * 24 + 48

        def tile_of(buf, c, i):
            return buf[:, c * CT + i, :]

        def column_of(buf, c, i):
            return buf[:, bass.ds(c * CT + i, 1)]

        block = stack.enter_context(nc.Block())

        @block.sync
        def _(sp):
            def weights(e, par, dense):
                for k, name in enumerate(("1", "3", "2")):
                    if not dense:
                        src = io[f"L0_ffn_ew{name}"][bass.ds(e, 1), :, :].rearrange("a (k p) n -> p (a k) n", p=P)
                    elif name == "2":
                        s = e - E_N
                        src = io["L0_ffn_w2"][s * E_H:(s + 1) * E_H, :].rearrange("(k p) n -> p k n", p=P)
                    else:
                        s = e - E_N
                        src = io[f"L0_ffn_w{name}"][:, s * E_H:(s + 1) * E_H].rearrange("(k p) n -> p k n", p=P)
                    sp.dma_start(raw[par][:, k], src).then_inc(raw_in[par], 16)

            def rows(c, name, dst, sem):
                for k in range(2):
                    sp.dma_start(dst[:, k, :, c * CN:(c + 1) * CN].bitcast(F32),
                                 scratch[name][k, :, :, c * CN:(c + 1) * CN]).then_inc(sem, 16)
                sp.wait_ge(sem, 32 * (c + 1))

            weights(0, 0, False)
            rows(0, "uT", uT, x_in)
            weights(1, 1, False)
            for k, name in enumerate(("moe_norm_w", "ff_norm_w")):
                sp.dma_start(norm_w[:, k], io[f"L0_ffn_{name}"].rearrange("(a d) -> a d", a=1).to_broadcast([TT, D]))\
                  .then_inc(const_in, 16)
            sp.dma_start(half[:], io["minus_half"]).then_inc(const_in, 16)
            for c in range(1, NCH):
                rows(c, "uT", uT, x_in)
            for c in range(NCH):
                rows(c, "hdT", hdT, hd_in)
            with sp.Fori(1, PAIRS) as pair:
                for par in range(2):
                    sp.wait_ge(made_lo, pair * 2 + par - 1)
                    weights(pair * 2 + par, par, False)
            for e in range(E_N, NALL):
                sp.wait_ge(made_lo, e - 1)
                weights(e, e % 2, True)

        @block.tensor
        def _(pe):
            def prepare(e, par):
                if isinstance(e, int) and e == 0:
                    pe.wait_ge(made_lo, 1)

            def head(par, c, n, dense):
                if isinstance(c, int):
                    pe.wait_ge(made_lo, n // NCH + 1 if isinstance(n, int) else next_expert[0] + 1)
                pe.wait_ge(hd_in if dense else x_in, c * 32 + 32)
                pe.wait_ge(gated, FIRST + n * 2)
                x = hdT if dense else uT
                for hc in range(2):
                    for k in range(2):
                        for kc in range(KC):
                            mm = split3(pe, ps[:, 2 * hc + k, 0:CN],
                                        [w[par][:, k, kc, hc * P:(hc + 1) * P] for w in (w_hi, w_lo)],
                                        [x[:, s, kc, bass.ds(c * CN, CN)] for s in range(2)], kc == 0, kc == KC - 1)
                    mm.then_inc(up_mm, 1)

            def tail(par, c, n, e, dense, final, opens):
                pe.wait_ge(gated_lo, FIRST + n * 2 + 2)
                pe.wait_ge(added, FIRST + n * 4)
                for i in range(CT):
                    for hc in range(2):
                        mm = split3(pe, ps[:TT, 4 + i, 0:D], [x[:, hc, i * TT:(i + 1) * TT] for x in (g_hi, g_lo)],
                                    [w[par][:, 2, hc, :] for w in (w_hi, w_lo)], hc == 0, hc == 1)
                    mm.then_inc(down_mm, 1)

            next_expert = [0]

            def note(e, par):
                next_expert[0] = e

            walk(pe, note, head, tail)

        @block.scalar
        def _(act):
            def prepare(e, par):
                act.wait_ge(raw_in[par], raw_count(e, par))
                if not (isinstance(e, int) and e == 0):
                    act.wait_ge(down_mm, FIRST + (e - 1) * (CT * NCH))
                act.activation(w_hi[par][:], raw[par][:], ACT.Copy).then_inc(made_hi, 1)

            def head(par, c, n, dense):
                for hc in range(2):
                    act.wait_ge(up_mm, n * 2 + hc + 1)
                    act.wait_ge(gated, FIRST + n * 2)
                    act.activation(act_a[:, hc], ps[:, 2 * hc, 0:CN], ACT.Silu).then_inc(silu, 1)
                for hc in range(2):
                    act.wait_ge(gated, FIRST + n * 2 + hc + 1)
                    act.wait_ge(down_mm, FIRST + n * CT)
                    act.activation(g_hi[:, hc], g[:, hc], ACT.Copy).then_inc(gated_hi, 1)

            def tail(par, c, n, e, dense, final, opens):
                if final is None:
                    return
                for i in range(CT):
                    act.wait_ge(added, FIRST + n * CT + i + 1)
                    act.wait_ge(sq, FIRST + c * CT + (final * NTILES + i))
                    act.activation(junk[:], tile_of(acc, c, i), ACT.Square, accum_out=column_of(ss, c, i))\
                       .then_inc(sq, 1)

            walk(act, prepare, head, tail)

        @block.gpsimd
        def _(pool):
            def prepare(e, par):
                pool.wait_ge(made_hi, e + 1)
                pool.tensor_tensor(w_lo[par][:], raw[par][:], w_hi[par][:].bitcast(F32), ALU.subtract)\
                    .then_inc(made_lo, 1)

            def head(par, c, n, dense):
                for hc in range(2):
                    pool.wait_ge(gated_hi, n * 2 + hc + 1)
                    pool.tensor_tensor(g_lo[:, hc], g[:, hc], g_hi[:, hc].bitcast(F32), ALU.subtract)\
                        .then_inc(gated_lo, 1)

            def tail(par, c, n, e, dense, final, opens):
                if final is None:
                    return
                pool.wait_ge(ve, c + (final * NCH + 1))
                pool.tensor_tensor(rms_p[:], rms_p[:], half[:, 0:CT], ALU.pow).then_inc(rms_ok, 1)

            for sem in (gated, added, gated_lo, down_mm, sq):
                pool.sem_inc(sem, FIRST)
            pool.wait_ge(const_in, 48)
            pool.memset(acc[:], 0.0).then_inc(zeroed, 1)
            pool.wait_ge(zeroed, 1)
            walk(pool, prepare, head, tail)

        @block.vector
        def _(dve):
            def head(par, c, n, dense):
                for hc in range(2):
                    dve.wait_ge(silu, n * 2 + hc + 1)
                    dve.wait_ge(gated_lo, FIRST + n * 2)
                    dve.tensor_tensor(g[:, hc], act_a[:, hc], ps[:, 2 * hc + 1, 0:CN], ALU.mult).then_inc(gated, 1)

            def tail(par, c, n, e, dense, final, opens):
                for i in range(CT):
                    dve.wait_ge(down_mm, FIRST + n * CT + i + 1)
                    a, out = tile_of(acc, c, i), ps[:TT, 4 + i, 0:D]
                    if opens:
                        dve.wait_ge(scaled, c * CT + CT)
                        dve.tensor_copy(a, out).then_inc(added, 1)
                    elif dense:
                        dve.tensor_tensor(a, out, a, ALU.add).then_inc(added, 1)
                    else:
                        dve.scalar_tensor_tensor(a, out, route[:, c * CT + i, bass.ds(e, 1)], a, ALU.mult, ALU.add)\
                           .then_inc(added, 1)
                if final is not None:
                    dve.wait_ge(sq, FIRST + c * CT + (final * NTILES + CT))
                    dve.tensor_scalar(rms_p[:], ss[:, bass.ds(c * CT, CT)], 1.0 / D, LN_EPS, ALU.mult, ALU.add)\
                       .then_inc(ve, 1)
                    dve.wait_ge(rms_ok, c + (final * NCH + 1))
                    for i in range(CT):
                        dve.scalar_tensor_tensor(t[:, i], tile_of(acc, c, i), rms_p[:, i:i + 1], norm_w[:, final],
                                                 ALU.mult, ALU.mult).then_inc(scaled, 1)
                    for i in range(CT):
                        dve.wait_ge(scaled, c * CT + (final * NTILES + i + 1))
                        dve.tensor_tensor(tile_of(h, c, i), tile_of(h, c, i), t[:, i], ALU.add).then_inc(h_upd, 1)

            dve.wait_ge(zeroed, 1)
            walk(dve, skip, head, tail)
            dve.wait_ge(h_upd, 2 * NTILES)


FH = 1024
FC = FH // P
QP, MIN_RANGE = 127.0, 1e-6
ROUND = 1.5 * 2.0 ** 23


def stage_quantised(nc, keep, io, h, ident):
    with ExitStack() as stack:
        m = Memory(nc, stack, keep)
        hid = m.sb("e_hid", [P, FC, B * T], F32)
        flat_hid = hid[:].rearrange("p c t -> p (c t)")
        w1 = flat_hid[:, 0:FC * D].rearrange("p (c d) -> p c d", c=FC)
        w2 = flat_hid[:, FC * D:FC * D + KC * FH].rearrange("p (c f) -> p c f", c=KC)
        w1T = m.sb("e_w1T", [P, KC, FC, P], BF16)
        w2T = m.sb("e_w2T", [P, FC, D], BF16)
        b1 = m.sb("e_b1", [P, FC], F32)
        b2 = m.sb("e_b2", [TT, D], F32)
        half = m.sb("e_half", [TT, NT], F32)
        stats = m.sb("e_stats", [TT, NTILES, 6], F32)
        mv = m.sb("e_mv", [TT, NTILES, 2], F32)
        rstd = m.sb("e_rstd", [TT, NTILES], F32)
        u = m.sb("e_u", [TT, NTILES, D], F32)
        uT = m.sb("e_uT", [P, KC, B * T], BF16)
        qh = m.sb("e_qh", [P, 2, FC, CN], BF16)
        peak = m.sb("e_peak", [P, 3], F32)
        peak_u = m.sb("e_peak_u", [TT, NTILES], F32)
        peak_h = m.sb("e_peak_h", [P, NCH * FC], F32)
        top = m.sb("e_top", [P, 4], F32)
        peak_p = m.sb("e_peak_p", [P, 1], F32)
        scale = m.sb("e_scale", [P, 4], F32)
        inv = m.sb("e_inv", [P, 4], F32)
        out_scale = m.sb("e_out_scale", [P, 2], F32)
        b1s = m.sb("e_b1s", [P, FC], F32)
        b2s = m.sb("e_b2s", [TT, D], F32)
        ps = m.ps("e_ps", [P, 8, BANK])

        loaded = m.sem("e_loaded")
        stat, agg, ve, rstd_ok, norm = (m.sem(f"e_{n}") for n in ("stat", "agg", "ve", "rstd_ok", "norm"))
        peaked, topped, scaled = m.sem("e_peaked"), m.sem("e_topped"), m.sem("e_scaled")
        w_shift, w_int, w_turned, w_ready = (m.sem(f"e_{n}") for n in ("w_shift", "w_int", "w_turned", "w_ready"))
        u_shift, u_int, u_turned, u_ready = (m.sem(f"e_{n}") for n in ("u_shift", "u_int", "u_turned", "u_ready"))
        zero_p = m.sem("e_zero_p")
        up_mm, gelu, hid_peak = m.sem("e_up_mm"), m.sem("e_gelu"), m.sem("e_hid_peak")
        q_shift, q_ready, down_mm, added, biased = (m.sem(f"e_{n}") for n in
                                                    ("q_shift", "q_ready", "down_mm", "added", "biased"))
        W1, W2, U, HID = range(4)

        block = stack.enter_context(nc.Block())

        @block.sync
        def _(sp):
            sp.dma_start(w1, io["L1_ffn_w1"].rearrange("(p c) d -> p c d", c=FC)).then_inc(loaded, 16)
            sp.dma_start(w2, io["L1_ffn_w2"].rearrange("(c p) f -> p c f", p=P)).then_inc(loaded, 16)
            sp.dma_start(b1[:], io["L1_ffn_b1"].rearrange("(p c) -> p c", c=FC)).then_inc(loaded, 16)
            sp.dma_start(b2[:], io["L1_ffn_b2"].rearrange("(a d) -> a d", a=1).to_broadcast([TT, D])).then_inc(loaded, 16)
            sp.dma_start(half[:], io["minus_half"]).then_inc(loaded, 16)

        @block.gpsimd
        def _(pool):
            reduce_max = bass.bass_isa.ReduceOp.max

            def over_rows(k, src):
                pool.partition_all_reduce(top[:, k:k + 1], src, P, reduce_max).then_inc(topped, 1)

            for sem in (gelu, added, down_mm):
                pool.sem_inc(sem, FIRST)
            pool.memset(peak_p[:], 0.0).then_inc(zero_p, 1)
            pool.wait_ge(loaded, 80)
            for b in range(B):
                cols = slice(b * NT, (b + 1) * NT)
                pool.wait_ge(agg, (b + 1) * NT)
                pool.tensor_scalar(rstd[:, cols], mv[:, cols, 1], LN_EPS, None, ALU.add).then_inc(ve, 1)
                pool.wait_ge(ve, b + 1)
                pool.tensor_tensor(rstd[:, cols], rstd[:, cols], half[:], ALU.pow).then_inc(rstd_ok, 1)
                if b == 0:
                    for k in (W1, W2):
                        pool.wait_ge(peaked, k + 1)
                        over_rows(k, peak[:, k:k + 1])
            pool.wait_ge(peaked, U + 1)
            over_rows(U, peak_p[:])
            pool.wait_ge(peaked, HID + 1)
            over_rows(HID, peak[:, 2:3])

        @block.scalar
        def _(act):
            for k, w in ((W1, w1), (W2, w2)):
                act.wait_ge(scaled, k + 1)
                act.activation(w, w, ACT.Copy, scale=inv[:, k:k + 1], bias=ROUND).then_inc(w_shift, 1)
            for n in range(8):
                act.wait_ge(w_turned, n + 1)
                src = ps[:, n % 4, :].rearrange("p (c q) -> p c q", q=P)
                dst = w1T[:, n // 2, 4 * (n % 2):4 * (n % 2) + 4, :] if n < 4 else \
                    w2T[:, 2 * (n - 4):2 * (n - 4) + 2, :].rearrange("p c (k q) -> p (c k) q", q=P)
                act.activation(dst, src, ACT.Copy).then_inc(w_ready, 1)
            act.wait_ge(scaled, U + 1)
            for c in range(NCH):
                rows = u[:, c * CT:(c + 1) * CT, :]
                act.activation(rows, rows, ACT.Copy, scale=inv[:TT, U:U + 1], bias=ROUND).then_inc(u_shift, 1)
            for c in range(NCH):
                act.wait_ge(u_turned, c + 1)
                act.activation(uT[:, :, c * CN:(c + 1) * CN], ps[:, 4 + 2 * (c % 2):6 + 2 * (c % 2), 0:CN], ACT.Copy)\
                   .then_inc(u_ready, 1)
            act.wait_ge(biased, 1)
            with act.Fori(0, NCH) as c:
                for k in range(FC):
                    act.wait_ge(up_mm, c * FC + k + 1)
                    act.activation(hid[:, k, bass.ds(c * CN, CN)], ps[:, k, 0:CN], ACT.Gelu,
                                   scale=out_scale[:, 0:1], bias=b1s[:, k:k + 1]).then_inc(gelu, 1)
            act.wait_ge(scaled, HID + 1)
            with act.Fori(0, NCH) as c:
                rows = hid[:, :, bass.ds(c * CN, CN)]
                act.activation(rows, rows, ACT.Copy, scale=inv[:, HID:HID + 1], bias=ROUND).then_inc(q_shift, 1)

        @block.tensor
        def _(pe):
            pe.wait_ge(w_int, 1)
            for n in range(4):
                for k in range(4):
                    mm = pe.transpose(ps[:, n, k * P:(k + 1) * P],
                                      w1[:, 4 * (n % 2) + k, (n // 2) * P:(n // 2 + 1) * P], ident[:])
                mm.then_inc(w_turned, 1)
            pe.wait_ge(w_int, 2)
            for n in range(4):
                pe.wait_ge(w_ready, n + 1)
                for k in range(4):
                    f = 2 * n + k // 2
                    mm = pe.transpose(ps[:, n, k * P:(k + 1) * P], w2[:, k % 2, f:FH:FC], ident[:])
                mm.then_inc(w_turned, 1)
            for c in range(NCH):
                pe.wait_ge(u_int, c + 1)
                if c >= 2:
                    pe.wait_ge(u_ready, c - 1)
                for i in range(CT):
                    for kc in range(KC):
                        mm = pe.transpose(ps[:, 4 + 2 * (c % 2) + kc, i * TT:(i + 1) * TT],
                                          u[:, c * CT + i, kc * P:(kc + 1) * P], ident[:TT, :TT])
                mm.then_inc(u_turned, 1)
            pe.wait_ge(u_ready, NCH)
            pe.wait_ge(w_ready, 8)
            with pe.Fori(0, NCH) as c:
                for k in range(FC):
                    pe.wait_ge(gelu, FIRST + c * FC)
                    for kc in range(KC):
                        mm = pe.matmul(ps[:, k, 0:CN], w1T[:, kc, k, :], uT[:, kc, bass.ds(c * CN, CN)],
                                       start=kc == 0, stop=kc == KC - 1)
                    mm.then_inc(up_mm, 1)
            with pe.Fori(0, NCH // 2) as c2:
                for par in range(2):
                    pe.wait_ge(q_ready, c2 * 2 + par + 1)
                    for i in range(CT):
                        pe.wait_ge(added, FIRST + c2 * 8)
                        for k in range(FC):
                            mm = pe.matmul(ps[:TT, 4 * par + i, 0:D], qh[:, par, k, i * TT:(i + 1) * TT], w2T[:, k, :],
                                           start=k == 0, stop=k == FC - 1)
                        mm.then_inc(down_mm, 1)

        @block.vector
        def _(dve):
            chain = m.sem("e_chain")
            links = [0]

            def link(ins):
                links[0] += 1
                ins.then_inc(chain, 1)
                dve.wait_ge(chain, links[0])

            def scale_of(k):
                dve.wait_ge(topped, k + 1)
                col = slice(k, k + 1)
                link(dve.tensor_scalar(scale[:, col], top[:, col], MIN_RANGE, 1.0 / QP, ALU.max, ALU.mult))
                dve.reciprocal(inv[:, col], scale[:, col]).then_inc(scaled, 1)

            dve.wait_ge(loaded, 80)
            dve.tensor_reduce(peak[:, 0:1], flat_hid[:, 0:FC * D], AX_X, ALU.max, apply_absolute_value=True)\
               .then_inc(peaked, 1)
            dve.tensor_reduce(peak[:, 1:2], flat_hid[:, FC * D:2 * FC * D], AX_X, ALU.max, apply_absolute_value=True)\
               .then_inc(peaked, 1)
            for b in range(B):
                for i in range(b * NT, (b + 1) * NT):
                    dve.bn_stats(stats[:, i], h[:, i, :]).then_inc(stat, 1)
                for i in range(b * NT, (b + 1) * NT):
                    dve.wait_ge(stat, i + 1)
                    dve.bn_aggr(mv[:, i], stats[:, i]).then_inc(agg, 1)
            for b in range(B):
                dve.wait_ge(rstd_ok, b + 1)
                for i in range(b * NT, (b + 1) * NT):
                    dve.tensor_scalar(u[:, i], h[:, i, :], mv[:, i, 0:1], rstd[:, i:i + 1], ALU.subtract, ALU.mult)\
                       .then_inc(norm, 1)
                dve.wait_ge(norm, (b + 1) * NT)
                link(dve.tensor_reduce(peak_u[:, b * NT:(b + 1) * NT], u[:, b * NT:(b + 1) * NT, :], AX_X, ALU.max,
                                       apply_absolute_value=True))
            dve.wait_ge(zero_p, 1)
            dve.tensor_reduce(peak_p[:TT], peak_u[:], AX_X, ALU.max).then_inc(peaked, 1)
            scale_of(W1)
            scale_of(W2)
            for k, w in ((W1, flat_hid[:, 0:FC * D]), (W2, flat_hid[:, FC * D:2 * FC * D])):
                dve.wait_ge(w_shift, k + 1)
                dve.tensor_scalar(w, w, -ROUND, None, ALU.add).then_inc(w_int, 1)
            scale_of(U)
            for c in range(NCH):
                dve.wait_ge(u_shift, c + 1)
                rows = u[:, c * CT:(c + 1) * CT, :]
                dve.tensor_scalar(rows, rows, -ROUND, None, ALU.add).then_inc(u_int, 1)
            dve.wait_ge(scaled, 3)
            link(dve.tensor_tensor(out_scale[:, 0:1], scale[:, W1:W1 + 1], scale[:, U:U + 1], ALU.mult))
            dve.tensor_scalar(b1s[:], b1[:], out_scale[:, 0:1], None, ALU.mult).then_inc(biased, 1)
            with dve.Fori(0, NCH) as c:
                for k in range(FC):
                    dve.wait_ge(gelu, FIRST + c * FC + k + 1)
                    dve.tensor_reduce(peak_h[:, bass.ds(c * FC + k, 1)], hid[:, k, bass.ds(c * CN, CN)], AX_X, ALU.max,
                                      apply_absolute_value=True).then_inc(hid_peak, 1)
            dve.wait_ge(hid_peak, NCH * FC)
            dve.tensor_reduce(peak[:, 2:3], peak_h[:], AX_X, ALU.max).then_inc(peaked, 1)
            scale_of(HID)
            dve.wait_ge(scaled, 4)
            link(dve.tensor_tensor(out_scale[:, 1:2], scale[:, W2:W2 + 1], scale[:, HID:HID + 1], ALU.mult))
            link(dve.tensor_scalar(b2s[:], b2[:], out_scale[:TT, 1:2], None, ALU.mult))
            link(dve.tensor_tensor(h[:], h[:], b2s[:].unsqueeze(1).to_broadcast([TT, NTILES, D]), ALU.add))
            with dve.Fori(0, NCH // 2) as c2:
                for par in range(2):
                    dve.wait_ge(q_shift, c2 * 2 + par + 1)
                    dve.wait_ge(down_mm, FIRST + c2 * 8)
                    dve.tensor_scalar(qh[:, par], hid[:, :, bass.ds(c2 * (2 * CN) + par * CN, CN)], -ROUND, None, ALU.add)\
                       .then_inc(q_ready, 1)
                for par in range(2):
                    for i in range(CT):
                        tile = c2 * 8 + (par * CT + i)
                        dve.wait_ge(down_mm, FIRST + c2 * 8 + (par * CT + i + 1))
                        dve.scalar_tensor_tensor(h[:, tile, :], ps[:TT, 4 * par + i, 0:D], out_scale[:TT, 1:2],
                                                 h[:, tile, :], ALU.mult, ALU.add).then_inc(added, 1)
            dve.wait_ge(added, FIRST + NTILES)


def audio_tower(nc, io, out):
    with ExitStack() as stack:
        keep = Memory(nc, stack)
        h = keep.sb("h", [TT, NTILES, D], F32)
        ident = keep.sb("ident", [P, P], F32)
        identb = keep.sb("identb", [P, P], BF16)
        ready = keep.sem("const_ready")
        stored = keep.sem("stored")
        with nc.Block() as block:
            @block.gpsimd
            def _(pool):
                for k, t in enumerate((ident, identb)):
                    pool.memset(t[:], 0.0).then_inc(ready, 1)
                    pool.wait_ge(ready, 2 * k + 1)
                    pool.affine_select(out=t[:], in_=t[:], compare_op=ALU.not_equal, fill=1.0, base=0,
                                       pattern=[[-1, P]], channel_multiplier=1).then_inc(ready, 1)
                pool.wait_ge(ready, 4)
        route = keep.sb("route", [TT, NTILES, E_N], F32)
        scratch = {name: nc.dram_tensor(f"scratch_{name}", (2, P, KC, B * T), F32, kind="Internal").ap()
                   for name in ("uT", "hdT")}
        scratch["parts"] = nc.dram_tensor("scratch_parts", (2, 3, D, T), BF16, kind="Internal").ap()
        stage_tok_attn(nc, keep, io, h, ident, identb)
        stage_heads(nc, keep, io, h, ident, identb, False, route, scratch)
        stage_experts(nc, keep, io, h, route, scratch)
        stage_heads(nc, keep, io, h, ident, identb, True, None, scratch)
        stage_quantised(nc, keep, io, h, ident)
        with nc.Block() as block:
            @block.sync
            def _(sp):
                sp.dma_start(out.rearrange("b (i p) d -> p (b i) d", p=TT), h[:].rearrange("p (b i) d -> p (b i) d", b=B))\
                  .then_inc(stored, 16)
                sp.wait_ge(stored, 16)


def shape_constants():
    pos = np.arange(T, dtype=np.float32)
    theta = np.power(np.float32(10000.0), (np.float32(-2.0) * np.arange(D // 2, dtype=np.float32) / np.float32(D))
                     .astype(np.float32)).astype(np.float32)
    ang = (theta[:, None] * pos[None, :]).astype(np.float32)
    bf = mybir.dt.np(BF16)
    p, o = np.arange(TT)[:, None], np.arange(2 * TT)[None, :]
    freq = (np.float32(1.0) / np.power(np.float32(10000.0), np.arange(HD // 2, dtype=np.float32) / np.float32(HD // 2)))
    ang_h = (np.tile(freq.astype(np.float32), H)[:, None] * pos[None, :]).astype(np.float32)
    ow = np.arange(2 * TT + 2)[None, :]
    oc = np.arange(TT)[None, :]
    return {
        "cos_heads": np.cos(ang_h).astype(np.float32),
        "sin_heads": np.sin(ang_h).astype(np.float32),
        "mask_causal_q": np.where(oc <= p, 0.0, NEG).astype(bf),
        "mask_causal_k": np.where(oc >= p, 0.0, NEG).astype(bf),
        "mask_window_q": np.where((ow >= p) & (ow <= p + WINDOW - 1), 0.0, NEG).astype(bf),
        "mask_window_k": np.where((ow >= p) & (ow <= p + WINDOW - 1), 0.0, NEG).astype(bf),
        "expert_iota": np.tile(np.arange(E_N, dtype=np.float32), (TT, 1)),
        "cos_one": np.cos(ang).astype(np.float32),
        "sin_one": np.sin(ang).astype(np.float32),
        "mask_next": np.where(o <= p + 1, 0.0, NEG).astype(bf),
        "minus_half": np.full((TT, NT), -0.5, np.float32),
    }


_OUT = ("out_0_dram", (B, T, D), "float32")


def kernel(**inputs):
    import numpy as _np
    import concourse.bacc as _bacc
    from concourse import mybir as _mybir
    from concourse.bass_utils import run_bass_kernel_spmd as _run

    nc = _bacc.Bacc("TRN2", target_bir_lowering=False, num_devices=1)
    arrays, io = {}, {}
    for name, a in (dict(inputs) | shape_constants()).items():
        a = _np.ascontiguousarray(a)
        arrays[f"in_{name}_dram"] = a
        io[name] = nc.dram_tensor(f"in_{name}_dram", a.shape, _mybir.dt.from_np(a.dtype), kind="ExternalInput").ap()
    name, shape, dtype = _OUT
    out = nc.dram_tensor(name, shape, _mybir.dt.from_np(_np.dtype(dtype)), kind="ExternalOutput").ap()
    audio_tower(nc, io, out)
    r = _run(nc, [arrays], core_ids=[0])
    return r.results[0][name]
```

```python
from contextlib import ExitStack

import concourse.bass as bass
from concourse import mybir
import numpy as np

F32 = mybir.dt.float32
F32R = mybir.dt.float32r
BF16 = mybir.dt.bfloat16
U32 = mybir.dt.uint32
ACT = mybir.ActivationFunctionType
ALU = mybir.AluOpType
AX_X = mybir.AxisListType.X

P = 128
B, C_IN, T = 4, 128, 750
D, KC = 256, 2
TT, NT = 125, 6
NTILES = B * NT
BANK = 512
LN_EPS = 1e-5
FIRST = 1
SEGS = ((0, BANK), (BANK, T))
NEG = -1e30


class Count:

    def __init__(self, shared, name, per):
        self.shared, self.name, self.per, self.used = shared, name, per, False

    @property
    def sem(self):
        self.used = True
        return self.shared.get(self.name)

    def at(self, i, k=None):
        return i * self.per + (self.per if k is None else k) + self.shared.left.get(self.name, FIRST)


class SharedSemaphores:

    def __init__(self, nc, stack):
        self.nc, self.stack, self.held, self.left, self.started = nc, stack, {}, {}, set()

    def get(self, name):
        if name not in self.held:
            self.held[name] = self.stack.enter_context(self.nc.semaphore(name))
        return self.held[name]

    def start(self, pool, counts):
        for c in counts.values():
            if c.name not in self.started:
                self.started.add(c.name)
                pool.sem_inc(self.get(c.name), FIRST)

    def close(self, counts):
        for c in counts.values():
            if c.used:
                self.left[c.name] = self.left.get(c.name, FIRST) + B * c.per


class Memory:

    def __init__(self, nc, stack, keep=None):
        self.nc, self.stack, self.keep = nc, stack, keep.keep if keep else stack
        self.shared = keep.shared if keep else SharedSemaphores(nc, stack)

    def sb(self, name, shape, dt):
        return self.stack.enter_context(self.nc.sbuf_tensor(name, shape, dt))

    def ps(self, name, shape):
        return self.stack.enter_context(self.nc.psum_tensor(name, shape, F32))

    def sem(self, name):
        return self.keep.enter_context(self.nc.semaphore(name))

    def counts(self, **per):
        return {k: Count(self.shared, k, n) for k, n in per.items()}


def over(t0, t1, steps):
    return [(t0 + (t1 - t0) * (i + 0.5) / len(steps), s) for i, s in enumerate(steps)]


class Trips:

    def __init__(self, steps, length, units):
        def order(*batches):
            found = [(at + length * w, (name, w, args)) for at, (name, args) in steps for w in batches
                     if 0 <= at + length * w < length]
            out, place = [], 0
            for _, (name, w, args) in sorted(found, key=lambda x: x[0]):
                out.append((name, w, args, place))
                place += name in units
            return out, place

        assert all(-length <= at < 2 * length for at, _ in steps)
        self.before, n_before = order(1)
        self.first, n_first = order(0, 1)
        self.middle, self.per = order(-1, 0, 1)
        self.last, n_last = order(-1, 0)
        self.after, n_after = order(-1)
        self.at_1 = n_before + n_first - self.per
        self.starts = {-1: 0, 0: n_before, B - 1: self.at_1 + (B - 1) * self.per, B: B * self.per - n_after}
        assert self.starts[B - 1] + n_last == self.starts[B]

    def number(self, t, place):
        return (0, self.starts[t] + place) if isinstance(t, int) else (t, self.at_1 + place)

    def run(self, eng, step):
        for t, steps in ((-1, self.before), (0, self.first)):
            for s in steps:
                step(t, *s)
        with eng.Fori(1, B - 1) as t:
            for s in self.middle:
                step(t, *s)
        for t, steps in ((B - 1, self.last), (B, self.after)):
            for s in steps:
                step(t, *s)


def count_at(c, name, t, which, k=None):
    n = c[name]
    return n.at(t, which * n.per + (n.per if k is None else k))


def tile_no(t, which, i):
    return t * NT + (which * NT + i)


def split3(eng, out, lhs, rhs, first=True, last=True):
    eng.matmul(out, lhs[0], rhs[0], start=first, stop=False)
    eng.matmul(out, lhs[0], rhs[1], start=False, stop=False)
    return eng.matmul(out, lhs[1], rhs[0], start=False, stop=last)


def stage_tok_attn(nc, keep, io, h, ident, identb):
    with ExitStack() as stack:
        m = Memory(nc, stack, keep)
        x_sb = m.sb("a_x", [P, B, T], F32)
        w_raw = m.sb("a_w_raw", [P, 3, KC, D], F32)
        wt_raw = m.sb("a_wt_raw", [P, KC, P], F32)
        tok_wT = m.sb("a_tok_wT", [P, D], F32)
        bias = m.sb("a_bias", [TT, 2, D], F32)
        w_hi = m.sb("a_w_hi", [P, 3, KC, D], F32R)
        w_lo = m.sb("a_w_lo", [P, 3, KC, D], F32R)
        cos = m.sb("a_cos", [P, T], F32)
        sin = m.sb("a_sin", [P, T], F32)
        mask = m.sb("a_mask", [TT, 2 * TT], BF16)
        decay = m.sb("a_decay", [P, T], F32)
        xs = m.sb("a_xs", [P, T], F32)
        fwd = m.sb("a_fwd", [P, T], F32)
        bwd = m.sb("a_bwd", [P, T], F32)
        ew = m.sb("a_ew", [P, T], F32)
        stats = m.sb("a_stats", [TT, NT, 6], F32)
        waiter = m.sb("a_waiter", [TT, 1], F32)
        mv = m.sb("a_mv", [TT, NT, 2], F32)
        rstd = m.sb("a_rstd", [TT, NT], F32)
        half = m.sb("a_half", [TT, NT], F32)
        u = m.sb("a_u", [TT, NT, D], F32)
        uT_hi = m.sb("a_uT_hi", [P, KC, T], F32R)
        uT_lo = m.sb("a_uT_lo", [P, KC, T], F32R)
        prod = m.sb("a_prod", [P, 4, T], F32)
        rot = m.sb("a_rot", [P, 2, KC, T], F32)
        qk_hi = m.sb("a_qk_hi", [P, 2, KC, T], F32R)
        qk_lo = m.sb("a_qk_lo", [P, 2, KC, T], F32R)
        v_hi = m.sb("a_v_hi", [TT, NT, D], F32R)
        v_lo = m.sb("a_v_lo", [TT, NT, D], F32R)
        neg_max = m.sb("a_neg_max", [TT, NT], F32)
        denom = m.sb("a_denom", [TT, NT], F32)
        rden = m.sb("a_rden", [TT, NT], F32)
        probs = m.sb("a_probs", [TT, 2, T], F32)
        pT_hi = m.sb("a_pT_hi", [TT, 2, NT, TT], F32R)
        pT_lo = m.sb("a_pT_lo", [TT, 2, NT, TT], F32R)
        ps = m.ps("a_ps", [P, 8, BANK])

        HALF = T // 2 + T // 2 % 2
        HALVES = ((0, HALF), (HALF, T))
        UT = ((0, 2), (2, 4), (4, 5), (5, 6))
        EMA_AT, TOK_AT, NORM_AT, UT_AT, QK_AT, QK_BY, CUT_AT, CUT_BY = 0.268, 0.4, 1.196, 1.4, 1.9, 5.116, 5.003, 5.6
        TURN_AT, WEIGH_AT, V_BY = 1.367, 2.091, 1.8

        load = m.sem("a_load")
        set_wT = m.sem("a_set_wT")
        set_hi = m.sem("a_set_hi")
        set_lo = m.sem("a_set_lo")
        set_scale = m.sem("a_set_scale")
        set_const = m.sem("a_set_const")
        steps = [(EMA_AT - NT, ("ema", ())), (NORM_AT - NT, ("norm", ()))]
        steps += over(TOK_AT - NT, NORM_AT - NT - 0.01, [("tok", (g,)) for g in range(3)])
        steps += over(UT_AT - NT, QK_AT - NT, [("uT", (g,)) for g in range(len(UT))])
        steps += over(QK_AT - NT, QK_BY - NT, [("qk", (n, ec, s)) for n in range(2) for s in range(2) for ec in range(KC)])
        steps += [(QK_BY - NT, ("rotate", ()))] + over(CUT_AT - NT, CUT_BY - NT, [("cut", (s, n)) for s in range(2) for n in range(2)])
        steps += over(5 + WEIGH_AT - NT + 0.01, V_BY, [("v", (g,)) for g in range(3)])
        for i in range(NT):
            steps += [(i, ("scores", (i,))), (i + TURN_AT, ("turn", (i,))), (i + WEIGH_AT, ("weigh", (i,)))]
        trips = Trips(steps, NT, {"tok", "uT", "qk", "v", "weigh"})
        assert trips.per % 2 == 0
        c = m.counts(xs=1, scan=2, ew=1, h=3, stats=6, mv=6, ve=1, rstd=1, u=6, uT_hi=4, uT_lo=4, rope_mul=16,
                     rope_sum=4, qk_hi=4, qk_lo=4, v_hi=3, v_lo=3, unit_mm=trips.per,
                     free0=trips.per // 2, free1=trips.per // 2, s_mm=6,
                     neg_max=6, exp=6, pT_mm=6, pT_hi=6, pT_lo=6, rden=6, h_upd=6)

        def at(name, t, which, k=None):
            return count_at(c, name, t, which, k)

        def unit_done(t, p):
            trip, units = trips.number(t, p)
            return c["unit_mm"].at(trip, units + 1)

        def bank_of(t, p):
            return 6 + trips.number(t, p)[1] % 2

        def free_sem(t, p):
            return c[f"free{bank_of(t, p) - 6}"].sem

        def flat(bank):
            return ps[:, bank:bank + 2, :].rearrange("p b n -> p (b n)")

        def width(i):
            return min(T, (i + 2) * TT)

        block = stack.enter_context(nc.Block())
        loads = 16 * 11

        @block.sync
        def _(sp):
            sp.dma_start(wt_raw[:], io["L0_tok_W"].rearrange("(c p) d -> p c d", p=P)).then_inc(load, 16)
            sp.dma_start(x_sb[:], io["x"].rearrange("b c t -> c b t")).then_inc(load, 16)
            for n, name in enumerate(("L0_attn_Wq", "L0_attn_Wk")):
                sp.dma_start(w_raw[:, n], io[name].rearrange("(p c) d -> p c d", c=KC)).then_inc(load, 16)
            sp.dma_start(w_raw[:, 2], io["L0_attn_Wv"].rearrange("(c p) d -> p c d", p=P)).then_inc(load, 16)
            for k in range(2):
                sp.dma_start(bias[:, k], io["L0_tok_b"].rearrange("(a d) -> a d", a=1).to_broadcast([TT, D]))\
                  .then_inc(load, 16)
            sp.dma_start(cos[:], io["cos_one"]).then_inc(load, 16)
            sp.dma_start(sin[:], io["sin_one"]).then_inc(load, 16)
            sp.dma_start(mask[:], io["mask_next"]).then_inc(load, 16)
            sp.dma_start(half[:], io["minus_half"]).then_inc(load, 16)

        @block.tensor
        def _(pe):
            pe.wait_ge(load, loads)
            for ec in range(KC):
                mm = pe.transpose(ps[:, 0, ec * P:(ec + 1) * P], wt_raw[:, ec, :], ident[:])
            mm.then_inc(set_wT, 1)
            pe.wait_ge(set_scale, 1)
            for n in range(3):
                for kc in range(KC):
                    for ec in range(KC):
                        mm = pe.transpose(ps[:, 1 + n, (kc * KC + ec) * P:(kc * KC + ec + 1) * P],
                                          w_raw[:, n, ec, kc * P:(kc + 1) * P], ident[:])
                mm.then_inc(set_wT, 1)
            pe.wait_ge(set_lo, 3)
            def side(t, p):
                trip, units = trips.number(t, p)
                pe.wait_ge(free_sem(t, p), c[f"free{units % 2}"].at(trip, units // 2))
                return 6 + units % 2

            def step(t, kind, which, args, p):
                if kind == "tok":
                    (g,) = args
                    pe.wait_ge(c["ew"].sem, at("ew", t, which))
                    bank = side(t, p)
                    for i in (2 * g, 2 * g + 1):
                        mm = pe.matmul(ps[:TT, bank, (i % 2) * D:(i % 2 + 1) * D], ew[:, i * TT:(i + 1) * TT],
                                       tok_wT[:], start=True, stop=True)
                    mm.then_inc(c["unit_mm"].sem, 1)
                elif kind == "uT":
                    t0, t1 = UT[args[0]]
                    pe.wait_ge(c["u"].sem, at("u", t, which, t1))
                    bank = side(t, p)
                    for kc in range(KC):
                        for i in range(t0, t1):
                            col = (kc * (t1 - t0) + i - t0) * TT
                            mm = pe.transpose(ps[:, bank, col:col + TT], u[:, i, kc * P:(kc + 1) * P],
                                              ident[:TT, :TT])
                    mm.then_inc(c["unit_mm"].sem, 1)
                elif kind == "qk":
                    n, ec, s = args
                    s0, s1 = HALVES[s]
                    pe.wait_ge(c["uT_lo"].sem, at("uT_lo", t, which))
                    bank = side(t, p)
                    for kc in range(KC):
                        mm = split3(pe, ps[:, bank, 0:s1 - s0], [w[:, n, kc, ec * P:(ec + 1) * P] for w in (w_hi, w_lo)],
                                    [x[:, kc, s0:s1] for x in (uT_hi, uT_lo)], kc == 0, kc == KC - 1)
                    mm.then_inc(c["unit_mm"].sem, 1)
                elif kind == "v":
                    (g,) = args
                    bank = side(t, p)
                    for i in (2 * g, 2 * g + 1):
                        for kc in range(KC):
                            mm = split3(pe, ps[:TT, bank, (i % 2) * D:(i % 2 + 1) * D],
                                        [x[:, kc, i * TT:(i + 1) * TT] for x in (uT_hi, uT_lo)],
                                        [w[:, 2, kc, :] for w in (w_hi, w_lo)], kc == 0, kc == KC - 1)
                    mm.then_inc(c["unit_mm"].sem, 1)
                elif kind == "scores":
                    (i,) = args
                    pe.wait_ge(c["qk_lo"].sem, at("qk_lo", t, which, 2 if width(i) < HALF else 4))
                    if i >= 2 or not (isinstance(t, int) and t == 0):
                        pe.wait_ge(c["exp"].sem, at("exp", t, which, i - 1))
                    out = flat(2 * (i % 2))
                    for s0 in range(0, width(i), BANK):
                        s1 = min(s0 + BANK, width(i))
                        s2 = s1 + (s1 - s0) % 2
                        for kc in range(KC):
                            mm = split3(pe, out[:TT, s0:s2], [x[:, 0, kc, i * TT:(i + 1) * TT] for x in (qk_hi, qk_lo)],
                                        [x[:, 1, kc, s0:s2] for x in (qk_hi, qk_lo)], kc == 0, kc == KC - 1)
                            m0 = max(s0, i * TT)
                            if kc == 0 and m0 < s1:
                                pe.matmul(out[:TT, m0:s1], identb[:TT, :TT], mask[:, m0 - i * TT:s1 - i * TT],
                                          start=False, stop=False)
                    mm.then_inc(c["s_mm"].sem, 1)
                elif kind == "turn":
                    (i,) = args
                    pe.wait_ge(c["exp"].sem, at("exp", t, which, i + 1))
                    pe.wait_ge(c["pT_lo"].sem, at("pT_lo", t, which, i))
                    for j in range(width(i) // TT):
                        mm = pe.transpose(ps[:TT, 4 + j // 4, (j % 4) * P:(j % 4) * P + TT],
                                          probs[:, i % 2, j * TT:(j + 1) * TT], ident[:TT, :TT])
                    mm.then_inc(c["pT_mm"].sem, 1)
                elif kind == "weigh":
                    (i,) = args
                    n = width(i) // TT
                    pe.wait_ge(c["pT_lo"].sem, at("pT_lo", t, which, i + 1))
                    pe.wait_ge(c["v_lo"].sem, at("v_lo", t, which, (n + 1) // 2))
                    bank = side(t, p)
                    for j in range(n):
                        mm = split3(pe, ps[:TT, bank, 0:D], [x[:, i % 2, j, :] for x in (pT_hi, pT_lo)],
                                    [x[:, j, :] for x in (v_hi, v_lo)], j == 0, j == n - 1)
                    mm.then_inc(c["unit_mm"].sem, 1)

            trips.run(pe, step)

        @block.scalar
        def _(act):
            for n in range(3):
                act.wait_ge(set_wT, n + 2)
                act.activation(w_hi[:, n].rearrange("p k e -> p (k e)"), ps[:, 1 + n, :], ACT.Copy)\
                   .then_inc(set_hi, 1)
            def step(t, kind, which, args, p):
                bank = bank_of(t, p)
                if kind == "uT":
                    t0, t1 = UT[args[0]]
                    act.wait_ge(c["unit_mm"].sem, unit_done(t, p))
                    act.activation(uT_hi[:, :, t0 * TT:t1 * TT],
                                   ps[:, bank, 0:KC * (t1 - t0) * TT].rearrange("p (k q) -> p k q", k=KC), ACT.Copy)\
                       .then_inc(c["uT_hi"].sem, 1)
                elif kind == "cut":
                    s, n = args
                    s0, s1 = HALVES[s]
                    act.wait_ge(c["rope_sum"].sem, at("rope_sum", t, which, 2 * n + 2))
                    if s == 0 and n == 0:
                        act.wait_ge(c["s_mm"].sem, at("s_mm", t, which, 0))
                    act.activation(qk_hi[:, n, :, s0:s1], rot[:, n, :, s0:s1], ACT.Copy).then_inc(c["qk_hi"].sem, 1)
                elif kind == "v":
                    (g,) = args
                    act.wait_ge(c["unit_mm"].sem, unit_done(t, p))
                    act.activation(v_hi[:, 2 * g:2 * g + 2, :].rearrange("p i d -> p (i d)"), ps[:TT, bank, :], ACT.Copy)\
                       .then_inc(c["v_hi"].sem, 1)
                elif kind == "scores":
                    (i,) = args
                    act.wait_ge(c["neg_max"].sem, at("neg_max", t, which, i + 1))
                    if i >= 2 or not (isinstance(t, int) and t == 0):
                        act.wait_ge(c["pT_mm"].sem, at("pT_mm", t, which, i - 1))
                    act.activation(probs[:, i % 2, 0:width(i)], flat(2 * (i % 2))[:TT, 0:width(i)], ACT.Exp,
                                   bias=neg_max[:, i:i + 1], accum_out=denom[:, i:i + 1]).then_inc(c["exp"].sem, 1)
                elif kind == "turn":
                    (i,) = args
                    act.wait_ge(c["pT_mm"].sem, at("pT_mm", t, which, i + 1))
                    if i >= 2 or not (isinstance(t, int) and t == 0):
                        act.wait_ge(c["h_upd"].sem, at("h_upd", t, which, i - 1))
                    n = width(i) // TT
                    act.activation(pT_hi[:, i % 2, 0:n, :],
                                   flat(4).rearrange("p (j q) -> p j q", q=P)[:TT, 0:n, 0:TT], ACT.Copy)\
                       .then_inc(c["pT_hi"].sem, 1)

            trips.run(act, step)

        @block.gpsimd
        def _(pool):
            keep.shared.start(pool, c)
            pool.memset(decay[:], 0.9).then_inc(set_const, 1)
            pool.wait_ge(load, loads)
            pool.tensor_scalar(w_raw[:, 0], w_raw[:, 0], float(D) ** -0.5, None, ALU.mult).then_inc(set_scale, 1)
            def step(t, kind, which, args, p):
                if kind == "norm":
                    pool.wait_ge(c["ve"].sem, at("ve", t, which))
                    pool.tensor_tensor(rstd[:], rstd[:], half[:], ALU.pow).then_inc(c["rstd"].sem, 1)
                elif kind == "rotate":
                    for n in range(2):
                        pool.wait_ge(c["rope_mul"].sem, at("rope_mul", t, which, 8 * n + 8))
                        if n == 0:
                            pool.wait_ge(c["qk_lo"].sem, at("qk_lo", t, which, 0))
                        pool.tensor_tensor(rot[:, n, 0], prod[:, 0], prod[:, 1], ALU.subtract)\
                            .then_inc(c["rope_sum"].sem, 1)
                        pool.tensor_tensor(rot[:, n, 1], prod[:, 2], prod[:, 3], ALU.add)\
                            .then_inc(c["rope_sum"].sem, 1)

            trips.run(pool, step)

        @block.vector
        def _(dve):
            dve.wait_ge(set_wT, 1)
            dve.tensor_scalar(tok_wT[:], ps[:, 0, 0:D], 0.5, None, ALU.mult)
            for n in range(3):
                dve.wait_ge(set_hi, n + 1)
                dve.tensor_tensor(w_lo[:, n].rearrange("p k e -> p (k e)"), ps[:, 1 + n, :],
                                  w_hi[:, n].bitcast(F32).rearrange("p k e -> p (k e)"), ALU.subtract)\
                   .then_inc(set_lo, 1)
            dve.wait_ge(set_const, 1)
            def step(t, kind, which, args, p):
                bank = bank_of(t, p)
                if kind in ("tok", "uT", "qk", "v", "weigh"):
                    dve.wait_ge(c["unit_mm"].sem, unit_done(t, p))
                if kind == "ema":
                    rows = x_sb[:, t + which, :]
                    dve.tensor_scalar(xs[:], rows, 0.1, None, ALU.mult).then_inc(c["xs"].sem, 1)
                    dve.wait_ge(c["xs"].sem, at("xs", t, which))
                    dve.tensor_tensor_scan(fwd[:], decay[:], xs[:], x_sb[:, t + which, 0:1], ALU.mult, ALU.add)\
                       .then_inc(c["scan"].sem, 1)
                    dve.tensor_tensor_scan(bwd[:, ::-1], decay[:], xs[:, ::-1], x_sb[:, t + which, T - 1:T], ALU.mult,
                                           ALU.add).then_inc(c["scan"].sem, 1)
                    dve.wait_ge(c["scan"].sem, at("scan", t, which))
                    dve.tensor_tensor(ew[:], fwd[:], bwd[:], ALU.add).then_inc(c["ew"].sem, 1)
                elif kind == "tok":
                    (g,) = args
                    dve.tensor_tensor(h[:, bass.ds(tile_no(t, which, 2 * g), 2), :],
                                      ps[:TT, bank, :].rearrange("p (i d) -> p i d", d=D), bias[:], ALU.add)\
                       .then_inc(c["h"].sem, 1)
                    dve.wait_ge(c["h"].sem, at("h", t, which, g + 1))
                    dve.memset(waiter[:], 0.0).then_inc(free_sem(t, p), 1)
                    for i in (2 * g, 2 * g + 1):
                        dve.bn_stats(stats[:, i], h[:, tile_no(t, which, i), :]).then_inc(c["stats"].sem, 1)
                elif kind == "norm":
                    dve.wait_ge(c["stats"].sem, at("stats", t, which))
                    dve.memset(waiter[:], 0.0)
                    for i in range(NT):
                        dve.bn_aggr(mv[:, i], stats[:, i]).then_inc(c["mv"].sem, 1)
                    dve.wait_ge(c["mv"].sem, at("mv", t, which))
                    dve.tensor_scalar(rstd[:], mv[:, :, 1], LN_EPS, None, ALU.add).then_inc(c["ve"].sem, 1)
                    dve.wait_ge(c["rstd"].sem, at("rstd", t, which))
                    for i in range(NT):
                        dve.tensor_scalar(u[:, i], h[:, tile_no(t, which, i), :], mv[:, i, 0:1], rstd[:, i:i + 1],
                                          ALU.subtract, ALU.mult).then_inc(c["u"].sem, 1)
                elif kind == "uT":
                    (g,) = args
                    t0, t1 = UT[g]
                    cols = slice(t0 * TT, t1 * TT)
                    dve.wait_ge(c["uT_hi"].sem, at("uT_hi", t, which, g + 1))
                    dve.tensor_tensor(uT_lo[:, :, cols],
                                      ps[:, bank, 0:KC * (t1 - t0) * TT].rearrange("p (k q) -> p k q", k=KC),
                                      uT_hi[:, :, cols].bitcast(F32), ALU.subtract).then_inc(c["uT_lo"].sem, 1)
                    dve.wait_ge(c["uT_lo"].sem, at("uT_lo", t, which, g + 1))
                    dve.sem_inc(free_sem(t, p), 1)
                elif kind == "qk":
                    n, ec, s = args
                    s0, s1 = HALVES[s]
                    if (ec, s) == (0, 0):
                        dve.wait_ge(c["rope_sum"].sem, at("rope_sum", t, which, 2 * n))
                    for k, table in (((0, cos), (2, sin)), ((1, sin), (3, cos)))[ec]:
                        dve.tensor_tensor(prod[:, k, s0:s1], ps[:, bank, 0:s1 - s0], table[:, s0:s1], ALU.mult)\
                           .then_inc(c["rope_mul"].sem, 1)
                    dve.wait_ge(c["rope_mul"].sem, at("rope_mul", t, which, 8 * n + 4 * s + 2 * ec + 2))
                    dve.sem_inc(free_sem(t, p), 1)
                elif kind == "cut":
                    s, n = args
                    s0, s1 = HALVES[s]
                    dve.wait_ge(c["qk_hi"].sem, at("qk_hi", t, which, 2 * s + n + 1))
                    dve.tensor_tensor(qk_lo[:, n, :, s0:s1], rot[:, n, :, s0:s1], qk_hi[:, n, :, s0:s1].bitcast(F32),
                                      ALU.subtract).then_inc(c["qk_lo"].sem, 1)
                elif kind == "v":
                    (g,) = args
                    dve.wait_ge(c["v_hi"].sem, at("v_hi", t, which, g + 1))
                    dve.tensor_tensor(v_lo[:, 2 * g:2 * g + 2, :].rearrange("p i d -> p (i d)"), ps[:TT, bank, :],
                                      v_hi[:, 2 * g:2 * g + 2, :].bitcast(F32).rearrange("p i d -> p (i d)"),
                                      ALU.subtract).then_inc(c["v_lo"].sem, 1)
                    dve.wait_ge(c["v_lo"].sem, at("v_lo", t, which, g + 1))
                    dve.sem_inc(free_sem(t, p), 1)
                elif kind == "scores":
                    (i,) = args
                    dve.wait_ge(c["s_mm"].sem, at("s_mm", t, which, i + 1))
                    dve.tensor_reduce(neg_max[:, i:i + 1], flat(2 * (i % 2))[:TT, 0:width(i)], AX_X, ALU.max,
                                      negate=True).then_inc(c["neg_max"].sem, 1)
                elif kind == "turn":
                    (i,) = args
                    dve.wait_ge(c["pT_hi"].sem, at("pT_hi", t, which, i + 1))
                    n = width(i) // TT
                    dve.tensor_tensor(pT_lo[:, i % 2, 0:n, :],
                                      flat(4).rearrange("p (j q) -> p j q", q=P)[:TT, 0:n, 0:TT],
                                      pT_hi[:, i % 2, 0:n, :].bitcast(F32), ALU.subtract)\
                       .then_inc(c["pT_lo"].sem, 1)
                    dve.reciprocal(rden[:, i:i + 1], denom[:, i:i + 1]).then_inc(c["rden"].sem, 1)
                elif kind == "weigh":
                    (i,) = args
                    tile = tile_no(t, which, i)
                    dve.wait_ge(c["rden"].sem, at("rden", t, which, i + 1))
                    dve.scalar_tensor_tensor(h[:, tile, :], ps[:TT, bank, 0:D], rden[:, i:i + 1], h[:, tile, :],
                                             ALU.mult, ALU.add).then_inc(c["h_upd"].sem, 1)
                    dve.wait_ge(c["h_upd"].sem, at("h_upd", t, which, i + 1))
                    dve.sem_inc(free_sem(t, p), 1)

            trips.run(dve, step)
            dve.wait_ge(c["h_upd"].sem, c["h_upd"].at(B - 1))
        keep.shared.close(c)


H, HD = 16, 16
HG = 4
GROUPS = H // HG
SLOTS = ((0, 0), (0, 1), (1, 0), (1, 1), (0, 2), (2, 0))
STACK = len(SLOTS) * HD
ROWS = STACK + 3
E_N = 8
WINDOW = 128


def stage_heads(nc, keep, io, h, ident, identb, local, route=None, scratch=None):
    L = "d" if local else "b"
    with ExitStack() as stack:
        m = Memory(nc, stack, keep)
        w_hi = m.sb(f"{L}_w_hi", [P, 3, KC, D], F32R)
        w_lo = m.sb(f"{L}_w_lo", [P, 3, KC, D], F32R)
        wo = m.sb(f"{L}_wo", [P, KC, D], F32)
        mask_w = 2 * TT + 2 if local else TT
        mask_q = m.sb(f"{L}_mask_q", [TT, mask_w], BF16)
        mask_k = m.sb(f"{L}_mask_k", [TT, mask_w], BF16)
        half = m.sb(f"{L}_half", [TT, NT], F32)
        stats = m.sb(f"{L}_stats", [TT, NT, 6], F32)
        waiter = m.sb(f"{L}_waiter", [TT, 1], F32)
        mv = m.sb(f"{L}_mv", [TT, NT, 2], F32)
        rstd = m.sb(f"{L}_rstd", [TT, NT], F32)
        u = m.sb(f"{L}_u", [TT, NT, D], F32)
        uT_hi = m.sb(f"{L}_uT_hi", [P, KC, T], F32R)
        uT_lo = m.sb(f"{L}_uT_lo", [P, KC, T], F32R)
        part = [m.sb(f"{L}_part{k}", [P, 2, KC, T], BF16) for k in range(3)]
        rest = m.sb(f"{L}_rest", [P, KC, T], F32)
        q_st = m.sb(f"{L}_q_st", [ROWS, H, T], BF16)
        k_st = m.sb(f"{L}_k_st", [ROWS, H, T], BF16)
        v_ext = m.sb(f"{L}_v_ext", [TT, NT, H, 2 * HD], F32)
        neg = m.sb(f"{L}_neg", [TT, NT, H], F32)
        neg_b = m.sb(f"{L}_neg_b", [TT, 2, H], F32)
        neg_part = m.sb(f"{L}_neg_part", [TT, NT, 3, HG], BF16)
        neg_rest = m.sb(f"{L}_neg_rest", [TT, NT, HG], F32)
        negT = m.sb(f"{L}_negT", [3 * HG, T], BF16)
        pw = 2 * TT + 2 if local else T
        probs = m.sb(f"{L}_probs", [TT, 2, HG, pw], F32)
        pv_sb = m.sb(f"{L}_pv_sb", [P, GROUPS, T], F32)
        rden = m.sb(f"{L}_rden", [TT, NT, H], F32)
        o_full = m.sb(f"{L}_o", [P, NT, D], F32)
        o = o_full[:TT]
        oT = m.sb(f"{L}_oT", [P, 2, KC, TT], F32)
        ps = m.ps(f"{L}_ps", [P, 8, BANK])
        if local:
            prod = m.sb(f"{L}_prod", [P, 4, T], F32)
            rot = m.sb(f"{L}_rot", [P, KC, T], F32)
            cos = m.sb(f"{L}_cos", [P, T], F32)
            sin = m.sb(f"{L}_sin", [P, T], F32)
        else:
            r_raw = m.sb("b_r_raw", [P, KC, E_N], F32)
            r_hi = m.sb("b_r_hi", [P, KC, E_N], F32R)
            r_lo = m.sb("b_r_lo", [P, KC, E_N], F32R)
            norm_w = m.sb("b_norm_w", [TT, D], F32)
            junk = m.sb("b_junk", [TT, D], F32)
            ss = m.sb("b_ss", [TT, NT], F32)
            rms = m.sb("b_rms", [TT, NT], F32)
            hd = o
            u_kept = m.sb("b_u_kept", [TT, NT, D], F32)
            hdT_hi = m.sb("b_hdT_hi", [P, 3, KC, TT], F32R)
            hdT_lo = m.sb("b_hdT_lo", [P, 3, KC, TT], F32R)
            r_max = m.sb("b_r_max", [TT, NT], F32)
            r_sum = m.sb("b_r_sum", [TT, NT], F32)
            r_inv = m.sb("b_r_inv", [TT, NT], F32)
            r_sub = m.sb("b_r_sub", [TT, NT, E_N], F32)
            r_exp = m.sb("b_r_exp", [TT, NT, E_N], F32)
            r_prob = m.sb("b_r_prob", [TT, NT, E_N], F32)
            top_v = m.sb("b_top_v", [TT, NT, E_N], F32)
            top_i = m.sb("b_top_i", [TT, NT, E_N], U32)
            top_f = m.sb("b_top_f", [TT, NT, E_N], F32)
            pick = m.sb("b_pick", [TT, 2, NT, E_N], F32)
            iota = m.sb("b_iota", [TT, E_N], F32)

        def flat(bank, n=2):
            return ps[:, bank:bank + n, :].rearrange("p b n -> p (b n)")

        firsts = []
        for i in range(NT):
            if local:
                k0 = max(0, i * TT - WINDOW + 1)
                segs = [(0, k0, (i + 1) * TT - k0, WINDOW - 1 - i * TT + k0)]
            elif i < 4:
                segs = [(0, 0, (i + 1) * TT, None)]
            else:
                segs = [(0, 0, 4 * TT, None), (1, 4 * TT, (i - 3) * TT, None)]
            for seg, k0, n, mc in segs:
                per = max(1, min(HG, BANK // n))
                for h0 in range(0, HG, per):
                    firsts.append((i, seg, h0, per, k0, n, mc))
        SEC_BANKS = 2
        seconds = []
        for j in range(NT):
            whole = min(pw, T - j * TT)
            for c0 in range(0, whole, BANK // TT * TT):
                n = min(BANK // TT * TT, whole - c0)
                nh = max(1, min(HG, BANK // n))
                for h0 in range(0, HG, nh):
                    seconds.append((j, h0, nh, n, c0))
        N_SEC = len(seconds)

        load = m.sem(f"{L}_load")
        set_w = m.sem(f"{L}_set_w")
        set_hi = m.sem(f"{L}_set_hi")
        set_const = m.sem(f"{L}_set_const")
        SIDE = (2, 3, 6, 7)
        NS = len(SIDE)
        UT = ((0, 2), (2, 4), (4, 6)) if local else ((0, 2), (2, 4), (4, 5), (5, 6))
        HALF = T // 2 + T // 2 % 2
        HALVES = ((0, HALF), (HALF, T))
        AHEAD, FIRSTS_BY, TURN_AT, MAX_IN_AT = (0.383, 0.673, 1.0, 1.148) if local else (0.219, 0.60, 0.783, 0.943)
        FRONT_AT, KEEP_AT, ROWS_OUT_BY, NORMED_BY = (0.0, -0.051, 1.42, 0.026) if local else (1.487, 1.469, 0.992, 1.337)

        def weigh_group(g):
            steps, at_col = [], 0
            for j in range(NT):
                for k, (jj, h0, nh, n, c0) in enumerate(seconds):
                    if jj == j:
                        steps.append((at_col, ("second", (g, k))))
                        at_col += nh * (n + TT)
                if j >= 1:
                    steps.append((at_col, ("weigh", (g, j - 1))))
                    at_col += HG * min(pw, T - (j - 1) * TT)
            steps.append((at_col, ("weigh", (g, NT - 1))))
            at_col += HG * TT
            return [(g + 0.999 * a / at_col, s) for a, s in steps] + [(g + 0.9995, ("weighed", (g,)))]

        rows_out = []
        for i in range(NT + 2):
            rows_out += [(name, (i - lag,)) for name, lag in (("back", 0), ("oT", 1), ("wo", 2)) if 0 <= i - lag < NT]
        steps_of_batch = []
        if not local:
            steps_of_batch += [(GROUPS + ROWS_OUT_BY, ("rms", ()))]
            steps_of_batch += over(GROUPS + ROWS_OUT_BY, GROUPS + NORMED_BY,
                                   [(name, (i,)) for name in ("hd", "hdT") for i in range(NT)])
            steps_of_batch += [(KEEP_AT - GROUPS + 0.001, ("keep", ()))]
        steps_of_batch += over(GROUPS, GROUPS + ROWS_OUT_BY, rows_out)
        steps_of_batch += [(FRONT_AT - GROUPS, ("norm", ()))]
        steps_of_batch += over(FRONT_AT + 0.14 - GROUPS, FRONT_AT + 0.30 - GROUPS, [("uT", (k,)) for k in range(len(UT))])
        for n in range(2):
            t0 = FRONT_AT + 0.36 - GROUPS + 0.35 * n
            steps_of_batch += over(t0, t0 + 0.30, [("qk", (n, ec, s)) for s in range(2) for ec in range(KC)])
            steps_of_batch += [(t0 + 0.33, ("cut", (n,)))]
        if not local:
            steps_of_batch += over(FRONT_AT + 1.1 - GROUPS, FRONT_AT + 1.2 - GROUPS, [("router", ()), ("route", ())])
        steps_of_batch += [(-4e-4 + 1e-4 * k, ("v", (k,))) for k in range(3)]
        for g in range(GROUPS):
            steps_of_batch += weigh_group(g)
            t0 = g - 1 - AHEAD
            steps_of_batch += over(t0, t0 + FIRSTS_BY, [("first", (g, k)) for k in range(len(firsts))])
            steps_of_batch += [(t0 + FIRSTS_BY, ("maxima", (g,)))]
            steps_of_batch += over(t0 + TURN_AT, t0 + TURN_AT + 0.04, [("turn", (g, k)) for k in range(2)])
            steps_of_batch += [(t0 + MAX_IN_AT, ("max_in", (g,)))]

        trips = Trips(steps_of_batch, GROUPS, {"uT", "qk", "router", "v", "first", "turn", "back", "oT", "wo", "hdT"})
        assert trips.per % NS == 0
        SPLITS = 1 if local else KC * 2
        LOADS = len(SLOTS) * (4 if local else 2)
        c = m.counts(stats=NT, mv=NT, ve=1, rstd=1, u=NT, uT_hi=len(UT), uT_lo=len(UT), rope_mul=16, rope_sum=4,
                     part0=2 * SPLITS, rest=2 * SPLITS, part1=2, part2=2, parts_out=96,
                     stacked0=16 * LOADS, stacked1=16 * LOADS, stacked2=16 * LOADS, stacked3=16 * LOADS, v=3,
                     unit_mm=trips.per, **{f'free{k}': trips.per // NS for k in range(NS)},
                     neg=GROUPS, neg_part=4 * GROUPS, negT=2 * GROUPS,
                     neg_in=48 * GROUPS, sec_mm=GROUPS * N_SEC, exp=GROUPS * N_SEC, pv_mm=GROUPS * NT, pv_sb=GROUPS,
                     rden=NT, o=NT, oT=NT, h=NT, r_max=1, r_sub=1, r_exp=1, r_sum=1, r_inv=1, r_prob=1, top_v=NT,
                     top_i=NT, top_f=1, pick=2 * NT, route=1, hd_raw=NT, ss=NT, rms_ve=1, rms=1, hd_t=NT,
                     hd=NT, hdT_hi=NT, hdT_lo=NT, uT_out=32, hdT_out0=64, hdT_out1=64, hdT_out2=64)

        def at(name, t, which, k=None):
            return count_at(c, name, t, which, k)

        def unit_done(t, p):
            trip, units = trips.number(t, p)
            return c["unit_mm"].at(trip, units + 1)

        def bank_of(t, p):
            return SIDE[trips.number(t, p)[1] % NS]

        def free_sem(t, p):
            return c[f"free{trips.number(t, p)[1] % NS}"].sem

        def second_out(x, unit):
            j, h0, nh, n, c0 = unit
            return ps[:TT, x % SEC_BANKS, 0:nh * n].rearrange("p (m n) -> p m n", n=n)

        with ExitStack() as inner:
            raw = pv_sb[:].rearrange("p g t -> p (g t)")[:, 0:3 * KC * D].rearrange("p (n k e) -> p n k e", n=3, k=KC)
            rawp = o_full[:].rearrange("p (n k) e -> p n k e", k=KC)
            names = ("L0_ffn_wq", "L0_ffn_wk", "L0_ffn_wv")
            block = inner.enter_context(nc.Block())
            n_loads = 16 * (9 if local else 10)

            @block.sync
            def _(sp):
                for n in range(3):
                    src = io["L1_attn_Wqkv"][:, n * D:(n + 1) * D] if local else io[names[n]]
                    sp.dma_start(raw[:, n], src.rearrange("(k p) e -> p k e", p=P)).then_inc(load, 16)
                src = io["L1_attn_Wout" if local else "L0_ffn_wo"]
                sp.dma_start(wo[:], src.rearrange("(k p) e -> p k e", p=P)).then_inc(load, 16)
                sp.dma_start(mask_q[:], io["mask_window_q" if local else "mask_causal_q"]).then_inc(load, 16)
                sp.dma_start(mask_k[:], io["mask_window_k" if local else "mask_causal_k"]).then_inc(load, 16)
                sp.dma_start(half[:], io["minus_half"]).then_inc(load, 16)
                if local:
                    sp.dma_start(cos[:], io["cos_heads"]).then_inc(load, 16)
                    sp.dma_start(sin[:], io["sin_heads"]).then_inc(load, 16)
                else:
                    sp.dma_start(r_raw[:], io["L0_ffn_router_w"].rearrange("(k p) e -> p k e", p=P)).then_inc(load, 16)
                    sp.dma_start(norm_w[:], io["L0_ffn_attn_norm_w"].rearrange("(a d) -> a d", a=1)
                                 .to_broadcast([TT, D])).then_inc(load, 16)
                    sp.dma_start(iota[:], io["expert_iota"]).then_inc(load, 16)
                sp.wait_ge(load, n_loads)

            @block.scalar
            def _(act):
                for n in range(3):
                    act.wait_ge(set_w, n + 1)
                    act.activation(w_hi[:, n], rawp[:, n], ACT.Copy).then_inc(set_hi, 1)
                if not local:
                    act.wait_ge(load, n_loads)
                    act.activation(r_hi[:], r_raw[:], ACT.Copy).then_inc(set_hi, 1)

            @block.vector
            def _(dve):
                dve.wait_ge(load, n_loads)
                for n in range(3):
                    for k in range(KC):
                        src, dst = raw[:, n, k], rawp[:, n, k]
                        if local and n < 2:
                            src = src.rearrange("p (h a f) -> p a h f", a=2, f=HD // 2)
                            dst = dst.rearrange("p (a h f) -> p a h f", a=2, f=HD // 2)
                        mm = dve.tensor_scalar(dst, src, float(HD) ** -0.5 if n == 0 else 1.0, None, ALU.mult)
                    mm.then_inc(set_w, 1)
                for n in range(3):
                    dve.wait_ge(set_hi, n + 1)
                    dve.tensor_tensor(w_lo[:, n], rawp[:, n], w_hi[:, n].bitcast(F32), ALU.subtract)
                if not local:
                    dve.wait_ge(set_hi, 4)
                    dve.tensor_tensor(r_lo[:], r_raw[:], r_hi[:].bitcast(F32), ALU.subtract)

        block = stack.enter_context(nc.Block())

        @block.sync
        def _(sp):
            def load_group(t, g):
                if not (isinstance(t, int) and t == -1):
                    sp.wait_ge(c["sec_mm"].sem, at("sec_mm", t, 0, (g + 1) * N_SEC))
                for n, dst in enumerate((q_st, k_st)):
                    for s, slot in enumerate(SLOTS):
                        src = scratch["parts"][n, slot[n]]
                        heads = slice(g * HG, (g + 1) * HG)
                        if local:
                            src = src.rearrange("(a h f) t -> a f h t", a=2, h=H)
                            for a in range(2):
                                r0 = s * HD + a * (HD // 2)
                                sp.dma_start(dst[r0:r0 + HD // 2, heads], src[a][:, heads])\
                                  .then_inc(c[f"stacked{g}"].sem, 16)
                        else:
                            src = src.rearrange("(h d) t -> d h t", d=HD)
                            sp.dma_start(dst[s * HD:(s + 1) * HD, heads], src[:, heads])\
                              .then_inc(c[f"stacked{g}"].sem, 16)

            def step(t, kind, which, args, p):
                if kind == "uT" and args[0] == len(UT) - 1 and not local:
                    sp.wait_ge(c["uT_lo"].sem, at("uT_lo", t, which))
                    for k, x in enumerate((uT_hi, uT_lo)):
                        sp.dma_start(scratch["uT"][k, :, :, bass.ds(t * T + which * T, T)], x[:].bitcast(F32))\
                          .then_inc(c["uT_out"].sem, 16)
                elif kind == "cut":
                    (n,) = args
                    if n == 0:
                        for g in range(GROUPS):
                            sp.wait_ge(c[f"stacked{g}"].sem, at(f"stacked{g}", t, which, 0))
                    for k in range(3):
                        full = (n + 1) * (SPLITS if k == 0 else 1)
                        sp.wait_ge(c[f"part{k}"].sem, at(f"part{k}", t, which, full))
                        sp.dma_start(scratch["parts"][n, k].rearrange("(c p) t -> p c t", p=P), part[k][:, n])\
                          .then_inc(c["parts_out"].sem, 16)
                    if n == 1:
                        sp.wait_ge(c["parts_out"].sem, at("parts_out", t, which))
                        for g in range(GROUPS if isinstance(t, int) and t == -1 else 2):
                            load_group(t, g)
                elif kind == "weighed" and args[0] >= 2 and not (isinstance(t, int) and t == B - 1):
                    load_group(t, args[0])
                elif kind == "hdT":
                    (i,) = args
                    sp.wait_ge(c["hdT_lo"].sem, at("hdT_lo", t, which, i + 1))
                    for k, x in enumerate((hdT_hi, hdT_lo)):
                        sp.dma_start(scratch["hdT"][k, :, :, bass.ds(t * T + (which * T + i * TT), TT)],
                                     x[:, i % 3].bitcast(F32)).then_inc(c[f"hdT_out{i % 3}"].sem, 16)

            trips.run(sp, step)
            if not local:
                sp.wait_ge(c["uT_out"].sem, c["uT_out"].at(B - 1))
                for k in range(3):
                    sp.wait_ge(c[f"hdT_out{k}"].sem, c[f"hdT_out{k}"].at(B - 1))

        @block.tensor
        def _(pe):
            def side(t, p):
                trip, units = trips.number(t, p)
                pe.wait_ge(free_sem(t, p), c[f"free{units % NS}"].at(trip, units // NS))
                return SIDE[units % NS]

            def step(t, kind, which, args, p):
                if kind == "uT":
                    t0, t1 = UT[args[0]]
                    pe.wait_ge(c["u"].sem, at("u", t, which, t1))
                    bank = side(t, p)
                    for kc in range(KC):
                        for i in range(t0, t1):
                            col = (kc * (t1 - t0) + i - t0) * TT
                            mm = pe.transpose(ps[:, bank, col:col + TT], u[:, i, kc * P:(kc + 1) * P],
                                              ident[:TT, :TT])
                    mm.then_inc(c["unit_mm"].sem, 1)
                elif kind == "qk":
                    n, ec, s = args
                    s0, s1 = HALVES[s]
                    pe.wait_ge(c["uT_lo"].sem, at("uT_lo", t, which))
                    bank = side(t, p)
                    for kc in range(KC):
                        mm = split3(pe, ps[:, bank, 0:s1 - s0], [w[:, n, kc, ec * P:(ec + 1) * P] for w in (w_hi, w_lo)],
                                    [x[:, kc, s0:s1] for x in (uT_hi, uT_lo)], kc == 0, kc == KC - 1)
                    mm.then_inc(c["unit_mm"].sem, 1)
                elif kind == "v":
                    bank = side(t, p)
                    for i in range(2):
                        cols = slice((2 * args[0] + i) * TT, (2 * args[0] + i + 1) * TT)
                        for kc in range(KC):
                            mm = split3(pe, ps[:TT, bank, i * D:(i + 1) * D], [x[:, kc, cols] for x in (uT_hi, uT_lo)],
                                        [w[:, 2, kc, :] for w in (w_hi, w_lo)], kc == 0, kc == KC - 1)
                    mm.then_inc(c["unit_mm"].sem, 1)
                elif kind == "router":
                    bank = side(t, p)
                    for i in range(NT):
                        for kc in range(KC):
                            mm = split3(pe, ps[:TT, bank, i * E_N:(i + 1) * E_N],
                                        [x[:, kc, i * TT:(i + 1) * TT] for x in (uT_hi, uT_lo)],
                                        [w[:, kc, :] for w in (r_hi, r_lo)], kc == 0, kc == KC - 1)
                    mm.then_inc(c["unit_mm"].sem, 1)
                elif kind == "first":
                    g, unit = args[0], firsts[args[1]]
                    i, seg, h0, per, k0, n, mc = unit
                    if args[1] == 0:
                        pe.wait_ge(c[f"stacked{g}"].sem, at(f"stacked{g}", t, which))
                    bank = side(t, p)
                    for k in range(per):
                        hh = g * HG + h0 + k
                        out = ps[:TT, bank, k * n:(k + 1) * n]
                        mm = pe.matmul(out, q_st[0:STACK, hh, i * TT:(i + 1) * TT], k_st[0:STACK, hh, k0:k0 + n],
                                       start=True, stop=True)
                        if local:
                            mm = pe.matmul(out, identb[:TT, :TT], mask_q[:, mc:mc + n], start=False, stop=True,
                                           skip_group_check=True)
                        elif k0 + n == (i + 1) * TT:
                            mm = pe.matmul(out[:, n - TT:n], identb[:TT, :TT], mask_q[:], start=False, stop=True,
                                           skip_group_check=True)
                    mm.then_inc(c["unit_mm"].sem, 1)
                elif kind == "turn":
                    g, k = args
                    t0, t1 = ((0, 4), (4, 6))[k]
                    if k == 0:
                        pe.wait_ge(c["neg_part"].sem, at("neg_part", t, which, 4 * (g + 1)))
                    bank = side(t, p)
                    for i in range(t0, t1):
                        mm = pe.matmul(ps[:3 * HG, bank, (i - t0) * TT:(i - t0 + 1) * TT],
                                       neg_part[:, i].rearrange("p k h -> p (k h)"), identb[:TT, :TT],
                                       start=True, stop=True)
                    mm.then_inc(c["unit_mm"].sem, 1)
                elif kind == "second":
                    g, k = args
                    x = g * N_SEC + k
                    j, h0, nh, n, c0 = seconds[k]
                    if x >= SEC_BANKS or not (isinstance(t, int) and t == 0):
                        pe.wait_ge(c["exp"].sem, at("exp", t, which, x - SEC_BANKS + 1))
                    if k == 0:
                        pe.wait_ge(c["neg_in"].sem, at("neg_in", t, which, 48 * (g + 1)))
                    if x == 0 and isinstance(t, int) and t == 0:
                        pe.wait_ge(set_const, 3)
                    for e in range(nh):
                        hh = g * HG + h0 + e
                        out = ps[:TT, x % SEC_BANKS, e * n:(e + 1) * n]
                        q0 = j * TT + c0
                        mm = pe.matmul(out, k_st[0:ROWS, hh, j * TT:(j + 1) * TT], q_st[0:ROWS, hh, q0:q0 + n],
                                       start=True, stop=True)
                        if c0 == 0:
                            w = min(mask_w, n)
                            mm = pe.matmul(out[:, 0:w], identb[:TT, :TT], mask_k[:, 0:w], start=False, stop=True,
                                           skip_group_check=True)
                    mm.then_inc(c["sec_mm"].sem, 1)
                elif kind == "weigh":
                    g, j = args
                    last = g * N_SEC + max(k for k, s in enumerate(seconds) if s[0] == j)
                    pe.wait_ge(c["exp"].sem, at("exp", t, which, last + 1))
                    if g == 0:
                        pe.wait_ge(c["v"].sem, at("v", t, which, j // 2 + 1))
                    if j == 0 and (g >= 1 or not (isinstance(t, int) and t == 0)):
                        pe.wait_ge(c["pv_sb"].sem, at("pv_sb", t, which, g))
                    q0, q1 = j * TT, min(T, j * TT + pw)
                    for bank, (s0, s1) in enumerate(SEGS):
                        a0, a1 = max(q0, s0), min(q1, s1)
                        if a0 >= a1:
                            continue
                        opens = not any(jj * TT < s1 and min(T, jj * TT + pw) > s0 for jj in range(j))
                        for e in range(HG):
                            mm = pe.matmul(ps[32 * e:32 * e + 32, 4 + bank, a0 - s0:a1 - s0],
                                           v_ext[:, j, g * HG + e, :],
                                           probs[:, (g * NT + j) % 2, e, a0 - q0:a1 - q0],
                                           start=opens, stop=True, skip_group_check=not opens)
                    mm.then_inc(c["pv_mm"].sem, 1)
                elif kind == "back":
                    (i,) = args
                    if i == 0:
                        pe.wait_ge(c["pv_sb"].sem, at("pv_sb", t, which))
                    bank = side(t, p)
                    for g in range(GROUPS):
                        mm = pe.transpose(ps[:TT, bank, g * P:(g + 1) * P], pv_sb[:, g, i * TT:(i + 1) * TT], ident[:])
                    mm.then_inc(c["unit_mm"].sem, 1)
                elif kind == "oT":
                    (i,) = args
                    pe.wait_ge(c["o"].sem, at("o", t, which, i + 1))
                    bank = side(t, p)
                    for kc in range(KC):
                        mm = pe.transpose(ps[:, bank, kc * TT:(kc + 1) * TT], o[:, i, kc * P:(kc + 1) * P],
                                          ident[:TT, :TT])
                    mm.then_inc(c["unit_mm"].sem, 1)
                elif kind == "wo":
                    (i,) = args
                    pe.wait_ge(c["oT"].sem, at("oT", t, which, i + 1))
                    bank = side(t, p)
                    for kc in range(KC):
                        mm = pe.matmul(ps[:TT, bank, 0:D], oT[:, i % 2, kc, :], wo[:, kc, :],
                                       start=kc == 0, stop=kc == KC - 1)
                    mm.then_inc(c["unit_mm"].sem, 1)
                elif kind == "hdT":
                    (i,) = args
                    pe.wait_ge(c["hd"].sem, at("hd", t, which, i + 1))
                    bank = side(t, p)
                    for kc in range(KC):
                        mm = pe.transpose(ps[:, bank, kc * TT:(kc + 1) * TT], hd[:, i, kc * P:(kc + 1) * P],
                                          ident[:TT, :TT])
                    mm.then_inc(c["unit_mm"].sem, 1)

            trips.run(pe, step)

        @block.scalar
        def _(act):
            def step(t, kind, which, args, p):
                bank = bank_of(t, p)
                if kind == "uT":
                    k = args[0]
                    t0, t1 = UT[k]
                    act.wait_ge(c["unit_mm"].sem, unit_done(t, p))
                    if k == 0 and not local:
                        act.wait_ge(c["uT_out"].sem, at("uT_out", t, which, 0))
                    act.activation(uT_hi[:, :, t0 * TT:t1 * TT],
                                   ps[:, bank, 0:KC * (t1 - t0) * TT].rearrange("p (k q) -> p k q", k=KC), ACT.Copy)\
                       .then_inc(c["uT_hi"].sem, 1)
                elif kind == "qk" and not local:
                    n, ec, s = args
                    s0, s1 = HALVES[s]
                    act.wait_ge(c["unit_mm"].sem, unit_done(t, p))
                    if (n, ec, s) == (0, 0, 0):
                        act.wait_ge(c["parts_out"].sem, at("parts_out", t, which, 0))
                    act.activation(part[0][:, n, ec, s0:s1], ps[:, bank, 0:s1 - s0], ACT.Copy)\
                       .then_inc(c["part0"].sem, 1)
                elif kind == "cut" and local:
                    (n,) = args
                    act.wait_ge(c["rope_sum"].sem, at("rope_sum", t, which, 2 * n + 2))
                    if n == 0:
                        act.wait_ge(c["parts_out"].sem, at("parts_out", t, which, 0))
                    act.activation(part[0][:, n], rot[:], ACT.Copy).then_inc(c["part0"].sem, 1)
                elif kind == "cut":
                    (n,) = args
                    act.wait_ge(c["rest"].sem, at("rest", t, which, SPLITS * (n + 1)))
                    act.activation(part[1][:, n], rest[:], ACT.Copy).then_inc(c["part1"].sem, 1)
                elif kind == "v":
                    act.wait_ge(c["unit_mm"].sem, unit_done(t, p))
                    for i in range(2):
                        a = act.activation(v_ext[:, 2 * args[0] + i, :, 0:HD],
                                           ps[:TT, bank, i * D:(i + 1) * D].rearrange("p (h d) -> p h d", d=HD),
                                           ACT.Copy)
                        if i == 0:
                            continue
                        a.then_inc(c["v"].sem, 1)
                    act.wait_ge(c["v"].sem, at("v", t, which, args[0] + 1))
                    act.sem_inc(free_sem(t, p), 1)
                elif kind == "route":
                    act.wait_ge(c["r_sub"].sem, at("r_sub", t, which))
                    act.activation(r_exp[:], r_sub[:], ACT.Exp).then_inc(c["r_exp"].sem, 1)
                elif kind == "max_in":
                    (g,) = args
                    act.wait_ge(c["negT"].sem, at("negT", t, which, 2 * g + 2))
                    for k in range(3):
                        act.dma_start(q_st[STACK + k:STACK + k + 1, g * HG:(g + 1) * HG, :],
                                      negT[k * HG:(k + 1) * HG]).then_inc(c["neg_in"].sem, 16)
                elif kind == "second":
                    g, k = args
                    unit = seconds[k]
                    j, h0, nh, n, c0 = unit
                    x = g * N_SEC + k
                    act.wait_ge(c["sec_mm"].sem, at("sec_mm", t, which, x + 1))
                    s = g * NT + j
                    if s >= 2:
                        act.wait_ge(c["pv_mm"].sem, at("pv_mm", t, which, s - 1))
                    else:
                        act.wait_ge(c["pv_mm"].sem, at("pv_mm", t, which, 0))
                    dst = probs[:, s % 2, h0:h0 + nh, c0:c0 + n]
                    act.activation(dst, second_out(x, unit), ACT.Exp).then_inc(c["exp"].sem, 1)
                elif kind == "oT":
                    act.wait_ge(c["unit_mm"].sem, unit_done(t, p))
                    act.activation(oT[:, args[0] % 2].rearrange("p k q -> p (k q)"), ps[:, bank, 0:KC * TT], ACT.Copy)\
                       .then_inc(c["oT"].sem, 1)
                    act.wait_ge(c["oT"].sem, at("oT", t, which, args[0] + 1))
                    act.sem_inc(free_sem(t, p), 1)
                elif kind == "rms":
                    for i in range(NT):
                        act.wait_ge(c["hd_raw"].sem, at("hd_raw", t, which, i + 1))
                        if i:
                            act.wait_ge(c["ss"].sem, at("ss", t, which, i))
                        act.activation(junk[:], hd[:, i], ACT.Square, accum_out=ss[:, i:i + 1])\
                           .then_inc(c["ss"].sem, 1)
                elif kind == "hdT":
                    (i,) = args
                    act.wait_ge(c["unit_mm"].sem, unit_done(t, p))
                    act.wait_ge(c[f"hdT_out{i % 3}"].sem, at("hdT_out0", t, which, 32 * (i // 3)))
                    act.activation(hdT_hi[:, i % 3].rearrange("p k q -> p (k q)"), ps[:, bank, 0:KC * TT],
                                   ACT.Copy).then_inc(c["hdT_hi"].sem, 1)

            trips.run(act, step)

        @block.gpsimd
        def _(pool):
            keep.shared.start(pool, c)

            def step(t, kind, which, args, p):
                if kind == "norm":
                    pool.wait_ge(c["ve"].sem, at("ve", t, which))
                    pool.tensor_tensor(rstd[:], rstd[:], half[:], ALU.pow).then_inc(c["rstd"].sem, 1)
                    if isinstance(t, int) and t == -1:
                        pool.memset(v_ext[:, :, :, HD:2 * HD], 0.0).then_inc(set_const, 1)
                        pool.wait_ge(set_const, 1)
                        pool.memset(v_ext[:, :, :, HD:HD + 1], 1.0).then_inc(set_const, 1)
                        pool.wait_ge(set_const, 2)
                        pool.memset(k_st[STACK:ROWS], 1.0).then_inc(set_const, 1)
                        pool.wait_ge(set_const, 3)
                elif kind == "cut":
                    (n,) = args
                    if local:
                        pool.wait_ge(c["rope_mul"].sem, at("rope_mul", t, which, 8 * n + 8))
                        if n == 0:
                            pool.wait_ge(c["rest"].sem, at("rest", t, which, 0))
                        else:
                            pool.wait_ge(c["rest"].sem, at("rest", t, which, 1))
                        pool.tensor_tensor(rot[:, 0], prod[:, 0], prod[:, 1], ALU.subtract)\
                            .then_inc(c["rope_sum"].sem, 1)
                        pool.tensor_tensor(rot[:, 1], prod[:, 2], prod[:, 3], ALU.add).then_inc(c["rope_sum"].sem, 1)
                    pool.wait_ge(c["part1"].sem, at("part1", t, which, n + 1))
                    pool.tensor_tensor(part[2][:, n], rest[:], part[1][:, n], ALU.subtract).then_inc(c["part2"].sem, 1)
                elif kind == "rms":
                    pool.wait_ge(c["rms_ve"].sem, at("rms_ve", t, which))
                    pool.tensor_tensor(rms[:], rms[:], half[:], ALU.pow).then_inc(c["rms"].sem, 1)

            trips.run(pool, step)

        @block.vector
        def _(dve):
            def step(t, kind, which, args, p):
                bank = bank_of(t, p)
                if kind in ("uT", "qk", "router", "first", "turn", "back", "wo", "hdT"):
                    dve.wait_ge(c["unit_mm"].sem, unit_done(t, p))
                if kind == "keep":
                    if not (isinstance(t, int) and t == -1):
                        dve.tensor_copy(u_kept[:], u[:])
                elif kind == "norm":
                    for i in range(NT):
                        dve.bn_stats(stats[:, i], h[:, tile_no(t, which, i), :]).then_inc(c["stats"].sem, 1)
                    dve.wait_ge(c["stats"].sem, at("stats", t, which))
                    dve.memset(waiter[:], 0.0)
                    for i in range(NT):
                        dve.bn_aggr(mv[:, i], stats[:, i]).then_inc(c["mv"].sem, 1)
                    dve.wait_ge(c["mv"].sem, at("mv", t, which))
                    dve.tensor_scalar(rstd[:], mv[:, :, 1], LN_EPS, None, ALU.add).then_inc(c["ve"].sem, 1)
                    dve.wait_ge(c["rstd"].sem, at("rstd", t, which))
                    for i in range(NT):
                        dve.tensor_scalar(u[:, i], h[:, tile_no(t, which, i), :], mv[:, i, 0:1], rstd[:, i:i + 1],
                                          ALU.subtract, ALU.mult).then_inc(c["u"].sem, 1)
                elif kind == "uT":
                    k = args[0]
                    t0, t1 = UT[k]
                    dve.wait_ge(c["uT_hi"].sem, at("uT_hi", t, which, k + 1))
                    dve.tensor_tensor(uT_lo[:, :, t0 * TT:t1 * TT],
                                      ps[:, bank, 0:KC * (t1 - t0) * TT].rearrange("p (k q) -> p k q", k=KC),
                                      uT_hi[:, :, t0 * TT:t1 * TT].bitcast(F32), ALU.subtract)\
                       .then_inc(c["uT_lo"].sem, 1)
                    dve.wait_ge(c["uT_lo"].sem, at("uT_lo", t, which, k + 1))
                    dve.sem_inc(free_sem(t, p), 1)
                elif kind == "qk" and local:
                    n, ec, s = args
                    s0, s1 = HALVES[s]
                    if (ec, s) == (0, 0):
                        dve.wait_ge(c["rope_sum"].sem, at("rope_sum", t, which, 2 * n))
                    for k, table in (((0, cos), (2, sin)), ((1, sin), (3, cos)))[ec]:
                        dve.tensor_tensor(prod[:, k, s0:s1], ps[:, bank, 0:s1 - s0], table[:, s0:s1], ALU.mult)\
                           .then_inc(c["rope_mul"].sem, 1)
                    dve.wait_ge(c["rope_mul"].sem, at("rope_mul", t, which, 8 * n + 4 * s + 2 * ec + 2))
                    dve.sem_inc(free_sem(t, p), 1)
                elif kind == "qk":
                    n, ec, s = args
                    s0, s1 = HALVES[s]
                    unit = 4 * n + 2 * s + ec
                    dve.wait_ge(c["part0"].sem, at("part0", t, which, unit + 1))
                    if (ec, s) == (0, 0):
                        dve.wait_ge(c["part2"].sem, at("part2", t, which, n))
                    dve.tensor_tensor(rest[:, ec, s0:s1], ps[:, bank, 0:s1 - s0], part[0][:, n, ec, s0:s1],
                                      ALU.subtract).then_inc(c["rest"].sem, 1)
                    dve.wait_ge(c["rest"].sem, at("rest", t, which, unit + 1))
                    dve.sem_inc(free_sem(t, p), 1)
                elif kind == "cut" and local:
                    (n,) = args
                    dve.wait_ge(c["part0"].sem, at("part0", t, which, n + 1))
                    dve.wait_ge(c["part2"].sem, at("part2", t, which, n))
                    dve.tensor_tensor(rest[:], rot[:], part[0][:, n], ALU.subtract).then_inc(c["rest"].sem, 1)
                    dve.wait_ge(c["rest"].sem, at("rest", t, which, n + 1))
                    dve.tensor_copy(part[1][:, n], rest[:]).then_inc(c["part1"].sem, 1)
                elif kind == "router":
                    logits = ps[:TT, bank, 0:NT * E_N].rearrange("p (i e) -> p i e", e=E_N)
                    dve.tensor_reduce(r_max[:], logits, AX_X, ALU.max).then_inc(c["r_max"].sem, 1)
                    dve.wait_ge(c["r_max"].sem, at("r_max", t, which))
                    dve.tensor_tensor(r_sub[:], logits, r_max[:].unsqueeze(2).to_broadcast([TT, NT, E_N]),
                                      ALU.subtract).then_inc(c["r_sub"].sem, 1)
                    dve.wait_ge(c["r_sub"].sem, at("r_sub", t, which))
                    dve.sem_inc(free_sem(t, p), 1)
                elif kind == "route":
                    dve.wait_ge(c["r_exp"].sem, at("r_exp", t, which))
                    dve.tensor_reduce(r_sum[:], r_exp[:], AX_X, ALU.add).then_inc(c["r_sum"].sem, 1)
                    dve.wait_ge(c["r_sum"].sem, at("r_sum", t, which))
                    dve.reciprocal(r_inv[:], r_sum[:]).then_inc(c["r_inv"].sem, 1)
                    dve.wait_ge(c["r_inv"].sem, at("r_inv", t, which))
                    dve.tensor_tensor(r_prob[:], r_exp[:], r_inv[:].unsqueeze(2).to_broadcast([TT, NT, E_N]),
                                      ALU.mult).then_inc(c["r_prob"].sem, 1)
                    dve.wait_ge(c["r_prob"].sem, at("r_prob", t, which))
                    dve.memset(waiter[:], 0.0)
                    for i in range(NT):
                        dve.max(top_v[:, i], r_prob[:, i]).then_inc(c["top_v"].sem, 1)
                    dve.wait_ge(c["top_v"].sem, at("top_v", t, which))
                    dve.memset(waiter[:], 0.0)
                    for i in range(NT):
                        dve.max_index(top_i[:, i], top_v[:, i], r_prob[:, i]).then_inc(c["top_i"].sem, 1)
                    dve.wait_ge(c["top_i"].sem, at("top_i", t, which))
                    dve.tensor_copy(top_f[:], top_i[:]).then_inc(c["top_f"].sem, 1)
                    dve.wait_ge(c["top_f"].sem, at("top_f", t, which))
                    for i in range(NT):
                        for k in range(2):
                            dve.tensor_scalar(pick[:, k, i], iota[:], top_f[:, i, k:k + 1], top_v[:, i, k:k + 1],
                                              ALU.is_equal, ALU.mult).then_inc(c["pick"].sem, 1)
                    dve.wait_ge(c["pick"].sem, at("pick", t, which))
                    dve.tensor_tensor(route[:, bass.ds(tile_no(t, which, 0), NT), :], pick[:, 0], pick[:, 1], ALU.add)\
                       .then_inc(c["route"].sem, 1)
                elif kind == "first":
                    g, unit = args[0], firsts[args[1]]
                    i, seg, h0, per, k0, n, mc = unit
                    dst = (neg_b[:, i - 4] if seg else neg[:, i])[:, g * HG + h0:g * HG + h0 + per]
                    dve.tensor_reduce(dst, ps[:TT, bank, 0:per * n].rearrange("p (m n) -> p m n", n=n),
                                      AX_X, ALU.max, negate=True).then_inc(free_sem(t, p), 1)
                elif kind == "maxima":
                    (g,) = args
                    trip, units = trips.number(t, p)
                    for back in range(1, NS + 1):
                        dve.wait_ge(c[f"free{(units - back) % NS}"].sem,
                                    c[f"free{(units - back) % NS}"].at(trip, (units - back) // NS + 1))
                    heads = slice(g * HG, (g + 1) * HG)
                    lo = 4 if not local else NT - 1
                    part_neg = neg[:, lo:NT, heads]
                    other = neg_b[:, :, heads] if not local else part_neg
                    dve.tensor_tensor(part_neg, part_neg, other, ALU.min).then_inc(c["neg"].sem, 1)
                    dve.wait_ge(c["neg"].sem, at("neg", t, which, g + 1))
                    dve.tensor_copy(neg_part[:, :, 0], neg[:, :, heads]).then_inc(c["neg_part"].sem, 1)
                    dve.wait_ge(c["neg_part"].sem, at("neg_part", t, which, 4 * g + 1))
                    dve.tensor_tensor(neg_rest[:], neg[:, :, heads], neg_part[:, :, 0], ALU.subtract)\
                       .then_inc(c["neg_part"].sem, 1)
                    dve.wait_ge(c["neg_part"].sem, at("neg_part", t, which, 4 * g + 2))
                    dve.tensor_copy(neg_part[:, :, 1], neg_rest[:]).then_inc(c["neg_part"].sem, 1)
                    dve.wait_ge(c["neg_part"].sem, at("neg_part", t, which, 4 * g + 3))
                    dve.tensor_tensor(neg_part[:, :, 2], neg_rest[:], neg_part[:, :, 1], ALU.subtract)\
                       .then_inc(c["neg_part"].sem, 1)
                elif kind == "turn":
                    g, k = args
                    t0, t1 = ((0, 4), (4, 6))[k]
                    if k == 0:
                        dve.wait_ge(c["neg_in"].sem, at("neg_in", t, which, 48 * g))
                    dve.tensor_copy(negT[:, t0 * TT:t1 * TT], ps[:3 * HG, bank, 0:(t1 - t0) * TT])\
                       .then_inc(c["negT"].sem, 1)
                    dve.wait_ge(c["negT"].sem, at("negT", t, which, 2 * g + k + 1))
                    dve.sem_inc(free_sem(t, p), 1)
                elif kind == "weighed":
                    (g,) = args
                    dve.wait_ge(c["pv_mm"].sem, at("pv_mm", t, which, (g + 1) * NT))
                    dve.tensor_copy(pv_sb[:, g, :], flat(4)[:, 0:T]).then_inc(c["pv_sb"].sem, 1)
                elif kind == "back":
                    (i,) = args
                    rows = ps[:TT, bank, :].rearrange("p (h w) -> p h w", w=2 * HD)
                    dve.reciprocal(rden[:, i], rows[:, :, HD]).then_inc(c["rden"].sem, 1)
                    dve.wait_ge(c["rden"].sem, at("rden", t, which, i + 1))
                    dve.tensor_tensor(o[:, i].rearrange("p (h d) -> p h d", d=HD), rows[:, :, 0:HD],
                                      rden[:, i].unsqueeze(2).to_broadcast([TT, H, HD]), ALU.mult)\
                       .then_inc(c["o"].sem, 1)
                    dve.wait_ge(c["o"].sem, at("o", t, which, i + 1))
                    dve.sem_inc(free_sem(t, p), 1)
                elif kind == "wo" and local:
                    (i,) = args
                    tile = tile_no(t, which, i)
                    dve.tensor_tensor(h[:, tile, :], ps[:TT, bank, 0:D], h[:, tile, :], ALU.add)\
                       .then_inc(c["h"].sem, 1)
                    dve.wait_ge(c["h"].sem, at("h", t, which, i + 1))
                    dve.sem_inc(free_sem(t, p), 1)
                elif kind == "wo":
                    (i,) = args
                    dve.tensor_copy(hd[:, i], ps[:TT, bank, 0:D]).then_inc(c["hd_raw"].sem, 1)
                    dve.wait_ge(c["hd_raw"].sem, at("hd_raw", t, which, i + 1))
                    dve.sem_inc(free_sem(t, p), 1)
                elif kind == "rms":
                    dve.wait_ge(c["ss"].sem, at("ss", t, which))
                    dve.tensor_scalar(rms[:], ss[:], 1.0 / D, LN_EPS, ALU.mult, ALU.add).then_inc(c["rms_ve"].sem, 1)
                elif kind == "hd":
                    (i,) = args
                    tile = tile_no(t, which, i)
                    if i == 0:
                        dve.wait_ge(c["rms"].sem, at("rms", t, which))
                    dve.scalar_tensor_tensor(hd[:, i], hd[:, i], rms[:, i:i + 1], norm_w[:], ALU.mult, ALU.mult)\
                       .then_inc(c["hd_t"].sem, 1)
                    dve.wait_ge(c["hd_t"].sem, at("hd_t", t, which, i + 1))
                    dve.tensor_tensor(hd[:, i], hd[:, i], rows_of(t)[:, i], ALU.add).then_inc(c["hd"].sem, 1)
                    dve.wait_ge(c["hd"].sem, at("hd", t, which, i + 1))
                    dve.tensor_tensor(h[:, tile, :], hd[:, i], h[:, tile, :], ALU.add).then_inc(c["h"].sem, 1)
                elif kind == "hdT":
                    (i,) = args
                    dve.wait_ge(c["hdT_hi"].sem, at("hdT_hi", t, which, i + 1))
                    dve.tensor_tensor(hdT_lo[:, i % 3].rearrange("p k q -> p (k q)"), ps[:, bank, 0:KC * TT],
                                      hdT_hi[:, i % 3].bitcast(F32).rearrange("p k q -> p (k q)"), ALU.subtract)\
                       .then_inc(c["hdT_lo"].sem, 1)
                    dve.wait_ge(c["hdT_lo"].sem, at("hdT_lo", t, which, i + 1))
                    dve.sem_inc(free_sem(t, p), 1)

            def rows_of(t):
                return u if isinstance(t, int) and t == B else u_kept

            trips.run(dve, step)
            dve.wait_ge(c["h"].sem, c["h"].at(B - 1))
        keep.shared.close(c)


E_H = 256
FF = 1024
CT = 4
CN = CT * TT
NCH = B * T // CN
PAIRS = E_N // 2
NALL = E_N + FF // E_H


def stage_experts(nc, keep, io, h, route, scratch):
    with ExitStack() as stack:
        m = Memory(nc, stack, keep)
        uT = m.sb("c_uT", [P, 2, KC, B * T], F32R)
        hdT = m.sb("c_hdT", [P, 2, KC, B * T], F32R)
        acc = m.sb("c_acc", [TT, NTILES, D], F32)
        raw = [m.sb(f"c_raw{k}", [P, 3, KC, E_H], F32) for k in range(2)]
        w_hi = [m.sb(f"c_w_hi{k}", [P, 3, KC, E_H], F32R) for k in range(2)]
        w_lo = [m.sb(f"c_w_lo{k}", [P, 3, KC, E_H], F32R) for k in range(2)]
        act_a = m.sb("c_act_a", [P, 2, CN], F32)
        g = m.sb("c_g", [P, 2, CN], F32)
        g_hi = m.sb("c_g_hi", [P, 2, CN], F32R)
        g_lo = m.sb("c_g_lo", [P, 2, CN], F32R)
        norm_w = m.sb("c_norm_w", [TT, 2, D], F32)
        half = m.sb("c_half", [TT, NT], F32)
        junk = m.sb("c_junk", [TT, D], F32)
        ss = m.sb("c_ss", [TT, NTILES], F32)
        rms_p = m.sb("c_rms", [TT, CT], F32)
        t = m.sb("c_t", [TT, CT, D], F32)
        ps = m.ps("c_ps", [P, 8, BANK])

        const_in = m.sem("c_const_in")
        zeroed = m.sem("c_zeroed")
        x_in, hd_in = m.sem("c_x_in"), m.sem("c_hd_in")
        raw_in = [m.sem(f"c_raw_in{k}") for k in range(2)]
        made_hi, made_lo = m.sem("c_made_hi"), m.sem("c_made_lo")
        up_mm, down_mm = m.sem("c_up_mm"), m.sem("c_down_mm")
        silu, gated, gated_hi, gated_lo = m.sem("c_silu"), m.sem("c_gated"), m.sem("c_gated_hi"), m.sem("c_gated_lo")
        added = m.sem("c_added")
        sq, ve, rms_ok, scaled, h_upd = m.sem("c_sq"), m.sem("c_ve"), m.sem("c_rms_ok"), m.sem("c_scaled"), m.sem("c_h")

        def walk(eng, prepare, head, tail):

            def expert(e, par, last=False, before_dense=False, dense=False, final=None, opens=False):
                n0 = e * NCH
                if not last:
                    prepare(e + 1, 1 - par)
                with eng.Fori(1, NCH) as k:
                    head(par, k, n0 + k, dense)
                    tail(par, k - 1, n0 + k - 1, e, dense, final, opens)
                if not last:
                    head(1 - par, 0, n0 + NCH, dense or before_dense)
                tail(par, NCH - 1, n0 + NCH - 1, e, dense, final, opens)

            prepare(0, 0)
            head(0, 0, 0, False)
            with eng.Fori(0, PAIRS - 1) as pair:
                for par in range(2):
                    expert(pair * 2 + par, par)
            expert(E_N - 2, 0)
            expert(E_N - 1, 1, before_dense=True, final=0)
            for e in range(E_N, NALL):
                expert(e, e % 2, last=e == NALL - 1, dense=True, final=1 if e == NALL - 1 else None, opens=e == E_N)

        def skip(*_):
            return

        def raw_count(e, par):
            return (e - par) * 24 + 48

        def tile_of(buf, c, i):
            return buf[:, c * CT + i, :]

        def column_of(buf, c, i):
            return buf[:, bass.ds(c * CT + i, 1)]

        block = stack.enter_context(nc.Block())

        @block.sync
        def _(sp):
            def weights(e, par, dense):
                for k, name in enumerate(("1", "3", "2")):
                    if not dense:
                        src = io[f"L0_ffn_ew{name}"][bass.ds(e, 1), :, :].rearrange("a (k p) n -> p (a k) n", p=P)
                    elif name == "2":
                        s = e - E_N
                        src = io["L0_ffn_w2"][s * E_H:(s + 1) * E_H, :].rearrange("(k p) n -> p k n", p=P)
                    else:
                        s = e - E_N
                        src = io[f"L0_ffn_w{name}"][:, s * E_H:(s + 1) * E_H].rearrange("(k p) n -> p k n", p=P)
                    sp.dma_start(raw[par][:, k], src).then_inc(raw_in[par], 16)

            def rows(c, name, dst, sem):
                for k in range(2):
                    sp.dma_start(dst[:, k, :, c * CN:(c + 1) * CN].bitcast(F32),
                                 scratch[name][k, :, :, c * CN:(c + 1) * CN]).then_inc(sem, 16)
                sp.wait_ge(sem, 32 * (c + 1))

            weights(0, 0, False)
            rows(0, "uT", uT, x_in)
            weights(1, 1, False)
            for k, name in enumerate(("moe_norm_w", "ff_norm_w")):
                sp.dma_start(norm_w[:, k], io[f"L0_ffn_{name}"].rearrange("(a d) -> a d", a=1).to_broadcast([TT, D]))\
                  .then_inc(const_in, 16)
            sp.dma_start(half[:], io["minus_half"]).then_inc(const_in, 16)
            for c in range(1, NCH):
                rows(c, "uT", uT, x_in)
            for c in range(NCH):
                rows(c, "hdT", hdT, hd_in)
            with sp.Fori(1, PAIRS) as pair:
                for par in range(2):
                    sp.wait_ge(made_lo, pair * 2 + par - 1)
                    weights(pair * 2 + par, par, False)
            for e in range(E_N, NALL):
                sp.wait_ge(made_lo, e - 1)
                weights(e, e % 2, True)

        @block.tensor
        def _(pe):
            def prepare(e, par):
                if isinstance(e, int) and e == 0:
                    pe.wait_ge(made_lo, 1)

            def head(par, c, n, dense):
                if isinstance(c, int):
                    pe.wait_ge(made_lo, n // NCH + 1 if isinstance(n, int) else next_expert[0] + 1)
                pe.wait_ge(hd_in if dense else x_in, c * 32 + 32)
                pe.wait_ge(gated, FIRST + n * 2)
                x = hdT if dense else uT
                for hc in range(2):
                    for k in range(2):
                        for kc in range(KC):
                            mm = split3(pe, ps[:, 2 * hc + k, 0:CN],
                                        [w[par][:, k, kc, hc * P:(hc + 1) * P] for w in (w_hi, w_lo)],
                                        [x[:, s, kc, bass.ds(c * CN, CN)] for s in range(2)], kc == 0, kc == KC - 1)
                    mm.then_inc(up_mm, 1)

            def tail(par, c, n, e, dense, final, opens):
                pe.wait_ge(gated_lo, FIRST + n * 2 + 2)
                pe.wait_ge(added, FIRST + n * 4)
                for i in range(CT):
                    for hc in range(2):
                        mm = split3(pe, ps[:TT, 4 + i, 0:D], [x[:, hc, i * TT:(i + 1) * TT] for x in (g_hi, g_lo)],
                                    [w[par][:, 2, hc, :] for w in (w_hi, w_lo)], hc == 0, hc == 1)
                    mm.then_inc(down_mm, 1)

            next_expert = [0]

            def note(e, par):
                next_expert[0] = e

            walk(pe, note, head, tail)

        @block.scalar
        def _(act):
            def prepare(e, par):
                act.wait_ge(raw_in[par], raw_count(e, par))
                if not (isinstance(e, int) and e == 0):
                    act.wait_ge(down_mm, FIRST + (e - 1) * (CT * NCH))
                act.activation(w_hi[par][:], raw[par][:], ACT.Copy).then_inc(made_hi, 1)

            def head(par, c, n, dense):
                for hc in range(2):
                    act.wait_ge(up_mm, n * 2 + hc + 1)
                    act.wait_ge(gated, FIRST + n * 2)
                    act.activation(act_a[:, hc], ps[:, 2 * hc, 0:CN], ACT.Silu).then_inc(silu, 1)
                for hc in range(2):
                    act.wait_ge(gated, FIRST + n * 2 + hc + 1)
                    act.wait_ge(down_mm, FIRST + n * CT)
                    act.activation(g_hi[:, hc], g[:, hc], ACT.Copy).then_inc(gated_hi, 1)

            def tail(par, c, n, e, dense, final, opens):
                if final is None:
                    return
                for i in range(CT):
                    act.wait_ge(added, FIRST + n * CT + i + 1)
                    act.wait_ge(sq, FIRST + c * CT + (final * NTILES + i))
                    act.activation(junk[:], tile_of(acc, c, i), ACT.Square, accum_out=column_of(ss, c, i))\
                       .then_inc(sq, 1)

            walk(act, prepare, head, tail)

        @block.gpsimd
        def _(pool):
            def prepare(e, par):
                pool.wait_ge(made_hi, e + 1)
                pool.tensor_tensor(w_lo[par][:], raw[par][:], w_hi[par][:].bitcast(F32), ALU.subtract)\
                    .then_inc(made_lo, 1)

            def head(par, c, n, dense):
                for hc in range(2):
                    pool.wait_ge(gated_hi, n * 2 + hc + 1)
                    pool.tensor_tensor(g_lo[:, hc], g[:, hc], g_hi[:, hc].bitcast(F32), ALU.subtract)\
                        .then_inc(gated_lo, 1)

            def tail(par, c, n, e, dense, final, opens):
                if final is None:
                    return
                pool.wait_ge(const_in, 48)
                pool.wait_ge(ve, c + (final * NCH + 1))
                pool.tensor_tensor(rms_p[:], rms_p[:], half[:, 0:CT], ALU.pow).then_inc(rms_ok, 1)

            for sem in (gated, added, gated_lo, down_mm, sq):
                pool.sem_inc(sem, FIRST)
            pool.memset(acc[:], 0.0).then_inc(zeroed, 1)
            pool.wait_ge(zeroed, 1)
            walk(pool, prepare, head, tail)

        @block.vector
        def _(dve):
            def head(par, c, n, dense):
                for hc in range(2):
                    dve.wait_ge(silu, n * 2 + hc + 1)
                    dve.wait_ge(gated_lo, FIRST + n * 2)
                    dve.tensor_tensor(g[:, hc], act_a[:, hc], ps[:, 2 * hc + 1, 0:CN], ALU.mult).then_inc(gated, 1)

            def tail(par, c, n, e, dense, final, opens):
                for i in range(CT):
                    dve.wait_ge(down_mm, FIRST + n * CT + i + 1)
                    a, out = tile_of(acc, c, i), ps[:TT, 4 + i, 0:D]
                    if opens:
                        dve.wait_ge(scaled, c * CT + CT)
                        dve.tensor_copy(a, out).then_inc(added, 1)
                    elif dense:
                        dve.tensor_tensor(a, out, a, ALU.add).then_inc(added, 1)
                    else:
                        dve.scalar_tensor_tensor(a, out, route[:, c * CT + i, bass.ds(e, 1)], a, ALU.mult, ALU.add)\
                           .then_inc(added, 1)
                if final is not None:
                    dve.wait_ge(sq, FIRST + c * CT + (final * NTILES + CT))
                    dve.tensor_scalar(rms_p[:], ss[:, bass.ds(c * CT, CT)], 1.0 / D, LN_EPS, ALU.mult, ALU.add)\
                       .then_inc(ve, 1)
                    dve.wait_ge(rms_ok, c + (final * NCH + 1))
                    for i in range(CT):
                        dve.scalar_tensor_tensor(t[:, i], tile_of(acc, c, i), rms_p[:, i:i + 1], norm_w[:, final],
                                                 ALU.mult, ALU.mult).then_inc(scaled, 1)
                    for i in range(CT):
                        dve.wait_ge(scaled, c * CT + (final * NTILES + i + 1))
                        dve.tensor_tensor(tile_of(h, c, i), tile_of(h, c, i), t[:, i], ALU.add).then_inc(h_upd, 1)

            dve.wait_ge(zeroed, 1)
            walk(dve, skip, head, tail)
            dve.wait_ge(h_upd, 2 * NTILES)


FH = 1024
FC = FH // P
QP, MIN_RANGE = 127.0, 1e-6
ROUND = 1.5 * 2.0 ** 23


def stage_quantised(nc, keep, io, h, ident):
    with ExitStack() as stack:
        m = Memory(nc, stack, keep)
        hid = m.sb("e_hid", [P, FC, B * T], F32)
        flat_hid = hid[:].rearrange("p c t -> p (c t)")
        w1 = flat_hid[:, 0:FC * D].rearrange("p (c d) -> p c d", c=FC)
        w2 = flat_hid[:, FC * D:FC * D + KC * FH].rearrange("p (c f) -> p c f", c=KC)
        w1T = m.sb("e_w1T", [P, KC, FC, P], BF16)
        w2T = m.sb("e_w2T", [P, FC, D], BF16)
        b1 = m.sb("e_b1", [P, FC], F32)
        b2 = m.sb("e_b2", [TT, D], F32)
        half = m.sb("e_half", [TT, NT], F32)
        stats = m.sb("e_stats", [TT, NTILES, 6], F32)
        mv = m.sb("e_mv", [TT, NTILES, 2], F32)
        rstd = m.sb("e_rstd", [TT, NTILES], F32)
        u = m.sb("e_u", [TT, NTILES, D], F32)
        uT = m.sb("e_uT", [P, KC, B * T], BF16)
        qh = m.sb("e_qh", [P, 2, FC, CN], BF16)
        peak = m.sb("e_peak", [P, 3], F32)
        peak_u = m.sb("e_peak_u", [TT, NTILES], F32)
        peak_h = m.sb("e_peak_h", [P, NCH * FC], F32)
        top = m.sb("e_top", [P, 4], F32)
        peak_p = m.sb("e_peak_p", [P, 1], F32)
        scale = m.sb("e_scale", [P, 4], F32)
        inv = m.sb("e_inv", [P, 4], F32)
        out_scale = m.sb("e_out_scale", [P, 2], F32)
        b1s = m.sb("e_b1s", [P, FC], F32)
        b2s = m.sb("e_b2s", [TT, D], F32)
        ps = m.ps("e_ps", [P, 8, BANK])

        GELU_FIRST, ADDED_FIRST = FC, 2 * CT
        loaded = m.sem("e_loaded")
        stat, agg, ve, rstd_ok, norm = (m.sem(f"e_{n}") for n in ("stat", "agg", "ve", "rstd_ok", "norm"))
        peaked, topped, scaled = m.sem("e_peaked"), m.sem("e_topped"), m.sem("e_scaled")
        w_shift, w_int, w_turned, w_ready = (m.sem(f"e_{n}") for n in ("w_shift", "w_int", "w_turned", "w_ready"))
        u_shift, u_int, u_turned, u_ready = (m.sem(f"e_{n}") for n in ("u_shift", "u_int", "u_turned", "u_ready"))
        zero_p, b2_scaled, b2_added = m.sem("e_zero_p"), m.sem("e_b2_scaled"), m.sem("e_b2_added")
        up_mm, gelu, hid_peak = m.sem("e_up_mm"), m.sem("e_gelu"), m.sem("e_hid_peak")
        q_shift, q_ready, down_mm, added, biased = (m.sem(f"e_{n}") for n in
                                                    ("q_shift", "q_ready", "down_mm", "added", "biased"))
        W1, W2, U, HID = range(4)

        block = stack.enter_context(nc.Block())

        @block.sync
        def _(sp):
            sp.dma_start(w1, io["L1_ffn_w1"].rearrange("(p c) d -> p c d", c=FC)).then_inc(loaded, 16)
            sp.dma_start(w2, io["L1_ffn_w2"].rearrange("(c p) f -> p c f", p=P)).then_inc(loaded, 16)
            sp.dma_start(b1[:], io["L1_ffn_b1"].rearrange("(p c) -> p c", c=FC)).then_inc(loaded, 16)
            sp.dma_start(b2[:], io["L1_ffn_b2"].rearrange("(a d) -> a d", a=1).to_broadcast([TT, D])).then_inc(loaded, 16)
            sp.dma_start(half[:], io["minus_half"]).then_inc(loaded, 16)

        @block.gpsimd
        def _(pool):
            reduce_max = bass.bass_isa.ReduceOp.max

            def over_rows(k, src):
                pool.partition_all_reduce(top[:, k:k + 1], src, P, reduce_max).then_inc(topped, 1)

            for sem, first in ((gelu, GELU_FIRST), (added, ADDED_FIRST), (down_mm, FIRST)):
                pool.sem_inc(sem, first)
            pool.memset(peak_p[:], 0.0).then_inc(zero_p, 1)
            pool.wait_ge(loaded, 80)
            for b in range(B):
                cols = slice(b * NT, (b + 1) * NT)
                pool.wait_ge(agg, (b + 1) * NT)
                pool.tensor_scalar(rstd[:, cols], mv[:, cols, 1], LN_EPS, None, ALU.add).then_inc(ve, 1)
                pool.wait_ge(ve, b + 1)
                pool.tensor_tensor(rstd[:, cols], rstd[:, cols], half[:], ALU.pow).then_inc(rstd_ok, 1)
            for k in (W1, W2):
                pool.wait_ge(peaked, k + 1)
                over_rows(k, peak[:, k:k + 1])
            pool.wait_ge(peaked, U + 1)
            over_rows(U, peak_p[:])
            pool.wait_ge(peaked, HID + 1)
            over_rows(HID, peak[:, 2:3])
            pool.wait_ge(b2_scaled, 1)
            for c2 in range(NCH // 2):
                rows = h[:, c2 * 2 * CT:(c2 + 1) * 2 * CT, :]
                pool.tensor_tensor(rows, rows, b2s[:].unsqueeze(1).to_broadcast([TT, 2 * CT, D]), ALU.add)\
                    .then_inc(b2_added, 1)

        @block.scalar
        def _(act):
            for k, w in ((W1, w1), (W2, w2)):
                act.wait_ge(scaled, k + 1)
                act.activation(w, w, ACT.Copy, scale=inv[:, k:k + 1], bias=ROUND).then_inc(w_shift, 1)
            for n in range(8):
                act.wait_ge(w_turned, n + 1)
                src = ps[:, n % 4, :].rearrange("p (c q) -> p c q", q=P)
                dst = w1T[:, n // 2, 4 * (n % 2):4 * (n % 2) + 4, :] if n < 4 else \
                    w2T[:, 2 * (n - 4):2 * (n - 4) + 2, :].rearrange("p c (k q) -> p (c k) q", q=P)
                act.activation(dst, src, ACT.Copy).then_inc(w_ready, 1)
            act.wait_ge(scaled, U + 1)
            for c in range(NCH):
                rows = u[:, c * CT:(c + 1) * CT, :]
                act.activation(rows, rows, ACT.Copy, scale=inv[:TT, U:U + 1], bias=ROUND).then_inc(u_shift, 1)
            act.wait_ge(biased, 1)
            with act.Fori(0, NCH) as c:
                for k in range(FC):
                    act.wait_ge(up_mm, c * FC + k + 1)
                    act.activation(hid[:, k, bass.ds(c * CN, CN)], ps[:, k, 0:CN], ACT.Gelu,
                                   scale=out_scale[:, 0:1], bias=b1s[:, k:k + 1]).then_inc(gelu, 1)
            act.wait_ge(scaled, HID + 1)
            with act.Fori(0, NCH) as c:
                rows = hid[:, :, bass.ds(c * CN, CN)]
                act.activation(rows, rows, ACT.Copy, scale=inv[:, HID:HID + 1], bias=ROUND).then_inc(q_shift, 1)

        @block.tensor
        def _(pe):
            pe.wait_ge(w_int, 1)
            for n in range(4):
                for k in range(4):
                    mm = pe.transpose(ps[:, n, k * P:(k + 1) * P],
                                      w1[:, 4 * (n % 2) + k, (n // 2) * P:(n // 2 + 1) * P], ident[:])
                mm.then_inc(w_turned, 1)
            pe.wait_ge(w_int, 2)
            for n in range(4):
                pe.wait_ge(w_ready, n + 1)
                for k in range(4):
                    f = 2 * n + k // 2
                    mm = pe.transpose(ps[:, n, k * P:(k + 1) * P], w2[:, k % 2, f:FH:FC], ident[:])
                mm.then_inc(w_turned, 1)
            for c in range(NCH):
                pe.wait_ge(u_int, c + 1)
                if c >= 2:
                    pe.wait_ge(u_ready, c - 1)
                for i in range(CT):
                    for kc in range(KC):
                        mm = pe.transpose(ps[:, 4 + 2 * (c % 2) + kc, i * TT:(i + 1) * TT],
                                          u[:, c * CT + i, kc * P:(kc + 1) * P], ident[:TT, :TT])
                mm.then_inc(u_turned, 1)
            pe.wait_ge(u_ready, NCH)
            pe.wait_ge(w_ready, 8)
            with pe.Fori(0, NCH) as c:
                for k in range(FC):
                    pe.wait_ge(gelu, GELU_FIRST + c * FC + (k + 1 - FC))
                    for kc in range(KC):
                        mm = pe.matmul(ps[:, k, 0:CN], w1T[:, kc, k, :], uT[:, kc, bass.ds(c * CN, CN)],
                                       start=kc == 0, stop=kc == KC - 1)
                    mm.then_inc(up_mm, 1)
            with pe.Fori(0, NCH // 2) as c2:
                for par in range(2):
                    pe.wait_ge(q_ready, c2 * 2 + par + 1)
                    for i in range(CT):
                        pe.wait_ge(added, ADDED_FIRST + c2 * 8 + (par * CT + i + 1 - 2 * CT))
                        for k in range(FC):
                            mm = pe.matmul(ps[:TT, 4 * par + i, 0:D], qh[:, par, k, i * TT:(i + 1) * TT], w2T[:, k, :],
                                           start=k == 0, stop=k == FC - 1)
                        mm.then_inc(down_mm, 1)

        @block.vector
        def _(dve):
            chain = m.sem("e_chain")
            links = [0]

            def link(ins):
                links[0] += 1
                ins.then_inc(chain, 1)
                dve.wait_ge(chain, links[0])

            def scale_of(k):
                dve.wait_ge(topped, k + 1)
                col = slice(k, k + 1)
                link(dve.tensor_scalar(scale[:, col], top[:, col], MIN_RANGE, 1.0 / QP, ALU.max, ALU.mult))
                dve.reciprocal(inv[:, col], scale[:, col]).then_inc(scaled, 1)

            for b in range(B):
                for i in range(b * NT, (b + 1) * NT):
                    dve.bn_stats(stats[:, i], h[:, i, :]).then_inc(stat, 1)
                for i in range(b * NT, (b + 1) * NT):
                    dve.wait_ge(stat, i + 1)
                    dve.bn_aggr(mv[:, i], stats[:, i]).then_inc(agg, 1)
            for b in range(B):
                dve.wait_ge(rstd_ok, b + 1)
                for i in range(b * NT, (b + 1) * NT):
                    dve.tensor_scalar(u[:, i], h[:, i, :], mv[:, i, 0:1], rstd[:, i:i + 1], ALU.subtract, ALU.mult)\
                       .then_inc(norm, 1)
                dve.wait_ge(norm, (b + 1) * NT)
                link(dve.tensor_reduce(peak_u[:, b * NT:(b + 1) * NT], u[:, b * NT:(b + 1) * NT, :], AX_X, ALU.max,
                                       apply_absolute_value=True))
            dve.wait_ge(loaded, 80)
            dve.tensor_reduce(peak[:, 0:1], flat_hid[:, 0:FC * D], AX_X, ALU.max, apply_absolute_value=True)\
               .then_inc(peaked, 1)
            dve.tensor_reduce(peak[:, 1:2], flat_hid[:, FC * D:2 * FC * D], AX_X, ALU.max, apply_absolute_value=True)\
               .then_inc(peaked, 1)
            dve.wait_ge(zero_p, 1)
            dve.tensor_reduce(peak_p[:TT], peak_u[:], AX_X, ALU.max).then_inc(peaked, 1)
            scale_of(W1)
            scale_of(W2)
            for k, w in ((W1, flat_hid[:, 0:FC * D]), (W2, flat_hid[:, FC * D:2 * FC * D])):
                dve.wait_ge(w_shift, k + 1)
                dve.tensor_scalar(w, w, -ROUND, None, ALU.add).then_inc(w_int, 1)
            scale_of(U)
            dve.wait_ge(scaled, 3)
            link(dve.tensor_tensor(out_scale[:, 0:1], scale[:, W1:W1 + 1], scale[:, U:U + 1], ALU.mult))
            dve.tensor_scalar(b1s[:], b1[:], out_scale[:, 0:1], None, ALU.mult).then_inc(biased, 1)

            def turned(c):
                dve.wait_ge(u_turned, c + 1)
                dve.tensor_copy(uT[:, :, c * CN:(c + 1) * CN], ps[:, 4 + 2 * (c % 2):6 + 2 * (c % 2), 0:CN])\
                   .then_inc(u_ready, 1)

            for c in range(NCH):
                dve.wait_ge(u_shift, c + 1)
                rows = u[:, c * CT:(c + 1) * CT, :]
                dve.tensor_scalar(rows, rows, -ROUND, None, ALU.add).then_inc(u_int, 1)
                if c:
                    turned(c - 1)
            turned(NCH - 1)
            with dve.Fori(0, NCH) as c:
                for k in range(FC):
                    dve.wait_ge(gelu, GELU_FIRST + c * FC + k + 1)
                    dve.tensor_reduce(peak_h[:, bass.ds(c * FC + k, 1)], hid[:, k, bass.ds(c * CN, CN)], AX_X, ALU.max,
                                      apply_absolute_value=True).then_inc(hid_peak, 1)
            dve.wait_ge(hid_peak, NCH * FC)
            dve.tensor_reduce(peak[:, 2:3], peak_h[:], AX_X, ALU.max).then_inc(peaked, 1)
            scale_of(HID)
            dve.wait_ge(scaled, 4)
            link(dve.tensor_tensor(out_scale[:, 1:2], scale[:, W2:W2 + 1], scale[:, HID:HID + 1], ALU.mult))
            dve.tensor_scalar(b2s[:], b2[:], out_scale[:TT, 1:2], None, ALU.mult).then_inc(b2_scaled, 1)

            def integers(c2, par):
                dve.wait_ge(q_shift, c2 * 2 + par + 1)
                dve.tensor_scalar(qh[:, par % 2], hid[:, :, bass.ds(c2 * (2 * CN) + par * CN, CN)], -ROUND, None, ALU.add)\
                   .then_inc(q_ready, 1)

            def add(c2, par):
                dve.wait_ge(b2_added, c2 + 1)
                for i in range(CT):
                    tile = c2 * 8 + (par * CT + i)
                    dve.wait_ge(down_mm, FIRST + c2 * 8 + (par * CT + i + 1))
                    dve.scalar_tensor_tensor(h[:, tile, :], ps[:TT, 4 * par + i, 0:D], out_scale[:TT, 1:2],
                                             h[:, tile, :], ALU.mult, ALU.add).then_inc(added, 1)

            integers(0, 0)
            with dve.Fori(0, NCH // 2 - 1) as c2:
                for par in range(2):
                    integers(c2, par + 1)
                    add(c2, par)
            integers(NCH // 2 - 1, 1)
            for par in range(2):
                add(NCH // 2 - 1, par)
            dve.wait_ge(added, ADDED_FIRST + NTILES)


def audio_tower(nc, io, out):
    with ExitStack() as stack:
        keep = Memory(nc, stack)
        h = keep.sb("h", [TT, NTILES, D], F32)
        ident = keep.sb("ident", [P, P], F32)
        identb = keep.sb("identb", [P, P], BF16)
        ready = keep.sem("const_ready")
        stored = keep.sem("stored")
        with nc.Block() as block:
            @block.gpsimd
            def _(pool):
                for k, t in enumerate((ident, identb)):
                    pool.memset(t[:], 0.0).then_inc(ready, 1)
                    pool.wait_ge(ready, 2 * k + 1)
                    pool.affine_select(out=t[:], in_=t[:], compare_op=ALU.not_equal, fill=1.0, base=0,
                                       pattern=[[-1, P]], channel_multiplier=1).then_inc(ready, 1)
                pool.wait_ge(ready, 4)
        route = keep.sb("route", [TT, NTILES, E_N], F32)
        scratch = {name: nc.dram_tensor(f"scratch_{name}", (2, P, KC, B * T), F32, kind="Internal").ap()
                   for name in ("uT", "hdT")}
        scratch["parts"] = nc.dram_tensor("scratch_parts", (2, 3, D, T), BF16, kind="Internal").ap()
        stage_tok_attn(nc, keep, io, h, ident, identb)
        stage_heads(nc, keep, io, h, ident, identb, False, route, scratch)
        stage_experts(nc, keep, io, h, route, scratch)
        stage_heads(nc, keep, io, h, ident, identb, True, None, scratch)
        stage_quantised(nc, keep, io, h, ident)
        with nc.Block() as block:
            @block.sync
            def _(sp):
                sp.dma_start(out.rearrange("b (i p) d -> p (b i) d", p=TT), h[:].rearrange("p (b i) d -> p (b i) d", b=B))\
                  .then_inc(stored, 16)
                sp.wait_ge(stored, 16)


def shape_constants():
    pos = np.arange(T, dtype=np.float32)
    theta = np.power(np.float32(10000.0), (np.float32(-2.0) * np.arange(D // 2, dtype=np.float32) / np.float32(D))
                     .astype(np.float32)).astype(np.float32)
    ang = (theta[:, None] * pos[None, :]).astype(np.float32)
    bf = mybir.dt.np(BF16)
    p, o = np.arange(TT)[:, None], np.arange(2 * TT)[None, :]
    freq = (np.float32(1.0) / np.power(np.float32(10000.0), np.arange(HD // 2, dtype=np.float32) / np.float32(HD // 2)))
    ang_h = (np.tile(freq.astype(np.float32), H)[:, None] * pos[None, :]).astype(np.float32)
    ow = np.arange(2 * TT + 2)[None, :]
    oc = np.arange(TT)[None, :]
    return {
        "cos_heads": np.cos(ang_h).astype(np.float32),
        "sin_heads": np.sin(ang_h).astype(np.float32),
        "mask_causal_q": np.where(oc <= p, 0.0, NEG).astype(bf),
        "mask_causal_k": np.where(oc >= p, 0.0, NEG).astype(bf),
        "mask_window_q": np.where((ow >= p) & (ow <= p + WINDOW - 1), 0.0, NEG).astype(bf),
        "mask_window_k": np.where((ow >= p) & (ow <= p + WINDOW - 1), 0.0, NEG).astype(bf),
        "expert_iota": np.tile(np.arange(E_N, dtype=np.float32), (TT, 1)),
        "cos_one": np.cos(ang).astype(np.float32),
        "sin_one": np.sin(ang).astype(np.float32),
        "mask_next": np.where(o <= p + 1, 0.0, NEG).astype(bf),
        "minus_half": np.full((TT, NT), -0.5, np.float32),
    }


_OUT = ("out_0_dram", (B, T, D), "float32")


def kernel(**inputs):
    import numpy as _np
    import concourse.bacc as _bacc
    from concourse import mybir as _mybir
    from concourse.bass_utils import run_bass_kernel_spmd as _run

    nc = _bacc.Bacc("TRN2", target_bir_lowering=False, num_devices=1)
    arrays, io = {}, {}
    for name, a in (dict(inputs) | shape_constants()).items():
        a = _np.ascontiguousarray(a)
        arrays[f"in_{name}_dram"] = a
        io[name] = nc.dram_tensor(f"in_{name}_dram", a.shape, _mybir.dt.from_np(a.dtype), kind="ExternalInput").ap()
    name, shape, dtype = _OUT
    out = nc.dram_tensor(name, shape, _mybir.dt.from_np(_np.dtype(dtype)), kind="ExternalOutput").ap()
    audio_tower(nc, io, out)
    r = _run(nc, [arrays], core_ids=[0])
    return r.results[0][name]
```
